# Optimizing a Trainium2 kernel written in Bass

```python
import numpy as np
import jax
import jax.numpy as jnp

def _softmax(x, axis=-1):
    return jax.nn.softmax(x, axis=axis)

def _gelu(x):
    return jax.nn.gelu(x, approximate=True)

def _silu(x):
    return jax.nn.silu(x)

def _sigmoid(x):
    return jax.nn.sigmoid(x)

def _layernorm(x, axis=-1, eps=1e-05):
    m = jnp.mean(x, axis=axis, keepdims=True)
    v = jnp.var(x, axis=axis, keepdims=True)
    return (x - m) / jnp.sqrt(v + eps)

def _scatter_add(tgt, idx, src, axis=0):
    return tgt.at[idx].add(src)

def _segment_sum(src, seg, n):
    return jax.ops.segment_sum(src, seg, n)
kernel_name = 'mk_xattn_ffn_d2_seqx_r8_498633'

def setup_inputs(seed: int=0):
    np.random.seed(seed)
    _w = jnp.asarray

    def _rec_inputs():
        import jax
        import jax.numpy as jnp
        _rk = jax.random.key(seed)
        x = 7.971e-05 + 1 * jax.random.normal(jax.random.fold_in(_rk, 1), (32, 64, 128), jnp.float32)
        _lenS = 64 - jax.random.randint(jax.random.fold_in(_rk, 7), (32,), 0, max(1, 64 // 4) + 1, jnp.int32)
        _lenS2 = 64 - jax.random.randint(jax.random.fold_in(_rk, 8), (32,), 0, max(1, 64 // 4) + 1, jnp.int32)
        _ctx_1024P = jax.random.normal(jax.random.fold_in(_rk, 11), (32, 16, 128), jnp.float32)
        _ctx_1024c = jax.random.dirichlet(jax.random.fold_in(_rk, 511), 0.3 * jnp.ones((16,), jnp.float32), (32, 64))
        _ctx_1024t = jnp.einsum('bsk,bkd->bsd', _ctx_1024c, _ctx_1024P)
        _ctx_1024t = _ctx_1024t * jax.lax.rsqrt(jnp.mean(jnp.square(_ctx_1024t)) + 1e-12) * 0.953939
        ctx_1024 = -2.71503e-05 + 1.0001 * (_ctx_1024t + 0.3 * jax.random.normal(jax.random.fold_in(_rk, 611), (32, 64, 128), jnp.float32))
        _validS = jnp.arange(64)[None, :] < _lenS[:, None]
        _validS2 = jnp.arange(64)[None, :] < _lenS2[:, None]
        _causal = jnp.tril(jnp.ones((64, 64), dtype=bool))
        mask_Bx1xS2_ik1 = jnp.where(jnp.broadcast_to(_validS2[:, None, :], (32, 1, 64)), 1, 0).astype(jnp.int32)
        return (x, ctx_1024, mask_Bx1xS2_ik1)
    x, ctx_1024, mask_Bx1xS2_ik1 = _rec_inputs()

    def _L0_xattn_setup():
        import jax, jax.numpy as jnp
        import numpy as np
        import math
        B, L, S = (16, 256, 256)
        D = 128
        H = 16
        SCALE = 1

        def _linear_params(k, fan_in, fan_out):
            lim = 1.0 / np.sqrt(fan_in)
            kw, kb = jax.random.split(k)
            W = jax.random.uniform(kw, (fan_in, fan_out), jnp.float32, -lim, lim)
            b = jax.random.uniform(kb, (fan_out,), jnp.float32, -lim, lim)
            return (W, b)
        key = jax.random.key(seed)
        ks = jax.random.split(key, 7)
        Wq, bq = _linear_params(ks[0], D, D)
        Wk, bk = _linear_params(ks[1], D, D)
        Wv, bv = _linear_params(ks[2], D, D)
        Wo, bo = _linear_params(ks[3], D, D)
        return {'queries': jax.random.normal(ks[4], (B, L, D), jnp.float32), 'keys': jax.random.normal(ks[5], (B, S, D), jnp.float32), 'values': jax.random.normal(ks[6], (B, S, D), jnp.float32), 'Wq': Wq, 'bq': bq, 'Wk': Wk, 'bk': bk, 'Wv': Wv, 'bv': bv, 'Wo': Wo, 'bo': bo}
    _L0_xattn_all = _L0_xattn_setup()
    _L0_xattn_in = {k: v for k, v in _L0_xattn_all.items() if k in ('Wq', 'bq', 'Wk', 'bk', 'Wv', 'bv', 'Wo', 'bo')}
    del _L0_xattn_all

    def _L0_ffn_setup():
        import math
        import jax, jax.numpy as jnp
        import numpy as np
        K = 2
        CAP_FACTOR = 1.0
        EPS = 1e-09
        key = jax.random.key(seed)
        ks = jax.random.split(key, 6)
        B, S, D, H, E = (4, 256, 128, 512, 8)
        x = jax.random.normal(ks[0], (B, S, D), jnp.float32)
        wg = jax.random.normal(ks[1], (D, E), jnp.float32) * 0.02
        w1 = jax.random.normal(ks[2], (E, D, H), jnp.float32) * 0.02
        b1 = jnp.zeros((E, H), jnp.float32)
        w2 = jax.random.normal(ks[3], (E, H, D), jnp.float32) * 0.02
        b2 = jnp.zeros((E, D), jnp.float32)
        return {'x': x, 'wg': wg, 'w1': w1, 'b1': b1, 'w2': w2, 'b2': b2}
    _L0_ffn_all = _L0_ffn_setup()
    _L0_ffn_in = {k: v for k, v in _L0_ffn_all.items() if k in ('wg', 'w1', 'b1', 'w2', 'b2')}
    del _L0_ffn_all

    def _L1_xattn_setup():
        import jax, jax.numpy as jnp
        import numpy as np
        B, NQ, NK = (8, 256, 256)
        DQ = DK = DV = 128
        EPS = 1e-05

        def _xavier(key, shape):
            fan_in, fan_out = (shape[0], shape[1])
            lim = float(np.sqrt(6.0 / (fan_in + fan_out)))
            return jax.random.uniform(key, shape, jnp.float32, -lim, lim)

        def _layernorm(x, g, b):
            mu = jnp.mean(x, axis=-1, keepdims=True)
            var = jnp.mean(jnp.square(x - mu), axis=-1, keepdims=True)
            return (x - mu) * jax.lax.rsqrt(var + EPS) * g + b
        key = jax.random.key(seed)
        ks = jax.random.split(key, 12)
        return {'Q': jax.random.normal(ks[0], (B, NQ, DQ), jnp.float32), 'K': jax.random.normal(ks[1], (B, NK, DK), jnp.float32), 'V': jax.random.normal(ks[2], (B, NK, DK), jnp.float32), 'pad_mask': jax.random.randint(ks[3], (B, 1, NK), 0, 2, jnp.int32), 'Wq': _xavier(ks[4], (DQ, DV)), 'bq': jnp.zeros((DV,), jnp.float32), 'Wk': _xavier(ks[5], (DK, DV)), 'bk': jnp.zeros((DV,), jnp.float32), 'Wv': _xavier(ks[6], (DK, DV)), 'bv': jnp.zeros((DV,), jnp.float32), 'Wo': _xavier(ks[7], (DV, DV)), 'bo': jnp.zeros((DV,), jnp.float32), 'g0': jnp.ones((DV,), jnp.float32), 'beta0': jnp.zeros((DV,), jnp.float32)}
    _L1_xattn_all = _L1_xattn_setup()
    _L1_xattn_in = {k: v for k, v in _L1_xattn_all.items() if k in ('Wq', 'bq', 'Wk', 'bk', 'Wv', 'bv', 'Wo', 'bo', 'g0', 'beta0')}
    del _L1_xattn_all

    def _L1_ffn_setup():
        import jax, jax.numpy as jnp
        import numpy as np
        key = jax.random.key(seed)
        k_x, k_W, k_b, k_ids, k_w = jax.random.split(key, 5)
        N_ADAPTERS, D_OUT, D_IN = (32, 128, 128)
        B, S = (2, 256)
        K = 8
        x = jax.random.normal(k_x, (B, S, D_IN), dtype=jnp.float32)
        W = jax.random.normal(k_W, (N_ADAPTERS, D_OUT, D_IN), dtype=jnp.float32)
        b = jax.random.normal(k_b, (N_ADAPTERS, D_OUT), dtype=jnp.float32)
        ids = jax.random.randint(k_ids, (K,), 0, N_ADAPTERS, dtype=jnp.int64)
        weights = jax.random.uniform(k_w, (K,), dtype=jnp.float32)
        return {'x': x, 'W': W, 'b': b, 'ids': ids, 'weights': weights}
    _L1_ffn_all = _L1_ffn_setup()
    _L1_ffn_in = {k: v for k, v in _L1_ffn_all.items() if k in ('W', 'b', 'ids', 'weights')}
    del _L1_ffn_all
    return {'x': x, 'ctx_1024': ctx_1024, 'mask_Bx1xS2_ik1': mask_Bx1xS2_ik1, 'L0_xattn_Wq': _L0_xattn_in['Wq'], 'L0_xattn_bq': _L0_xattn_in['bq'], 'L0_xattn_Wk': _L0_xattn_in['Wk'], 'L0_xattn_bk': _L0_xattn_in['bk'], 'L0_xattn_Wv': _L0_xattn_in['Wv'], 'L0_xattn_bv': _L0_xattn_in['bv'], 'L0_xattn_Wo': _L0_xattn_in['Wo'], 'L0_xattn_bo': _L0_xattn_in['bo'], 'L0_ffn_wg': _L0_ffn_in['wg'], 'L0_ffn_w1': _L0_ffn_in['w1'], 'L0_ffn_b1': _L0_ffn_in['b1'], 'L0_ffn_w2': _L0_ffn_in['w2'], 'L0_ffn_b2': _L0_ffn_in['b2'], 'L1_xattn_Wq': _L1_xattn_in['Wq'], 'L1_xattn_bq': _L1_xattn_in['bq'], 'L1_xattn_Wk': _L1_xattn_in['Wk'], 'L1_xattn_bk': _L1_xattn_in['bk'], 'L1_xattn_Wv': _L1_xattn_in['Wv'], 'L1_xattn_bv': _L1_xattn_in['bv'], 'L1_xattn_Wo': _L1_xattn_in['Wo'], 'L1_xattn_bo': _L1_xattn_in['bo'], 'L1_xattn_g0': _L1_xattn_in['g0'], 'L1_xattn_beta0': _L1_xattn_in['beta0'], 'L1_ffn_W': _L1_ffn_in['W'], 'L1_ffn_b': _L1_ffn_in['b'], 'L1_ffn_ids': _L1_ffn_in['ids'], 'L1_ffn_weights': _L1_ffn_in['weights']}

def reference(x, ctx_1024, mask_Bx1xS2_ik1, L0_xattn_Wq, L0_xattn_bq, L0_xattn_Wk, L0_xattn_bk, L0_xattn_Wv, L0_xattn_bv, L0_xattn_Wo, L0_xattn_bo, L0_ffn_wg, L0_ffn_w1, L0_ffn_b1, L0_ffn_w2, L0_ffn_b2, L1_xattn_Wq, L1_xattn_bq, L1_xattn_Wk, L1_xattn_bk, L1_xattn_Wv, L1_xattn_bv, L1_xattn_Wo, L1_xattn_bo, L1_xattn_g0, L1_xattn_beta0, L1_ffn_W, L1_ffn_b, L1_ffn_ids, L1_ffn_weights):
    import jax
    import jax.numpy as jnp

    def _L0_xattn_ref(queries, keys, values, Wq, bq, Wk, bk, Wv, bv, Wo, bo):
        import jax, jax.numpy as jnp
        import numpy as np
        import math
        B, L, S = (16, 256, 256)
        D = 128
        H = 16
        SCALE = 1

        def _linear_params(k, fan_in, fan_out):
            lim = 1.0 / np.sqrt(fan_in)
            kw, kb = jax.random.split(k)
            W = jax.random.uniform(kw, (fan_in, fan_out), jnp.float32, -lim, lim)
            b = jax.random.uniform(kb, (fan_out,), jnp.float32, -lim, lim)
            return (W, b)
        Bsz, Lq, _ = queries.shape
        q = (queries @ Wq + bq).reshape(Bsz, Lq, H, -1).transpose(0, 2, 3, 1)
        k = (keys @ Wk + bk).reshape(Bsz, Lq, H, -1).transpose(0, 2, 3, 1)
        v = (values @ Wv + bv).reshape(Bsz, Lq, H, -1).transpose(0, 2, 3, 1)
        q_fft = jnp.fft.rfft(q, axis=-1)
        k_fft = jnp.fft.rfft(k, axis=-1)
        corr = jnp.fft.irfft(q_fft * jnp.conj(k_fft), n=Lq, axis=-1)
        top_k = max(int(SCALE * math.log(Lq)), 1)
        weights, delay = jax.lax.top_k(corr, top_k)
        tmp_corr = jax.nn.softmax(weights, axis=-1)
        init = jnp.arange(Lq)
        agg = jnp.zeros_like(v)
        for i in range(top_k):
            idx = (init[None, None, None, :] + delay[..., i][..., None]) % Lq
            pattern = jnp.take_along_axis(v, idx, axis=-1)
            agg = agg + pattern * tmp_corr[..., i][..., None]
        out = agg.transpose(0, 3, 1, 2).reshape(Bsz, Lq, -1)
        return out @ Wo + bo

    def _L0_ffn_ref(x, wg, w1, b1, w2, b2):
        import math
        import jax, jax.numpy as jnp
        import numpy as np
        K = 2
        CAP_FACTOR = 1.0
        EPS = 1e-09
        B, S, D = x.shape
        E = wg.shape[1]
        xt = x.reshape(-1, D)
        N = xt.shape[0]
        cap = int(math.ceil(CAP_FACTOR * K * N / E))
        logits = xt.astype(jnp.float32) @ wg.astype(jnp.float32)
        scores = jax.nn.softmax(logits, axis=-1)
        gvals, gidx = jax.lax.top_k(scores, K)
        gvals = gvals / jnp.clip(gvals.sum(-1, keepdims=True), EPS)
        offset = jnp.zeros((E,), jnp.int32)
        pos_l, keep_l = ([], [])
        for kk in range(K):
            m = jax.nn.one_hot(gidx[:, kk], E, dtype=jnp.int32)
            loc = jnp.cumsum(m, axis=0) - 1 + offset[None, :]
            offset = offset + m.sum(axis=0)
            pos = jnp.take_along_axis(loc, gidx[:, kk:kk + 1], axis=1)[:, 0]
            keep = pos < cap
            pos_l.append(jnp.where(keep, pos, 0))
            keep_l.append(keep)
        pos = jnp.stack(pos_l, axis=1)
        keep = jnp.stack(keep_l, axis=1)
        gvals = gvals * keep
        e_flat = gidx.reshape(-1)
        p_flat = pos.reshape(-1)
        kmask = keep.reshape(-1).astype(x.dtype)
        x_rep = jnp.repeat(xt, K, axis=0)
        disp = jnp.zeros((E, cap, D), x.dtype).at[e_flat, p_flat].add(x_rep * kmask[:, None])
        h = jax.nn.gelu(jnp.einsum('ecd,edh->ech', disp, w1) + b1[:, None, :], approximate=False)
        y = jnp.einsum('ech,ehd->ecd', h, w2) + b2[:, None, :]
        yk = y[e_flat, p_flat]
        w = gvals.reshape(-1).astype(x.dtype)
        out = (yk * w[:, None]).reshape(N, K, D).sum(axis=1)
        return out.reshape(B, S, D)

    def _L1_xattn_ref(Q, K, V, pad_mask, Wq, bq, Wk, bk, Wv, bv, Wo, bo, g0, beta0):
        import jax, jax.numpy as jnp
        import numpy as np
        B, NQ, NK = (8, 256, 256)
        DQ = DK = DV = 128
        EPS = 1e-05

        def _xavier(key, shape):
            fan_in, fan_out = (shape[0], shape[1])
            lim = float(np.sqrt(6.0 / (fan_in + fan_out)))
            return jax.random.uniform(key, shape, jnp.float32, -lim, lim)

        def _layernorm(x, g, b):
            mu = jnp.mean(x, axis=-1, keepdims=True)
            var = jnp.mean(jnp.square(x - mu), axis=-1, keepdims=True)
            return (x - mu) * jax.lax.rsqrt(var + EPS) * g + b
        q = Q @ Wq + bq
        k = K @ Wk + bk
        v = V @ Wv + bv
        scale = 1.0 / jnp.sqrt(jnp.float32(DV))
        scores = jnp.einsum('bqd,bkd->bqk', q, k) * scale
        scores = jnp.where(pad_mask == 0, jnp.float32(-1000000000.0), scores)
        w = jax.nn.softmax(scores, axis=-1)
        out = jnp.einsum('bqk,bkd->bqd', w, v)
        out = out @ Wo + bo
        out = _layernorm(out, g0, beta0)
        return out

    def _L1_ffn_ref(x, W, b, ids, weights):
        import jax, jax.numpy as jnp
        import numpy as np
        Wsel = W[ids]
        bsel = b[ids]
        out = jnp.einsum('k,kod,bsd->bso', weights, Wsel, x)
        out = out + jnp.einsum('k,ko->o', weights, bsel)
        return out
    x = x + _L0_xattn_ref(_layernorm(x, axis=-1), ctx_1024, ctx_1024, L0_xattn_Wq, L0_xattn_bq, L0_xattn_Wk, L0_xattn_bk, L0_xattn_Wv, L0_xattn_bv, L0_xattn_Wo, L0_xattn_bo)
    x = x + _L0_ffn_ref(_layernorm(x, axis=-1), L0_ffn_wg, L0_ffn_w1, L0_ffn_b1, L0_ffn_w2, L0_ffn_b2)
    x = x + _L1_xattn_ref(_layernorm(x, axis=-1), ctx_1024, ctx_1024, mask_Bx1xS2_ik1, L1_xattn_Wq, L1_xattn_bq, L1_xattn_Wk, L1_xattn_bk, L1_xattn_Wv, L1_xattn_bv, L1_xattn_Wo, L1_xattn_bo, L1_xattn_g0, L1_xattn_beta0)
    x = x + _L1_ffn_ref(_layernorm(x, axis=-1), L1_ffn_W, L1_ffn_b, L1_ffn_ids, L1_ffn_weights)
    return x

_drawn_inputs = setup_inputs


def setup_inputs(seed=0):
    import zlib

    import numpy as np

    out = dict(_drawn_inputs(seed))
    spreads = {'L0_ffn_b1': (0.0, 0.639),
     'L0_ffn_b2': (0.0, 0.1),
     'L1_xattn_bq': (0.0, 0.289),
     'L1_xattn_bk': (0.0, 0.8),
     'L1_xattn_bv': (0.0, 0.1),
     'L1_xattn_bo': (0.0, 0.1),
     'L1_xattn_g0': (1.0, 0.2),
     'L1_xattn_beta0': (0.0, 0.1)}
    factors = {'L0_xattn_bq': 8.0, 'L0_xattn_bk': 8.0}
    for name, (base, spread) in spreads.items():
        noise = np.random.default_rng([zlib.crc32(name.encode()), seed]).standard_normal(out[name].shape)
        drawn = base * np.exp(spread * noise) if base else spread * noise
        out[name] = jnp.asarray(drawn.astype(out[name].dtype))
    for name, factor in factors.items():
        out[name] = (out[name] * factor).astype(out[name].dtype)
    return out
```

```python
from contextlib import ExitStack

import numpy as np
import concourse.bass as bass
from concourse import mybir

F32 = mybir.dt.float32
BF16 = mybir.dt.bfloat16
I32 = mybir.dt.int32
ALU = mybir.AluOpType
ACT = mybir.ActivationFunctionType
AX = mybir.AxisListType.X

P = 128
SEQS, LEN, D = 32, 64, 128
TOKENS = SEQS * LEN
TILES = TOKENS // P
PER = 2
GROUPS = TILES // PER
GC = PER * P
NSEQ = PER * P // LEN
TOPK = int(np.log(LEN))
PAD = 68
EXPERTS, HID = 8, 512
HC = HID // P
CAP = -(-2 * TOKENS // EXPERTS)
SLOTS = EXPERTS * CAP
SC = CAP // P
ADAPTERS, PICKS = 32, 8
EPS = 1e-5
GATE_EPS = 1e-9
SCALE = float(1.0 / np.sqrt(np.float32(D)))
SENTINEL = -3e38
CHOSEN = 3e38
MASKED = -1e9
FOREIGN = -1e30


def dft_constants():
    t = np.arange(LEN)
    fwd = np.zeros((P, 2, 2, 32))
    c1 = np.zeros((2, 2, 32, 2, LEN))
    c2 = np.zeros((2, 2, 32, 2, LEN))
    for b in range(2):
        rows = slice(b * LEN, (b + 1) * LEN)
        for k in range(32):
            cos, sin = np.cos(2 * np.pi * k * t / LEN), np.sin(2 * np.pi * k * t / LEN)
            last = np.cos(np.pi * t)
            fwd[rows, 0, b, k] = cos
            fwd[rows, 1, b, k] = sin if k else last
            w = (2.0 if k else 1.0) / LEN
            c1[0, b, k, b] = w * cos
            c1[1, b, k, b] = w * (cos if k else last)
            if k:
                c2[0, b, k, b] = -w * sin
                c2[1, b, k, b] = w * sin
    fwd = fwd.reshape(P, P)
    turned = np.roll(fwd, -64, axis=1)
    return fwd, turned, c1.reshape(P, P), c2.reshape(P, P)


def constants():
    fwd, turned, c1, c2 = dft_constants()
    before = np.triu(np.ones((P, P)), 1)
    seq = np.arange(P) // LEN
    foreign = np.where(seq[:, None] == seq[None, :], 0.0, FOREIGN)
    small = np.zeros((P, P))
    small[:, 0:8] = np.arange(8)[None, :] * CAP
    small[:, 8:16] = 8 - np.arange(8)[None, :]
    small[:, 16] = np.arange(P)
    small[:, 17] = -0.5
    small[:, 18] = -0.5
    seg = np.ones((P, EXPERTS, 2 * TILES))
    seg[:, :, 0] = 0.0
    return np.concatenate([np.eye(P), fwd, turned, c1, c2, before, foreign, small, seg.reshape(P, -1)],
                          axis=1).astype(np.float32)


def build(nc, x, ctx, mask, Wq0, bq0, Wk0, bk0, Wv0, bv0, Wo0, bo0, wg, w1, b1, w2, b2,
          Wq1, bq1, Wk1, bk1, Wv1, bv1, Wo1, bo1, g0, beta0, WA, bA, ids, weights, consts, out):
    es = ExitStack()
    with es:
        def sb(name, shape, dt=F32):
            return es.enter_context(nc.sbuf_tensor(name, shape, dt))

        def pb(name):
            return es.enter_context(nc.psum_tensor(name, [P, 512], F32))

        def sem(name):
            return es.enter_context(nc.semaphore(name))

        xbuf = nc.dram_tensor("expert_rows_in", [SLOTS, D], F32, kind="Internal").ap()
        ybuf = nc.dram_tensor("expert_rows_out", [SLOTS, D], F32, kind="Internal").ap()

        cst = sb("cst", [P, 8 * P + EXPERTS * 2 * TILES])
        ident = cst[:, 0:128]
        fwd = cst[:, 128:256]
        turned = cst[:, 256:384]
        c1 = cst[:, 384:512]
        c2 = cst[:, 512:640]
        before = cst[:, 640:768]
        foreign = cst[:, 768:896]
        small = cst[:, 896:1024]
        slot0 = small[:, 0:8]
        prio = small[:, 8:16]
        lane = small[:, 16:17]
        neghalf = small[:, 17:19]
        segment = cst[:, 1024:1024 + 2 * TILES * EXPERTS]

        x_all = sb("x_all", [P, TILES, D])
        ctx_all = sb("ctx_all", [P, TILES, D])
        x1_all = sb("x1_all", [P, TILES, D])
        y_all = sb("y_all", [P, TILES, 2, D])
        v_all = y_all[:, :, 0, :]
        xh2_all = y_all[:, :, 1, :]
        wv0k0 = sb("wv0k0", [P, 2 * D])
        wq0 = sb("wq0", [P, D])
        wo0 = sb("wo0", [P, D])
        wg_s = sb("wg_s", [P, EXPERTS])
        biasf = sb("biasf", [P, 4 * D])
        bhi = sb("bhi", [P, 4 * D], BF16)
        bmid = sb("bmid", [P, 4 * D], BF16)
        bres = sb("bres", [P, 4 * D])
        bias3 = sb("bias3", [P, 4 * D], BF16)
        at_dc = sb("at_dc", [P, P], BF16)
        at_all = sb("at_all", [P, P], BF16)
        before16 = sb("before16", [P, P], BF16)
        ones16 = sb("ones16", [P, P], BF16)

        st = sb("st", [P, 2, 6])
        mv = sb("mv", [P, PER, 2])
        ve = sb("ve", [P, PER])
        rstd = sb("rstd", [P, PER])
        st2 = sb("st2", [P, 2, 6])
        mv2 = sb("mv2", [P, PER, 2])
        ve2 = sb("ve2", [P, PER])
        rstd2 = sb("rstd2", [P, PER])
        xh_g = sb("xh_g", [P, PER, D])
        ctx_g = sb("ctx_g", [P, PER, D])
        xf_g = sb("xf_g", [P, PER, P])
        cf_g = sb("cf_g", [P, PER, 192])
        q_g = sb("q_g", [P, PER, D])
        qk_g = sb("qk_g", [P, PER, 2, D])
        corr_g = sb("corr_g", [P, NSEQ, PAD])
        top = sb("top", [P, NSEQ, 16])
        picked = sb("picked", [P, NSEQ, PAD])
        diff_g = sb("diff_g", [P, NSEQ, LEN + 4])
        exp_g = sb("exp_g", [P, NSEQ, LEN + 4])
        ssum = sb("ssum", [P, NSEQ])
        rs_all = sb("rs_all", [P, GROUPS, NSEQ])
        s_g = sb("s_g", [P, NSEQ, LEN])
        sT_g = sb("sT_g", [P, GC])
        sv_g = sb("sv_g", [P, PER, 2, D])
        agg_g = sb("agg_g", [P, NSEQ, LEN])
        xh2_g = sb("xh2_g", [P, PER, D])
        xT2_g = sb("xT2_g", [P, GC])
        lg_all = sb("lg_all", [P, TILES, EXPERTS])

        sc_a = sb("sc_a", [P, TILES, EXPERTS])
        sc_b = sb("sc_b", [P, TILES, EXPERTS])
        sc_t = sb("sc_t", [P, TILES, EXPERTS])
        hot = sb("hot", [P, EXPERTS, 2, TILES])
        hot16 = sb("hot16", [P, EXPERTS, 2, TILES], BF16)
        col = sb("col", [P, 8, TILES])
        run_s = sb("run_s", [P, EXPERTS * 2 * TILES])
        where = sb("where", [P, EXPERTS, 2, TILES])
        prod = sb("prod", [P, EXPERTS, 2, TILES])
        pos = sb("pos", [P, 2, TILES])
        base = sb("base", [P, 2, TILES])
        keep = sb("keep", [P, 2, TILES])
        tmp2 = sb("tmp2", [P, 2, TILES])
        to_slot = sb("to_slot", [P, 2, TILES], I32)
        from_slot = sb("from_slot", [P, 2, TILES], I32)
        gate = sb("gate", [P, 2, TILES])
        zeros = sb("zeros", [P, 1024])

        w1_all = sb("w1_all", [P, EXPERTS, HID])
        w2_all = sb("w2_all", [P, EXPERTS, HC, D])
        rows35 = sb("rows35", [35, P])
        cols35 = sb("cols35", [P, 35])
        b2_b = sb("b2_b", [P, EXPERTS, D])
        w1_g = sb("w1_g", [P, HID])
        xr_g = sb("xr_g", [P, SC, D])
        xrT_g = sb("xrT_g", [P, CAP])
        h_g = sb("h_g", [P, HC, CAP])
        y_g = sb("y_g", [P, SC, D])

        wq1 = sb("wq1", [P, D])
        wk1 = sb("wk1", [P, D])
        wv1 = sb("wv1", [P, D])
        wo1 = sb("wo1", [P, D])
        ctxT_g = sb("ctxT_g", [P, GC])
        vT_g = sb("vT_g", [P, GC])
        kT_all = sb("kT_all", [P, TILES, P])
        vw_all = sb("vw_all", [P, TILES, D])
        bo1_b = sb("bo1_b", [P, D])
        g0_b = sb("g0_b", [P, D])
        beta0_b = sb("beta0_b", [P, D])
        mask_i = sb("mask_i", [P, TILES, LEN], I32)
        live = sb("live", [P, TILES, P])
        penalty = sb("penalty", [P, TILES, P])
        ids_b = sb("ids_b", [P, PICKS], I32)
        w_b = sb("w_b", [P, PICKS])
        ids_c = sb("ids_c", [PICKS, 1], I32)
        w_c = sb("w_c", [PICKS, 1])
        w_rep = sb("w_rep", [PICKS, P])
        b_sel = sb("b_sel", [PICKS, D])
        a_idx = sb("a_idx", [P, PICKS], I32)
        a_rows = sb("a_rows", [P, PICKS, D])
        a_sum = sb("a_sum", [P, D])
        a_mat = sb("a_mat", [P, D])
        a_bias = sb("a_bias", [P, D])
        xh3_g = sb("xh3_g", [P, PER, D])
        xT3_g = sb("xT3_g", [P, GC])
        qT_g = sb("qT_g", [P, GC])
        sc_g = sb("sc_g", [P, PER, P])
        nmax = sb("nmax", [P, PER])
        p_g = sb("p_g", [P, PER, P])
        psums = sb("psums", [P, PER])
        prec = sb("prec", [P, PER])
        pT_g = sb("pT_g", [P, GC])
        o_g = sb("o_g", [P, PER, D])
        st3 = sb("st3", [P, 2, 6])
        mv3 = sb("mv3", [P, PER, 2])
        ve3 = sb("ve3", [P, PER])
        rstd3 = sb("rstd3", [P, PER])
        xh4_g = sb("xh4_g", [P, PER, D])
        xT4_g = sb("xT4_g", [P, GC])
        fin_g = sb("fin_g", [P, PER, D])
        warm = sb("warm", [P, 1])

        bank = [pb(f"bank{i}") for i in range(8)]

        s_c_in = sem("s_c_in")
        s_x_in0 = sem("s_x_in0")
        s_x_in1 = sem("s_x_in1")
        s_ctx_in0 = sem("s_ctx_in0")
        s_ctx_in1 = sem("s_ctx_in1")
        s_w0_in = sem("s_w0_in")
        s_wg_in = sem("s_wg_in")
        s_b0_in = sem("s_b0_in")
        s_w1_in = sem("s_w1_in")
        s_w2_in = sem("s_w2_in")
        s_rows_in = sem("s_rows_in")
        s_b2_in = sem("s_b2_in")
        s_l1w_in = sem("s_l1w_in")
        s_vec_in = sem("s_vec_in")
        s_mask_in = sem("s_mask_in")
        s_ad_in = sem("s_ad_in")
        s_zf_out = sem("s_zf_out")
        s_pset = sem("s_pset")
        s_bset = sem("s_bset")
        s_zset = sem("s_zset")
        s_ctx_copied = sem("s_ctx_copied")
        s_var1 = sem("s_var1")
        s_rstd1 = sem("s_rstd1")
        s_xh = sem("s_xh")
        s_dft = sem("s_dft")
        s_dft_ev = sem("s_dft_ev")
        s_proj = sem("s_proj")
        s_q_ev = sem("s_q_ev")
        s_qk = sem("s_qk")
        s_corr = sem("s_corr")
        s_corr_ev = sem("s_corr_ev")
        s_maxed = sem("s_maxed")
        s_exped = sem("s_exped")
        s_chosen = sem("s_chosen")
        s_sT = sem("s_sT")
        s_sT_ev = sem("s_sT_ev")
        s_spec = sem("s_spec")
        s_sv = sem("s_sv")
        s_inv = sem("s_inv")
        s_agg = sem("s_agg")
        s_outp = sem("s_outp")
        s_x1 = sem("s_x1")
        s_var2 = sem("s_var2")
        s_rstd2_ok = sem("s_rstd2_ok")
        s_xh2 = sem("s_xh2")
        s_xh2_kept = sem("s_xh2_kept")
        s_xT2 = sem("s_xT2")
        s_xT2_ev = sem("s_xT2_ev")
        s_logit = sem("s_logit")
        s_logit_ev = sem("s_logit_ev")
        s_lg_exp = sem("s_lg_exp")
        s_onehot = sem("s_onehot")
        s_counted = sem("s_counted")
        s_slots = sem("s_slots")
        s_scat = sem("s_scat")
        s_ctx2 = sem("s_ctx2")
        s_ctxT = sem("s_ctxT")
        s_ctxT_ev = sem("s_ctxT_ev")
        s_kp = sem("s_kp")
        s_kp_ev = sem("s_kp_ev")
        s_vw = sem("s_vw")
        s_vw_ev = sem("s_vw_ev")
        s_cT = sem("s_cT")
        s_cT_ev = sem("s_cT_ev")
        s_aidx = sem("s_aidx")
        s_ag = sem("s_ag")
        s_abg = sem("s_abg")
        s_asum = sem("s_asum")
        s_aT = sem("s_aT")
        s_aT_ev = sem("s_aT_ev")
        s_wrep = sem("s_wrep")
        s_xr_in = sem("s_xr_in")
        s_xrT = sem("s_xrT")
        s_xrT_ev = sem("s_xrT_ev")
        s_w1c = sem("s_w1c")
        s_f1 = sem("s_f1")
        s_gelu = sem("s_gelu")
        s_f2 = sem("s_f2")
        s_y = sem("s_y")
        s_y_out = sem("s_y_out")
        s_x2 = sem("s_x2")
        s_var3 = sem("s_var3")
        s_rstd3_ok = sem("s_rstd3_ok")
        s_xh3 = sem("s_xh3")
        s_xT3 = sem("s_xT3")
        s_xT3_ev = sem("s_xT3_ev")
        s_qp = sem("s_qp")
        s_qp_ev = sem("s_qp_ev")
        s_scr = sem("s_scr")
        s_scr_max = sem("s_scr_max")
        s_p_ok = sem("s_p_ok")
        s_pT = sem("s_pT")
        s_pT_ev = sem("s_pT_ev")
        s_pv = sem("s_pv")
        s_o = sem("s_o")
        s_varo = sem("s_varo")
        s_rstdo_ok = sem("s_rstdo_ok")
        s_var4 = sem("s_var4")
        s_rstd4_ok = sem("s_rstd4_ok")
        s_xh4 = sem("s_xh4")
        s_xT4 = sem("s_xT4")
        s_xT4_ev = sem("s_xT4_ev")
        s_ad = sem("s_ad")
        s_fin = sem("s_fin")
        s_out_done = sem("s_out_done")
        g_in = [sem(f"s_gather{i}") for i in range(2)]

        def tiles(t, g):
            return t[:, bass.ds(PER * g, PER), :]

        def tokens_of(ap):
            return ap.rearrange("(t b) l d -> (b l) t d", b=2)

        block = es.enter_context(nc.Block())

        FRONT, PICK, BACK, ROUTE = 0, 1, 2, 3
        LAST = GROUPS - 1

        def sweep(eng, step, lag, last=GROUPS):
            for j in range(lag + 1):
                step(j, j)
            with eng.Fori(lag + 1, last) as j:
                step(j, lag + 1)
            for j in range(last, GROUPS + lag):
                step(j, j)

        def sweep2(eng, step):
            for j in range(4):
                step(j, j)
            with eng.Fori(2, GROUPS // 2) as i:
                step(2 * i, 4)
                step(2 * i + 1, 5)
            step(GROUPS, GROUPS)
            step(GROUPS + 1, GROUPS + 1)

        def on(k, lag):
            return lag <= k <= LAST + lag

        @block.sync
        def _(sp):
            xv, cv = tokens_of(x), tokens_of(ctx)
            sp.dma_start(cst[:], consts).then_inc(s_c_in, 16)
            sp.dma_start(x_all[:, 0:4], xv[:, 0:4]).then_inc(s_x_in0, 16)
            sp.dma_start(ctx_all[:, 0:4], cv[:, 0:4]).then_inc(s_ctx_in0, 16)
            for w, dst in ((Wv0, wv0k0[:, 0:D]), (Wk0, wv0k0[:, D:2 * D]), (Wq0, wq0[:]), (Wo0, wo0[:])):
                sp.dma_start(dst, w).then_inc(s_w0_in, 16)
            sp.dma_start(x_all[:, 4:16], xv[:, 4:16]).then_inc(s_x_in1, 16)
            sp.dma_start(ctx_all[:, 4:16], cv[:, 4:16]).then_inc(s_ctx_in1, 16)
            sp.dma_start(wg_s[:], wg).then_inc(s_wg_in, 16)
            sp.dma_start(rows35[0:32, :], b1.rearrange("e (c h) -> (e c) h", c=HC)).then_inc(s_rows_in, 16)
            for i, b in enumerate((bq1, bk1, bv1)):
                sp.dma_start(rows35[32 + i:33 + i, :], b.unsqueeze(0)).then_inc(s_rows_in, 16)
            for w, dst in ((Wq1, wq1), (Wk1, wk1), (Wv1, wv1), (Wo1, wo1)):
                sp.dma_start(dst[:], w).then_inc(s_l1w_in, 16)
            sp.dma_start(w1_all[:], w1.rearrange("e d h -> d e h")).then_inc(s_w1_in, 16)
            sp.dma_start(w2_all[:], w2.rearrange("e (c h) d -> h e c d", c=HC)).then_inc(s_w2_in, 16)
            sp.dma_start(b2_b[:].rearrange("p e d -> p (e d)"),
                         b2.rearrange("e d -> (e d)").partition_broadcast(P)).then_inc(s_b2_in, 16)
            sp.wait_ge(s_scat, 16 * 2 * TILES)

            def load_rows(e, first=False):
                if not first:
                    sp.wait_ge(s_xrT, e)
                sp.dma_start(xr_g[:], xbuf[bass.ds(e * CAP, CAP), :].rearrange("(p c) d -> p c d", c=SC)
                             ).then_inc(s_xr_in, 16)

            def store_rows(e):
                sp.wait_ge(s_y, e + 1)
                sp.dma_start(ybuf[bass.ds(e * CAP, CAP), :].rearrange("(p c) d -> p c d", c=SC), y_g[:]
                             ).then_inc(s_y_out, 16)

            load_rows(0, first=True)
            load_rows(1)
            with sp.Fori(2, EXPERTS) as e:
                load_rows(e)
                store_rows(e - 2)
            store_rows(EXPERTS - 2)
            store_rows(EXPERTS - 1)
            ov = tokens_of(out)
            with sp.Fori(0, GROUPS) as g:
                sp.wait_ge(s_fin, g + 1)
                sp.dma_start(tiles(ov, g), fin_g[:]).then_inc(s_out_done, 16)
            sp.wait_ge(s_out_done, 16 * GROUPS)
            sp.wait_ge(s_zf_out, 64)

        @block.gpsimd
        def _(pool):
            pool.memset(bias3[:], 0.0).then_inc(s_pset, 1)
            pool.memset(biasf[:], 0.0).then_inc(s_pset, 1)
            pool.memset(top[:], SENTINEL).then_inc(s_pset, 1)
            pool.memset(corr_g[:], SENTINEL).then_inc(s_pset, 1)
            pool.memset(ones16[:], 1.0).then_inc(s_pset, 1)
            pool.memset(zeros[:], 0.0).then_inc(s_zset, 1)
            pool.wait_ge(s_c_in, 16)

            def step(j, k):
                if on(k, FRONT):
                    if k in (0, 2):
                        pool.wait_ge(s_ctx_in0 if k == 0 else s_ctx_in1, 16)
                    if k > 0:
                        pool.wait_ge(s_dft, j)
                    pool.tensor_copy(ctx_g[:], tiles(ctx_all, j)).then_inc(s_ctx_copied, 1)
                if on(k, BACK):
                    pool.wait_ge(s_var2, j - 1)
                    pool.tensor_tensor(rstd2[:], ve2[:], neghalf, ALU.pow).then_inc(s_rstd2_ok, 1)
                    pool.wait_ge(s_xh2, j - 1)
                    pool.tensor_copy(tiles(xh2_all, j - 2), xh2_g[:]).then_inc(s_xh2_kept, 1)
                if k < LAST:
                    pool.wait_ge(s_var1, j + 2)
                    pool.tensor_tensor(rstd[:], ve[:], neghalf, ALU.pow).then_inc(s_rstd1, 1)

            pool.wait_ge(s_var1, 1)
            pool.tensor_tensor(rstd[:], ve[:], neghalf, ALU.pow).then_inc(s_rstd1, 1)
            sweep(pool, step, 2, LAST)

            pool.wait_ge(s_ad_in, 64)
            pool.wait_ge(s_aidx, 1)
            for i in range(PICKS):
                pool.indirect_dma_start(out=a_rows[:, i, :], out_offset=None, in_=WA.rearrange("a o d -> (a o) d"),
                                        in_offset=bass.IndirectOffsetOnAxis(ap=a_idx[:, i:i + 1], axis=0)
                                        ).then_inc(s_ag, 16)
            pool.indirect_dma_start(out=b_sel[:], out_offset=None, in_=bA,
                                    in_offset=bass.IndirectOffsetOnAxis(ap=ids_c[:], axis=0)).then_inc(s_abg, 16)
            pool.wait_ge(s_slots, 1)
            pool.wait_ge(s_zf_out, 64)
            pool.wait_ge(s_xh2_kept, GROUPS)
            for k in range(2):
                for t in range(TILES):
                    pool.indirect_dma_start(out=xbuf, in_=xh2_all[:, t, :], in_offset=None,
                                            out_offset=bass.IndirectOffsetOnAxis(ap=to_slot[:, k, t:t + 1], axis=0),
                                            bounds_check=SLOTS - 1, oob_is_err=False).then_inc(s_scat, 16)

            pool.wait_ge(s_w1_in, 16)

            def first_layer(e, first=False):
                if not first:
                    pool.wait_ge(s_f1, HC * e)
                pool.tensor_copy(w1_g[:], w1_all[:, bass.ds(e, 1), :].rearrange("p a h -> p (a h)")
                                 ).then_inc(s_w1c, 1)

            first_layer(0, first=True)
            with pool.Fori(1, EXPERTS) as e:
                first_layer(e)

            pool.wait_ge(s_y_out, 16 * EXPERTS)

            def gather(j, parity, tile):
                for k in range(2):
                    t = PER * j + tile
                    pool.indirect_dma_start(out=y_all[:, t, k, :], out_offset=None, in_=ybuf,
                                            in_offset=bass.IndirectOffsetOnAxis(
                                                ap=from_slot[:, k, t:t + 1], axis=0)
                                            ).then_inc(g_in[parity], 16)

            def step(j, k):
                if on(k, FRONT):
                    pool.wait_ge(s_var3, j + 1)
                    pool.tensor_tensor(rstd[:], ve[:], neghalf, ALU.pow).then_inc(s_rstd3_ok, 1)
                    if k < LAST:
                        if k > 0:
                            pool.wait_ge(s_x2, j)
                        gather(j + 1, (k + 1) % 2, 0)
                if on(k, 1):
                    pool.wait_ge(s_varo, j)
                    pool.tensor_tensor(rstd2[:], ve2[:], neghalf, ALU.pow).then_inc(s_rstdo_ok, 1)
                if k < LAST:
                    gather(j + 1, (k + 1) % 2, 1)
                if on(k, 1):
                    pool.wait_ge(s_var4, j)
                    pool.tensor_tensor(rstd3[:], ve3[:], neghalf, ALU.pow).then_inc(s_rstd4_ok, 1)

            for tile in range(PER):
                gather(0, 0, tile)
            for j in range(GROUPS + 1):
                step(j, j)

        @block.scalar
        def _(act):
            for i, b in enumerate((bv0, bk0, bq0, bo0)):
                if i == 0:
                    act.wait_ge(s_pset, 2)
                act.dma_start(biasf[0:65:32, i * D:(i + 1) * D], b.partition_broadcast(3)).then_inc(s_b0_in, 16)
            for v, dst in ((bo1, bo1_b), (g0, g0_b), (beta0, beta0_b)):
                act.dma_start(dst[:], v.partition_broadcast(P)).then_inc(s_vec_in, 16)
            act.dma_start(ids_b[:], ids.partition_broadcast(P)).then_inc(s_ad_in, 16)
            act.dma_start(w_b[:], weights.partition_broadcast(P)).then_inc(s_ad_in, 16)
            act.dma_start(ids_c[:], ids.unsqueeze(1)).then_inc(s_ad_in, 16)
            act.dma_start(w_c[:], weights.unsqueeze(1)).then_inc(s_ad_in, 16)
            for b in range(2):
                src = mask.rearrange("(t b) a l -> b (a t) l", b=2)[b]
                act.dma_start(mask_i[b * LEN:(b + 1) * LEN, :, :],
                              src.partition_broadcast(LEN)).then_inc(s_mask_in, 16)
            act.wait_ge(s_zset, 1)
            for i in range(4):
                act.dma_start(xbuf[i * 1024:(i + 1) * 1024, :].rearrange("(p r) d -> p (r d)", p=P), zeros[:]
                              ).then_inc(s_zf_out, 16)
            act.activation(warm[:], zeros[:, 0:1], ACT.Exp)
            act.wait_ge(s_pset, 5)

            def step(j, k):
                if on(k, ROUTE):
                    act.wait_ge(s_xT2, j - 2)
                    if k > 3:
                        act.wait_ge(s_logit, j - 3)
                    act.activation(xT2_g[:], bank[7][:, 0:GC], ACT.Copy).then_inc(s_xT2_ev, 1)
                if on(k, BACK):
                    act.wait_ge(s_sT, j - 1)
                    if k > 2:
                        act.wait_ge(s_spec, j - 2)
                    act.activation(sT_g[:], bank[4][:, 0:GC], ACT.Copy).then_inc(s_sT_ev, 1)
                if on(k, FRONT):
                    act.wait_ge(s_dft, j + 1)
                    if k > 0:
                        act.wait_ge(s_proj, j)
                    act.activation(xf_g[:], bank[0][:, 0:GC].rearrange("p (t f) -> p t f", t=PER), ACT.Copy)
                    cf = bank[0][:, GC:2 * GC].rearrange("p (t f) -> p t f", t=PER)
                    act.activation(cf_g[:, :, 0:128], cf, ACT.Copy)
                    act.activation(cf_g[:, :, 128:192], cf[:, :, 0:64], ACT.Copy).then_inc(s_dft_ev, 1)
                if on(k, PICK):
                    act.wait_ge(s_maxed, j)
                    if k > 1:
                        act.wait_ge(s_chosen, j - 1)
                    act.activation(exp_g[:], diff_g[:], ACT.Exp).then_inc(s_exped, 1)
                if on(k, FRONT):
                    act.wait_ge(s_proj, j + 1)
                    if k > 0:
                        act.wait_ge(s_qk, j)
                    for t in range(PER):
                        act.activation(q_g[:, t, :], bank[1 + t][:, 3 * D:4 * D], ACT.Copy)
                        act.activation(v_all[:, bass.ds(PER * j + t, 1), :], bank[1 + t][:, 0:D], ACT.Copy
                                       ).then_inc(s_q_ev, 1)
                if on(k, FRONT):
                    act.wait_ge(s_corr, j + 1)
                    if k > 0:
                        act.wait_ge(s_chosen, j)
                    act.activation(corr_g[:, :, 0:LEN], bank[3][:, 0:GC].rearrange("p (s l) -> p s l", s=NSEQ),
                                   ACT.Copy).then_inc(s_corr_ev, 1)
                if on(k, ROUTE):
                    act.wait_ge(s_logit, j - 2)
                    act.activation(tiles(lg_all, j - 3),
                                   bank[7][:, GC:GC + PER * EXPERTS].rearrange("p (t e) -> p t e", t=PER),
                                   ACT.Copy).then_inc(s_logit_ev, 1)

            sweep(act, step, 3)

            act.wait_ge(s_cT, 1)
            act.activation(cols35[:], bank[0][:, 0:35], ACT.Copy).then_inc(s_cT_ev, 1)
            act.wait_ge(s_lg_exp, 1)
            act.activation(sc_b[:], sc_a[:], ACT.Exp).then_inc(s_lg_exp, 1)
            act.wait_ge(s_cT_ev, 1)

            def keys_values(j):
                act.wait_ge(s_ctxT, j + 1)
                act.activation(ctxT_g[:], bank[1][:, 0:GC], ACT.Copy).then_inc(s_ctxT_ev, 1)
                act.wait_ge(s_kp, j + 1)
                act.activation(tiles(kT_all, j), bank[2][:, 0:GC].rearrange("p (t k) -> p t k", t=PER), ACT.Identity,
                               bias=cols35[:, 33:34])
                act.activation(vT_g[:], bank[2][:, GC:2 * GC], ACT.Identity,
                               bias=cols35[:, 34:35]).then_inc(s_kp_ev, 1)
                act.wait_ge(s_vw, j + 1)
                act.activation(tiles(vw_all, j), bank[3][:, 0:GC].rearrange("p (t d) -> p t d", t=PER), ACT.Copy
                               ).then_inc(s_vw_ev, 1)

            with act.Fori(0, GROUPS) as j:
                keys_values(j)

            act.wait_ge(s_aT, 1)
            act.activation(a_mat[:], bank[0][:, 128:256], ACT.Copy)
            act.activation(a_bias[:], bank[0][:, 256:384], ACT.Copy).then_inc(s_aT_ev, 1)

            def evict_rows(e, first=False):
                act.wait_ge(s_xrT, e + 1)
                if not first:
                    act.wait_ge(s_f1, HC * e)
                act.activation(xrT_g[:], bank[5][:, :], ACT.Copy).then_inc(s_xrT_ev, 1)

            def gelu(e, first=False):
                for c in range(HC):
                    act.wait_ge(s_f1, HC * e + c + 1)
                    if not first:
                        act.wait_ge(s_f2, e)
                    act.activation(h_g[:, c, :], bank[1 + c][:, :], ACT.Gelu,
                                   bias=cols35[:, bass.ds(HC * e + c, 1)]).then_inc(s_gelu, 1)

            evict_rows(0, first=True)
            gelu(0, first=True)
            evict_rows(1)
            with act.Fori(1, EXPERTS - 1) as e:
                gelu(e)
                evict_rows(e + 1)
            gelu(EXPERTS - 1)

            def step(j, k):
                if on(k, FRONT):
                    act.wait_ge(s_xT3, j + 1)
                    act.activation(xT3_g[:], bank[0][:, 0:GC], ACT.Copy).then_inc(s_xT3_ev, 1)
                if on(k, BACK):
                    act.wait_ge(s_xT4, j - 1)
                    act.activation(xT4_g[:], bank[5][:, 0:GC], ACT.Copy).then_inc(s_xT4_ev, 1)
                if on(k, PICK):
                    act.wait_ge(s_pT, j)
                    act.activation(pT_g[:], bank[1][:, 0:GC], ACT.Copy).then_inc(s_pT_ev, 1)
                if on(k, FRONT):
                    act.wait_ge(s_qp, j + 1)
                    act.activation(qT_g[:], bank[2][:, 0:GC], ACT.Identity, bias=cols35[:, 32:33]
                                   ).then_inc(s_qp_ev, 1)
                    act.wait_ge(s_scr_max, j + 1)
                    if k > 0:
                        act.wait_ge(s_o, j)
                    for t in range(PER):
                        last = act.activation(p_g[:, t, :], sc_g[:, t, :], ACT.Exp, bias=nmax[:, t:t + 1],
                                              accum_out=psums[:, t:t + 1])
                    last.then_inc(s_p_ok, 1)

            act.activation(warm[:], zeros[:, 0:1], ACT.Exp)
            sweep2(act, step)

        @block.tensor
        def _(pe):
            pe.wait_ge(s_c_in, 16)
            pe.wait_ge(s_w0_in, 64)
            pe.wait_ge(s_bset, 1)
            pe.wait_ge(s_pset, 5)

            def step(j, k):
                if on(k, ROUTE):
                    pe.wait_ge(s_xh2, j - 2)
                    if k > 3:
                        pe.wait_ge(s_logit_ev, j - 3)
                    for t in range(PER):
                        last = pe.transpose(bank[7][:, t * P:(t + 1) * P], xh2_g[:, t, :], ident)
                    last.then_inc(s_xT2, 1)
                if on(k, BACK):
                    pe.wait_ge(s_chosen, j - 1)
                    if k > 2:
                        pe.wait_ge(s_sT_ev, j - 2)
                    for t in range(PER):
                        last = pe.transpose(bank[4][:, t * P:(t + 1) * P],
                                            s_g[:, 2 * t:2 * t + 2, :].rearrange("p s l -> p (s l)"), ident)
                    last.then_inc(s_sT, 1)
                if on(k, FRONT):
                    pe.wait_ge(s_xh, j + 1)
                    pe.wait_ge(s_ctx_copied, j + 1)
                    if k > 0:
                        pe.wait_ge(s_dft_ev, j)
                    for t in range(PER):
                        pe.matmul(bank[0][:, t * P:(t + 1) * P], xh_g[:, t, :], fwd, start=True, stop=True)
                        last = pe.matmul(bank[0][:, GC + t * P:GC + (t + 1) * P], ctx_g[:, t, :], fwd,
                                         start=True, stop=True)
                    last.then_inc(s_dft, 1)
                if on(k, ROUTE):
                    pe.wait_ge(s_xT2_ev, j - 2)
                    if k == ROUTE:
                        pe.wait_ge(s_wg_in, 16)
                    for t in range(PER):
                        last = pe.matmul(bank[7][:, GC + t * EXPERTS:GC + (t + 1) * EXPERTS],
                                         xT2_g[:, t * P:(t + 1) * P], wg_s[:], start=True, stop=True)
                    last.then_inc(s_logit, 1)
                if on(k, BACK):
                    pe.wait_ge(s_sT_ev, j - 1)
                    if k > 2:
                        pe.wait_ge(s_sv, j - 2)
                    spec = bank[5][:, :].rearrange("p (t h d) -> p t h d", t=PER, h=2)
                    for h, basis in enumerate((fwd, turned)):
                        last = pe.matmul(spec[:, :, h, :], basis, sT_g[:].rearrange("p (t d) -> p t d", t=PER),
                                         start=True, stop=True)
                    last.then_inc(s_spec, 1)
                if on(k, FRONT):
                    pe.wait_ge(s_dft_ev, j + 1)
                    if k > 0:
                        pe.wait_ge(s_qk, j)
                    if k > 0:
                        pe.wait_ge(s_q_ev, PER * j)
                    for t in range(PER):
                        b = bank[1 + t]
                        pe.matmul(b[:, 0:2 * D], cf_g[:, t, 0:128], wv0k0[:], start=True, stop=False)
                        pe.matmul(b[:, 0:2 * D], at_dc[:], bias3[:, 0:2 * D], start=False, stop=True)
                        pe.matmul(b[:, 2 * D:3 * D], cf_g[:, t, 64:192], wv0k0[:, D:2 * D], start=True, stop=True)
                        pe.matmul(b[:, 3 * D:4 * D], xf_g[:, t, :], wq0[:], start=True, stop=False)
                        last = pe.matmul(b[:, 3 * D:4 * D], at_dc[:], bias3[:, 2 * D:3 * D], start=False, stop=True)
                    last.then_inc(s_proj, 1)
                if on(k, BACK):
                    pe.wait_ge(s_sv, j - 1)
                    if k > 2:
                        pe.wait_ge(s_agg, j - 2)
                    for t in range(PER):
                        pe.matmul(bank[6][:, t * P:(t + 1) * P], sv_g[:, t, 0, :], c1, start=True, stop=False)
                        last = pe.matmul(bank[6][:, t * P:(t + 1) * P], sv_g[:, t, 1, :], c2, start=False, stop=True)
                    last.then_inc(s_inv, 1)
                if on(k, FRONT):
                    pe.wait_ge(s_qk, j + 1)
                    if k > 0:
                        pe.wait_ge(s_corr_ev, j)
                    for t in range(PER):
                        pe.matmul(bank[3][:, t * P:(t + 1) * P], qk_g[:, t, 0, :], c1, start=True, stop=False)
                        last = pe.matmul(bank[3][:, t * P:(t + 1) * P], qk_g[:, t, 1, :], c2, start=False, stop=True)
                    last.then_inc(s_corr, 1)
                if on(k, BACK):
                    pe.wait_ge(s_agg, j - 1)
                    if k > 2:
                        pe.wait_ge(s_x1, j - 2)
                    for t in range(PER):
                        o = bank[6][:, GC + t * D:GC + (t + 1) * D]
                        pe.matmul(o, agg_g[:, 2 * t:2 * t + 2, :].rearrange("p s l -> p (s l)"), wo0[:],
                                  start=True, stop=False)
                        last = pe.matmul(o, at_all[:], bias3[:, 3 * D:4 * D], start=False, stop=True)
                    last.then_inc(s_outp, 1)

            sweep(pe, step, 3)

            pe.wait_ge(s_rows_in, 64)
            pe.wait_ge(s_dft_ev, GROUPS)
            pe.transpose(bank[0][:, 0:35], rows35[:], ident[0:35, 0:35]).then_inc(s_cT, 1)
            pe.wait_ge(s_onehot, 1)
            pe.matmul(bank[7][:, 0:256], before16[:], hot16[:].rearrange("p e k t -> p (e k t)"), start=True, stop=True)
            pe.matmul(bank[7][:, 256:512], ones16[:], hot16[:].rearrange("p e k t -> p (e k t)"),
                      start=True, stop=True).then_inc(s_counted, 1)

            pe.wait_ge(s_l1w_in, 64)
            pe.wait_ge(s_q_ev, PER * GROUPS)
            pe.wait_ge(s_qk, GROUPS)
            pe.wait_ge(s_corr_ev, GROUPS)

            def keys_values(j, first=False):
                pe.wait_ge(s_ctx2, j + 1)
                if not first:
                    pe.wait_ge(s_ctxT_ev, j)
                for t in range(PER):
                    last = pe.transpose(bank[1][:, t * P:(t + 1) * P], ctx_g[:, t, :], ident)
                last.then_inc(s_ctxT, 1)
                pe.wait_ge(s_ctxT_ev, j + 1)
                if not first:
                    pe.wait_ge(s_kp_ev, j)
                pe.matmul(bank[2][:, 0:GC], wk1[:], ctxT_g[:], start=True, stop=True)
                pe.matmul(bank[2][:, GC:2 * GC], wv1[:], ctxT_g[:], start=True, stop=True).then_inc(s_kp, 1)
                pe.wait_ge(s_kp_ev, j + 1)
                if not first:
                    pe.wait_ge(s_vw_ev, j)
                for t in range(PER):
                    last = pe.matmul(bank[3][:, t * D:(t + 1) * D], vT_g[:, t * P:(t + 1) * P], wo1[:],
                                     start=True, stop=True)
                last.then_inc(s_vw, 1)

            keys_values(0, True)
            with pe.Fori(1, GROUPS) as j:
                keys_values(j)

            pe.wait_ge(s_asum, 1)
            pe.wait_ge(s_wrep, 1)
            pe.wait_ge(s_abg, 16)
            pe.transpose(bank[0][:, 128:256], a_sum[:], ident)
            pe.matmul(bank[0][:, 256:384], w_rep[:], b_sel[:], start=True, stop=True).then_inc(s_aT, 1)

            def turn_rows(e, first=False):
                pe.wait_ge(s_xr_in, 16 * (e + 1))
                if not first:
                    pe.wait_ge(s_xrT_ev, e)
                for c in range(SC):
                    last = pe.transpose(bank[5][:, c * P:(c + 1) * P], xr_g[:, c, :], ident)
                last.then_inc(s_xrT, 1)

            def expert(e, turn=True, first=False):
                pe.wait_ge(s_xrT_ev, e + 1)
                pe.wait_ge(s_w1c, e + 1)
                for c in range(HC):
                    if not first:
                        pe.wait_ge(s_gelu, HC * (e - 1) + c + 1)
                    pe.matmul(bank[1 + c][:, :], w1_g[:, c * P:(c + 1) * P], xrT_g[:], start=True, stop=True
                              ).then_inc(s_f1, 1)
                if turn:
                    turn_rows(e + 1)
                if not first:
                    pe.wait_ge(s_y, e)
                for c in range(HC):
                    pe.wait_ge(s_gelu, HC * e + c + 1)
                    for s in range(SC):
                        last = pe.matmul(bank[6][:, s * D:(s + 1) * D], h_g[:, c, s * P:(s + 1) * P],
                                         w2_all[:, bass.ds(e, 1), c, :].rearrange("p a d -> p (a d)"),
                                         start=(c == 0 and s == 0), stop=(c == HC - 1), skip_group_check=True)
                last.then_inc(s_f2, 1)

            pe.wait_ge(s_vw_ev, GROUPS)
            pe.wait_ge(s_w2_in, 16)
            turn_rows(0, first=True)
            expert(0, first=True)
            with pe.Fori(1, EXPERTS - 1) as e:
                expert(e)
            expert(EXPERTS - 1, turn=False)

            def step(j, k):
                if on(k, FRONT):
                    pe.wait_ge(s_xh3, j + 1)
                    if k > 0:
                        pe.wait_ge(s_xT3_ev, j)
                    for t in range(PER):
                        last = pe.transpose(bank[0][:, t * P:(t + 1) * P], xh3_g[:, t, :], ident)
                    last.then_inc(s_xT3, 1)
                if on(k, BACK):
                    pe.wait_ge(s_xh4, j - 1)
                    if k > 2:
                        pe.wait_ge(s_xT4_ev, j - 2)
                    for t in range(PER):
                        last = pe.transpose(bank[5][:, t * P:(t + 1) * P], xh4_g[:, t, :], ident)
                    last.then_inc(s_xT4, 1)
                if on(k, PICK):
                    pe.wait_ge(s_p_ok, j)
                    if k > 1:
                        pe.wait_ge(s_pT_ev, j - 1)
                    for t in range(PER):
                        last = pe.transpose(bank[1][:, t * P:(t + 1) * P], p_g[:, t, :], ident)
                    last.then_inc(s_pT, 1)
                if on(k, FRONT):
                    pe.wait_ge(s_xT3_ev, j + 1)
                    if k > 0:
                        pe.wait_ge(s_qp_ev, j)
                    pe.matmul(bank[2][:, 0:GC], wq1[:], xT3_g[:], start=True, stop=True).then_inc(s_qp, 1)
                if on(k, BACK):
                    pe.wait_ge(s_xT4_ev, j - 1)
                    if k > 2:
                        pe.wait_ge(s_fin, j - 2)
                    for t in range(PER):
                        last = pe.matmul(bank[3][:, t * D:(t + 1) * D], xT4_g[:, t * P:(t + 1) * P], a_mat[:],
                                         start=True, stop=True)
                    last.then_inc(s_ad, 1)
                if on(k, PICK):
                    pe.wait_ge(s_pT_ev, j)
                    if k > 1:
                        pe.wait_ge(s_o, j - 1)
                    for t in range(PER):
                        last = pe.matmul(bank[4][:, t * D:(t + 1) * D], pT_g[:, t * P:(t + 1) * P],
                                         vw_all[:, bass.ds(PER * (j - 1) + t, 1), :].rearrange("p a d -> p (a d)"),
                                         start=True, stop=True)
                    last.then_inc(s_pv, 1)
                if on(k, FRONT):
                    pe.wait_ge(s_qp_ev, j + 1)
                    if k > 0:
                        pe.wait_ge(s_scr_max, j)
                    for t in range(PER):
                        last = pe.matmul(bank[7][:, t * P:(t + 1) * P], qT_g[:, t * P:(t + 1) * P],
                                         kT_all[:, bass.ds(PER * j + t, 1), :].rearrange("p a d -> p (a d)"),
                                         start=True, stop=True)
                    last.then_inc(s_scr, 1)

            pe.wait_ge(s_aT_ev, 1)
            sweep2(pe, step)

        @block.vector
        def _(v):
            v.memset(at_dc[:], 0.0)
            v.memset(at_all[:], 0.0)
            v.drain()
            for r in (0, 32, 64):
                v.memset(at_all[r:r + 1, :], 1.0)
                v.memset(at_dc[r:r + 1, 0:1], float(LEN))
                v.memset(at_dc[r:r + 1, 32:33], float(LEN))
            v.wait_ge(s_pset, 5)
            v.wait_ge(s_b0_in, 64)
            v.tensor_copy(bhi[:], biasf[:])
            v.drain()
            v.tensor_tensor(bres[:], biasf[:], bhi[:], ALU.subtract)
            v.drain()
            v.tensor_copy(bmid[:], bres[:])
            v.drain()
            v.tensor_tensor(bres[:], bres[:], bmid[:], ALU.subtract)
            v.tensor_copy(bias3[0:1, :], bhi[0:1, :])
            v.tensor_copy(bias3[32:33, :], bmid[32:33, :])
            v.drain()
            v.tensor_copy(bias3[64:65, :], bres[64:65, :]).then_inc(s_bset, 1)

            v.wait_ge(s_c_in, 16)
            v.wait_ge(s_ad_in, 64)
            v.tensor_scalar(a_idx[:], ids_b[:], float(D), lane, ALU.mult, ALU.add).then_inc(s_aidx, 1)
            v.tensor_scalar(w_rep[:], ident[0:PICKS, :], 0.0, w_c[:], ALU.mult, ALU.add).then_inc(s_wrep, 1)

            def stats(src, tile0, s, m, e, done):
                for t in range(PER):
                    v.bn_stats(s[:, t, :], src[:, bass.ds(tile0 + t, 1), :])
                v.drain()
                for t in range(PER):
                    v.bn_aggr(m[:, t, :], s[:, t, :])
                v.drain()
                v.tensor_scalar(e[:], m[:, :, 1], EPS, None, ALU.add).then_inc(done, 1)

            def normalise(dst, src, tile0, m, r):
                for t in range(PER):
                    last = v.tensor_scalar(dst[:, t, :], src[:, bass.ds(tile0 + t, 1), :], m[:, t, 0:1], r[:, t:t + 1],
                                           ALU.subtract, ALU.mult)
                return last

            def step(j, k):
                if on(k, FRONT):
                    v.wait_ge(s_rstd1, j + 1)
                    if k > 0:
                        v.wait_ge(s_dft, j)
                    normalise(xh_g, x_all, PER * j, mv, rstd).then_inc(s_xh, 1)
                if on(k, PICK):
                    v.wait_ge(s_corr_ev, j)
                    v.nop(nofuse=True)
                    for s in range(NSEQ):
                        v.max(top[:, s, 0:8], corr_g[:, s, 0:LEN])
                    v.drain()
                    if k > 1:
                        v.wait_ge(s_exped, j - 1)
                    first = top[:, :, 0:1]
                    v.tensor_tensor(diff_g[:, :, 0:LEN], corr_g[:, :, 0:LEN], first.to_broadcast([P, NSEQ, LEN]),
                                    ALU.subtract)
                    v.tensor_tensor(diff_g[:, :, LEN:LEN + TOPK], top[:, :, 0:TOPK],
                                    first.to_broadcast([P, NSEQ, TOPK]), ALU.subtract).then_inc(s_maxed, 1)
                if on(k, BACK):
                    v.wait_ge(s_spec, j - 1)
                    if k > 2:
                        v.wait_ge(s_inv, j - 2)
                    v.tensor_tensor(sv_g[:], tiles(v_all, j - 2).unsqueeze(2).to_broadcast([P, PER, 2, D]),
                                    bank[5][:, :].rearrange("p (t h d) -> p t h d", t=PER, h=2), ALU.mult
                                    ).then_inc(s_sv, 1)
                if on(k, PICK):
                    for s in range(NSEQ):
                        v.match_replace(out=picked[:, s, :],
                                        in_to_replace=top[:, s, :].rearrange("p (a b) -> p a b", a=2)[:, :, 0:TOPK],
                                        in_values=corr_g[:, s, :], imm_value=CHOSEN)
                    v.wait_ge(s_exped, j)
                    if k > 1:
                        v.wait_ge(s_sT, j - 1)
                    v.tensor_reduce(ssum[:], exp_g[:, :, LEN:LEN + TOPK], AX, ALU.add)
                    v.drain()
                    v.reciprocal(rs_all[:, bass.ds(j - 1, 1), :], ssum[:])
                    v.scalar_tensor_tensor(out=s_g[:], in0=picked[:, :, 0:LEN], scalar=CHOSEN / 2,
                                           in1=exp_g[:, :, 0:LEN], op0=ALU.is_ge, op1=ALU.mult
                                           ).then_inc(s_chosen, 1)
                if on(k, FRONT):
                    v.wait_ge(s_proj, j + 1)
                    v.wait_ge(s_q_ev, PER * (j + 1))
                    if k > 0:
                        v.wait_ge(s_corr, j)
                    for t in range(PER):
                        last = v.tensor_tensor(qk_g[:, t, :, :], q_g[:, t:t + 1, :].to_broadcast([P, 2, D]),
                                               bank[1 + t][:, D:3 * D].rearrange("p (h d) -> p h d", h=2), ALU.mult)
                    last.then_inc(s_qk, 1)
                if on(k, BACK):
                    v.wait_ge(s_inv, j - 1)
                    if k > 2:
                        v.wait_ge(s_outp, j - 2)
                    rs = rs_all[:, bass.ds(j - 2, 1), :].rearrange("p a s -> p (a s)").unsqueeze(2)
                    v.tensor_tensor(agg_g[:], bank[6][:, 0:GC].rearrange("p (s l) -> p s l", s=NSEQ),
                                    rs.to_broadcast([P, NSEQ, LEN]), ALU.mult).then_inc(s_agg, 1)
                if k < LAST:
                    if k == 1:
                        v.wait_ge(s_x_in1, 16)
                    stats(x_all, PER * (j + 1), st, mv, ve, s_var1)
                if on(k, BACK):
                    v.wait_ge(s_outp, j - 1)
                    v.tensor_tensor(tiles(x1_all, j - 2), bank[6][:, GC:2 * GC].rearrange("p (t d) -> p t d", t=PER),
                                    tiles(x_all, j - 2), ALU.add).then_inc(s_x1, 1)
                    v.drain()
                    stats(x1_all, PER * (j - 2), st2, mv2, ve2, s_var2)
                    v.wait_ge(s_rstd2_ok, j - 1)
                    if k > 2:
                        v.wait_ge(s_xT2, j - 2)
                    if k > 2:
                        v.wait_ge(s_xh2_kept, j - 2)
                    normalise(xh2_g, x1_all, PER * (j - 2), mv2, rstd2).then_inc(s_xh2, 1)

            v.wait_ge(s_c_in, 16)
            v.wait_ge(s_x_in0, 16)
            stats(x_all, 0, st, mv, ve, s_var1)
            v.tensor_copy(before16[:], before)
            sweep(v, step, 2, LAST)

            def whole(ap):
                return ap.unsqueeze(2).to_broadcast([P, TILES, EXPERTS])

            v.wait_ge(s_logit_ev, GROUPS)
            v.tensor_reduce(col[:, 0, :], lg_all[:], AX, ALU.max)
            v.drain()
            v.tensor_tensor(sc_a[:], lg_all[:], whole(col[:, 0, :]), ALU.subtract).then_inc(s_lg_exp, 1)
            v.wait_ge(s_lg_exp, 2)
            v.tensor_reduce(col[:, 1, :], sc_b[:], AX, ALU.add)
            v.drain()
            v.reciprocal(col[:, 2, :], col[:, 1, :])
            v.drain()
            v.tensor_tensor(sc_a[:], sc_b[:], whole(col[:, 2, :]), ALU.mult)
            v.drain()
            cur = sc_a
            for k in range(2):
                v.tensor_reduce(col[:, 3 + k, :], cur[:], AX, ALU.max)
                v.drain()
                v.tensor_tensor(sc_t[:], cur[:], whole(col[:, 3 + k, :]), ALU.is_equal)
                v.drain()
                v.tensor_tensor(sc_t[:], sc_t[:], prio.unsqueeze(1).to_broadcast([P, TILES, EXPERTS]), ALU.mult)
                v.drain()
                v.tensor_reduce(col[:, 5, :], sc_t[:], AX, ALU.max)
                v.drain()
                v.tensor_tensor(hot[:, :, k, :].rearrange("p e t -> p t e"), sc_t[:], whole(col[:, 5, :]),
                                ALU.is_equal)
                v.drain()
                if k == 0:
                    v.scalar_tensor_tensor(out=sc_b[:], in0=hot[:, :, 0, :].rearrange("p e t -> p t e"), scalar=-2.0,
                                           in1=sc_a[:], op0=ALU.mult, op1=ALU.add)
                    v.drain()
                    cur = sc_b
            v.tensor_copy(hot16[:], hot[:]).then_inc(s_onehot, 1)
            v.tensor_tensor(col[:, 6, :], col[:, 3, :], col[:, 4, :], ALU.add)
            v.drain()
            v.tensor_scalar(col[:, 6, :], col[:, 6, :], GATE_EPS, None, ALU.max)
            v.drain()
            v.reciprocal(col[:, 7, :], col[:, 6, :])
            v.drain()
            v.tensor_tensor(gate[:], col[:, 3:5, :], col[:, 7:8, :].to_broadcast([P, 2, TILES]), ALU.mult)
            v.wait_ge(s_counted, 1)
            flat = "p e k t -> p (e k t)"
            v.tensor_tensor_scan(run_s[:], segment, bank[7][:, 256:512], 0.0, ALU.mult, ALU.add)
            v.drain()
            v.tensor_tensor(run_s[:], run_s[:], bank[7][:, 256:512], ALU.subtract)
            v.drain()
            v.tensor_tensor(where[:].rearrange(flat), bank[7][:, 0:256], run_s[:], ALU.add)
            v.drain()
            for h, dst, add in ((0, pos, None), (1, base, slot0)):
                if h == 0:
                    v.tensor_tensor(prod[:], hot[:], where[:], ALU.mult)
                else:
                    v.tensor_tensor(prod[:].rearrange("p e k t -> p e (k t)"), hot[:].rearrange("p e k t -> p e (k t)"),
                                    slot0.unsqueeze(2).to_broadcast([P, EXPERTS, 2 * TILES]), ALU.mult)
                v.drain()
                v.tensor_reduce(dst[:], prod[:].rearrange("p e k t -> p k t e"), AX, ALU.add)
                v.drain()
            v.tensor_scalar(keep[:], pos[:], float(CAP), None, ALU.is_lt)
            v.drain()
            v.tensor_tensor(gate[:], gate[:], keep[:], ALU.mult)
            v.tensor_tensor(tmp2[:], pos[:], keep[:], ALU.mult)
            v.drain()
            v.tensor_tensor(from_slot[:], tmp2[:], base[:], ALU.add)
            v.drain()
            v.tensor_scalar(tmp2[:], keep[:], -float(SLOTS), float(SLOTS), ALU.mult, ALU.add)
            v.drain()
            v.tensor_tensor(tmp2[:], tmp2[:], base[:], ALU.add)
            v.drain()
            v.tensor_tensor(to_slot[:], tmp2[:], pos[:], ALU.add).then_inc(s_slots, 1)

            def copy_ctx(j, first=False):
                if not first:
                    v.wait_ge(s_ctxT, j)
                v.tensor_copy(ctx_g[:], tiles(ctx_all, j)).then_inc(s_ctx2, 1)

            copy_ctx(0, first=True)
            with v.Fori(1, GROUPS) as j:
                copy_ctx(j)

            v.wait_ge(s_ag, 16 * PICKS)
            v.tensor_scalar(a_sum[:], a_rows[:, 0, :], w_b[:, 0:1], None, ALU.mult)
            for i in range(1, PICKS):
                v.drain()
                last = v.scalar_tensor_tensor(out=a_sum[:], in0=a_rows[:, i, :], scalar=w_b[:, i:i + 1], in1=a_sum[:],
                                              op0=ALU.mult, op1=ALU.add)
            last.then_inc(s_asum, 1)

            v.wait_ge(s_mask_in, 32)
            for b in range(2):
                rows, mine, other = slice(b * LEN, (b + 1) * LEN), slice(b * LEN, (b + 1) * LEN),                     slice((1 - b) * LEN, (2 - b) * LEN)
                v.tensor_scalar(live[rows, :, mine], mask_i[rows], 0.0, None, ALU.not_equal)
                v.memset(live[rows, :, other], 0.0)
                v.memset(penalty[rows, :, other], FOREIGN)
            v.drain()
            for b in range(2):
                rows, mine = slice(b * LEN, (b + 1) * LEN), slice(b * LEN, (b + 1) * LEN)
                last = v.tensor_scalar(penalty[rows, :, mine], live[rows, :, mine], -MASKED, MASKED, ALU.mult, ALU.add)
            v.drain()

            v.wait_ge(s_b2_in, 16)

            def expert_out(e, first=False):
                v.wait_ge(s_f2, e + 1)
                if not first:
                    v.wait_ge(s_y_out, 16 * e)
                v.tensor_tensor(y_g[:], bank[6][:, :].rearrange("p (s d) -> p s d", s=SC),
                                b2_b[:, bass.ds(e, 1), :].to_broadcast([P, SC, D]), ALU.add).then_inc(s_y, 1)

            expert_out(0, first=True)
            with v.Fori(1, EXPERTS) as e:
                expert_out(e)

            v.wait_ge(s_vec_in, 48)

            def group_stats(src, s, m, e, done):
                for t in range(PER):
                    v.bn_stats(s[:, t, :], src[:, t, :])
                v.drain()
                for t in range(PER):
                    v.bn_aggr(m[:, t, :], s[:, t, :])
                v.drain()
                v.tensor_scalar(e[:], m[:, :, 1], EPS, None, ALU.add).then_inc(done, 1)

            def step(j, k):
                if on(k, FRONT):
                    v.wait_ge(g_in[k % 2], 64 * (j // 2 + 1) if isinstance(j, int) else 32 * (j - k % 2) + 64)
                    for c in range(2):
                        for t in range(PER):
                            last = v.scalar_tensor_tensor(
                                out=x1_all[:, bass.ds(PER * j + t, 1), :].rearrange("p a d -> p (a d)"),
                                in0=y_all[:, bass.ds(PER * j + t, 1), c, :].rearrange("p a d -> p (a d)"),
                                scalar=gate[:, c, bass.ds(PER * j + t, 1)],
                                in1=x1_all[:, bass.ds(PER * j + t, 1), :].rearrange("p a d -> p (a d)"),
                                op0=ALU.mult, op1=ALU.add)
                        if c == 0:
                            v.drain()
                    last.then_inc(s_x2, 1)
                    v.drain()
                    stats(x1_all, PER * j, st, mv, ve, s_var3)
                if on(k, BACK):
                    v.wait_ge(s_rstd4_ok, j - 1)
                    if k > 2:
                        v.wait_ge(s_xT4, j - 2)
                    normalise(xh4_g, x_all, PER * (j - 2), mv3, rstd3).then_inc(s_xh4, 1)
                if on(k, FRONT):
                    v.wait_ge(s_rstd3_ok, j + 1)
                    if k > 0:
                        v.wait_ge(s_xT3, j)
                    normalise(xh3_g, x1_all, PER * j, mv, rstd).then_inc(s_xh3, 1)
                if on(k, PICK):
                    v.wait_ge(s_p_ok, j)
                    v.reciprocal(prec[:], psums[:])
                    v.drain()
                    v.wait_ge(s_pv, j)
                    for t in range(PER):
                        last = v.scalar_tensor_tensor(out=o_g[:, t, :], in0=bank[4][:, t * D:(t + 1) * D],
                                                      scalar=prec[:, t:t + 1], in1=bo1_b[:], op0=ALU.mult, op1=ALU.add)
                    last.then_inc(s_o, 1)
                    v.drain()
                    group_stats(o_g, st2, mv2, ve2, s_varo)
                if on(k, BACK):
                    v.wait_ge(s_ad, j - 1)
                    if k > 2:
                        v.wait_ge(s_out_done, 16 * (j - 2))
                    v.tensor_tensor(fin_g[:], bank[3][:, 0:GC].rearrange("p (t d) -> p t d", t=PER),
                                    tiles(x_all, j - 2), ALU.add)
                    v.drain()
                    v.tensor_tensor(fin_g[:], fin_g[:], a_bias[:].unsqueeze(1).to_broadcast([P, PER, D]), ALU.add
                                    ).then_inc(s_fin, 1)
                if on(k, PICK):
                    v.wait_ge(s_rstdo_ok, j)
                    for t in range(PER):
                        v.tensor_scalar(o_g[:, t, :], o_g[:, t, :], mv2[:, t, 0:1], rstd2[:, t:t + 1],
                                        ALU.subtract, ALU.mult)
                    v.drain()
                    v.tensor_tensor(o_g[:], o_g[:], g0_b[:].unsqueeze(1).to_broadcast([P, PER, D]), ALU.mult)
                    v.drain()
                    v.tensor_tensor(o_g[:], o_g[:], beta0_b[:].unsqueeze(1).to_broadcast([P, PER, D]), ALU.add)
                    v.drain()
                    v.tensor_tensor(tiles(x_all, j - 1), o_g[:], tiles(x1_all, j - 1), ALU.add)
                    v.drain()
                    stats(x_all, PER * (j - 1), st3, mv3, ve3, s_var4)
                if on(k, FRONT):
                    v.wait_ge(s_scr, j + 1)
                    scr = bank[7][:, 0:GC].rearrange("p (t k) -> p t k", t=PER)
                    v.scalar_tensor_tensor(out=sc_g[:], in0=scr, scalar=SCALE, in1=tiles(live, j),
                                           op0=ALU.mult, op1=ALU.mult)
                    v.drain()
                    v.tensor_tensor(sc_g[:], sc_g[:], tiles(penalty, j), ALU.add)
                    v.drain()
                    v.tensor_reduce(nmax[:], sc_g[:], AX, ALU.max)
                    v.drain()
                    v.tensor_scalar(nmax[:], nmax[:], -1.0, None, ALU.mult).then_inc(s_scr_max, 1)

            sweep2(v, step)


_INS = ["x", "ctx_1024", "mask_Bx1xS2_ik1", "L0_xattn_Wq", "L0_xattn_bq", "L0_xattn_Wk", "L0_xattn_bk",
        "L0_xattn_Wv", "L0_xattn_bv", "L0_xattn_Wo", "L0_xattn_bo", "L0_ffn_wg", "L0_ffn_w1", "L0_ffn_b1",
        "L0_ffn_w2", "L0_ffn_b2", "L1_xattn_Wq", "L1_xattn_bq", "L1_xattn_Wk", "L1_xattn_bk", "L1_xattn_Wv",
        "L1_xattn_bv", "L1_xattn_Wo", "L1_xattn_bo", "L1_xattn_g0", "L1_xattn_beta0", "L1_ffn_W", "L1_ffn_b",
        "L1_ffn_ids", "L1_ffn_weights"]


def kernel(**inputs):
    import concourse.bacc as _bacc
    from concourse.bass_utils import run_bass_kernel_spmd as _run

    nc = _bacc.Bacc("TRN2", target_bir_lowering=False, num_devices=1)
    arrays, args = {}, []
    data = [(name, inputs[name]) for name in _INS] + [("constants", constants())]
    for name, a in data:
        a = np.ascontiguousarray(a)
        arrays[f"in_{name}"] = a
        args.append(nc.dram_tensor(f"in_{name}", a.shape, mybir.dt.from_np(a.dtype), kind="ExternalInput").ap())
    args.append(nc.dram_tensor("out_0", (SEQS, LEN, D), F32, kind="ExternalOutput").ap())
    build(nc, *args)
    r = _run(nc, [arrays], core_ids=[0])
    return r.results[0]["out_0"]
```

```python
from contextlib import ExitStack

import numpy as np
import concourse.bass as bass
from concourse import mybir

F32 = mybir.dt.float32
BF16 = mybir.dt.bfloat16
I32 = mybir.dt.int32
ALU = mybir.AluOpType
ACT = mybir.ActivationFunctionType
AX = mybir.AxisListType.X

P = 128
SEQS, LEN, D = 32, 64, 128
TOKENS = SEQS * LEN
TILES = TOKENS // P
PER = 2
GROUPS = TILES // PER
GC = PER * P
NSEQ = PER * P // LEN
TOPK = int(np.log(LEN))
PAD = 68
EXPERTS, HID = 8, 512
HC = HID // P
CAP = -(-2 * TOKENS // EXPERTS)
SLOTS = EXPERTS * CAP
SC = CAP // P
ADAPTERS, PICKS = 32, 8
EPS = 1e-5
GATE_EPS = 1e-9
SCALE = float(1.0 / np.sqrt(np.float32(D)))
SENTINEL = -3e38
CHOSEN = 3e38
MASKED = -1e9
FOREIGN = -1e30


def dft_constants():
    t = np.arange(LEN)
    fwd = np.zeros((P, 2, 2, 32))
    c1 = np.zeros((2, 2, 32, 2, LEN))
    c2 = np.zeros((2, 2, 32, 2, LEN))
    for b in range(2):
        rows = slice(b * LEN, (b + 1) * LEN)
        for k in range(32):
            cos, sin = np.cos(2 * np.pi * k * t / LEN), np.sin(2 * np.pi * k * t / LEN)
            last = np.cos(np.pi * t)
            fwd[rows, 0, b, k] = cos
            fwd[rows, 1, b, k] = sin if k else last
            w = (2.0 if k else 1.0) / LEN
            c1[0, b, k, b] = w * cos
            c1[1, b, k, b] = w * (cos if k else last)
            if k:
                c2[0, b, k, b] = -w * sin
                c2[1, b, k, b] = w * sin
    fwd = fwd.reshape(P, P)
    turned = np.roll(fwd, -64, axis=1)
    return fwd, turned, c1.reshape(P, P), c2.reshape(P, P)


def constants():
    fwd, turned, c1, c2 = dft_constants()
    before = np.triu(np.ones((P, P)), 1)
    seq = np.arange(P) // LEN
    foreign = np.where(seq[:, None] == seq[None, :], 0.0, FOREIGN)
    small = np.zeros((P, P))
    small[:, 0:8] = np.arange(8)[None, :] * CAP
    small[:, 8:16] = 8 - np.arange(8)[None, :]
    small[:, 16] = np.arange(P)
    small[:, 32:48] = -0.5
    seg = np.ones((P, EXPERTS, 2 * TILES))
    seg[:, :, 0] = 0.0
    return np.concatenate([np.eye(P), fwd, turned, c1, c2, before, foreign, small, seg.reshape(P, -1)],
                          axis=1).astype(np.float32)


def build(nc, x, ctx, mask, Wq0, bq0, Wk0, bk0, Wv0, bv0, Wo0, bo0, wg, w1, b1, w2, b2,
          Wq1, bq1, Wk1, bk1, Wv1, bv1, Wo1, bo1, g0, beta0, WA, bA, ids, weights, consts, out):
    es = ExitStack()
    with es:
        def sb(name, shape, dt=F32):
            return es.enter_context(nc.sbuf_tensor(name, shape, dt))

        def pb(name):
            return es.enter_context(nc.psum_tensor(name, [P, 512], F32))

        def sem(name):
            return es.enter_context(nc.semaphore(name))

        xbuf = nc.dram_tensor("expert_rows_in", [SLOTS, D], F32, kind="Internal").ap()
        ybuf = nc.dram_tensor("expert_rows_out", [SLOTS, D], F32, kind="Internal").ap()

        cst = sb("cst", [P, 8 * P + EXPERTS * 2 * TILES])
        ident = cst[:, 0:128]
        fwd = cst[:, 128:256]
        turned = cst[:, 256:384]
        c1 = cst[:, 384:512]
        c2 = cst[:, 512:640]
        before = cst[:, 640:768]
        foreign = cst[:, 768:896]
        small = cst[:, 896:1024]
        slot0 = small[:, 0:8]
        prio = small[:, 8:16]
        lane = small[:, 16:17]
        neghalf = small[:, 32:48]
        segment = cst[:, 1024:1024 + 2 * TILES * EXPERTS]

        x_all = sb("x_all", [P, TILES, D])
        ctx_all = sb("ctx_all", [P, TILES, D])
        x1_all = sb("x1_all", [P, TILES, D])
        y_all = sb("y_all", [P, TILES, 2, D])
        v_all = y_all[:, :, 0, :]
        xh2_all = y_all[:, :, 1, :]
        wv0k0 = sb("wv0k0", [P, 2 * D])
        wq0 = sb("wq0", [P, D])
        wo0 = sb("wo0", [P, D])
        wg_s = sb("wg_s", [P, EXPERTS])
        biasf = sb("biasf", [P, 4 * D])
        bhi = sb("bhi", [P, 4 * D], BF16)
        bmid = sb("bmid", [P, 4 * D], BF16)
        bres = sb("bres", [P, 4 * D])
        bias3 = sb("bias3", [P, 4 * D], BF16)
        at_dc = sb("at_dc", [P, P], BF16)
        at_all = sb("at_all", [P, P], BF16)
        before16 = sb("before16", [P, P], BF16)
        ones16 = sb("ones16", [P, P], BF16)

        st1 = sb("st1", [P, TILES, 6])
        mv1 = sb("mv1", [P, TILES, 2])
        ve1 = sb("ve1", [P, TILES])
        rstd1 = sb("rstd1", [P, TILES])
        nmr1 = sb("nmr1", [P, TILES])
        st2 = sb("st2", [P, 2, 6])
        mv2 = sb("mv2", [P, PER, 2])
        ve2 = sb("ve2", [P, PER])
        rstd2 = sb("rstd2", [P, PER])
        xh_g = sb("xh_g", [P, PER, D])
        ctx_g = sb("ctx_g", [P, PER, D])
        xf_g = sb("xf_g", [P, PER, P])
        cf_g = sb("cf_g", [P, PER, 192])
        q_g = sb("q_g", [P, PER, D])
        qk_g = sb("qk_g", [P, PER, 2, D])
        corr_g = sb("corr_g", [P, NSEQ, PAD])
        top = sb("top", [P, NSEQ, 16])
        picked = sb("picked", [P, NSEQ, PAD])
        diff_g = sb("diff_g", [P, NSEQ, LEN + 4])
        exp_g = sb("exp_g", [P, NSEQ, LEN + 4])
        ssum = sb("ssum", [P, NSEQ])
        rs_all = sb("rs_all", [P, GROUPS, NSEQ])
        s_g = sb("s_g", [P, NSEQ, LEN])
        sT_g = sb("sT_g", [P, GC])
        sv_g = sb("sv_g", [P, PER, 2, D])
        agg_g = sb("agg_g", [P, NSEQ, LEN])
        xh2_g = sb("xh2_g", [P, PER, D])
        xT2_g = sb("xT2_g", [P, GC])
        lg_all = sb("lg_all", [P, TILES, EXPERTS])

        sc_a = sb("sc_a", [P, TILES, EXPERTS])
        sc_b = sb("sc_b", [P, TILES, EXPERTS])
        sc_t = sb("sc_t", [P, TILES, EXPERTS])
        hot = sb("hot", [P, EXPERTS, 2, TILES])
        hot16 = sb("hot16", [P, EXPERTS, 2, TILES], BF16)
        col = sb("col", [P, 8, TILES])
        run_s = sb("run_s", [P, EXPERTS * 2 * TILES])
        where = sb("where", [P, EXPERTS, 2, TILES])
        prod = sb("prod", [P, EXPERTS, 2, TILES])
        pos = sb("pos", [P, 2, TILES])
        base = sb("base", [P, 2, TILES])
        keep = sb("keep", [P, 2, TILES])
        tmp2 = sb("tmp2", [P, 2, TILES])
        to_slot = sb("to_slot", [P, 2, TILES], I32)
        from_slot = sb("from_slot", [P, 2, TILES], I32)
        gate = sb("gate", [P, 2, TILES])
        zeros = sb("zeros", [P, 1024])

        w1_all = sb("w1_all", [P, EXPERTS, HID])
        w2_all = sb("w2_all", [P, EXPERTS, HC, D])
        rows35 = sb("rows35", [35, P])
        cols35 = sb("cols35", [P, 35])
        b2_b = sb("b2_b", [P, EXPERTS, D])
        w1_g = sb("w1_g", [P, HID])
        xr_g = sb("xr_g", [P, SC, D])
        xrT_g = sb("xrT_g", [P, CAP])
        h_g = sb("h_g", [P, HC, CAP])
        y_g = sb("y_g", [P, SC, D])

        wq1 = sb("wq1", [P, D])
        wk1 = sb("wk1", [P, D])
        wv1 = sb("wv1", [P, D])
        wo1 = sb("wo1", [P, D])
        ctxT_g = sb("ctxT_g", [P, GC])
        vT_g = sb("vT_g", [P, GC])
        kT_all = sb("kT_all", [P, TILES, P])
        vw_all = sb("vw_all", [P, TILES, D])
        bo1_b = sb("bo1_b", [P, D])
        g0_b = sb("g0_b", [P, D])
        beta0_b = sb("beta0_b", [P, D])
        mask_i = sb("mask_i", [P, TILES, LEN], I32)
        live = sb("live", [P, TILES, P])
        penalty = sb("penalty", [P, TILES, P])
        ids_b = sb("ids_b", [P, PICKS], I32)
        w_b = sb("w_b", [P, PICKS])
        ids_c = sb("ids_c", [PICKS, 1], I32)
        w_c = sb("w_c", [PICKS, 1])
        w_rep = sb("w_rep", [P, P])
        b_sel = sb("b_sel", [P, D])
        a_idx = sb("a_idx", [P, PICKS], I32)
        a_rows = sb("a_rows", [P, PICKS, D])
        a_sum = sb("a_sum", [P, D])
        a_mat = sb("a_mat", [P, D])
        xh3_g = sb("xh3_g", [P, PER, D])
        xT3_g = sb("xT3_g", [P, GC])
        qT_g = sb("qT_g", [P, GC])
        sc_g = sb("sc_g", [P, PER, P])
        nmax = sb("nmax", [P, PER])
        p_g = sb("p_g", [P, PER, P])
        psums = sb("psums", [P, PER])
        prec = sb("prec", [P, PER])
        pT_g = sb("pT_g", [P, GC])
        o_g = sb("o_g", [P, PER, D])
        t_g = sb("t_g", [P, PER, D])
        st3 = sb("st3", [P, 3, PER, 6])
        mv3 = sb("mv3", [P, 3, PER, 2])
        ve3 = sb("ve3", [P, 3 * PER])
        rstd3 = sb("rstd3", [P, 3, PER])
        nmr3 = sb("nmr3", [P, 3, PER])
        xh4_g = sb("xh4_g", [P, PER, D])
        xT4_g = sb("xT4_g", [P, GC])
        fin_g = sb("fin_g", [P, PER, D])
        warm = sb("warm", [P, 1])

        bank = [pb(f"bank{i}") for i in range(8)]

        s_c_in = sem("s_c_in")
        s_x_in0 = sem("s_x_in0")
        s_x_in1 = sem("s_x_in1")
        s_ctx_in0 = sem("s_ctx_in0")
        s_ctx_in1 = sem("s_ctx_in1")
        s_w0_in = sem("s_w0_in")
        s_wg_in = sem("s_wg_in")
        s_b0_in = sem("s_b0_in")
        s_w1_in = sem("s_w1_in")
        s_w2_in = sem("s_w2_in")
        s_rows_in = sem("s_rows_in")
        s_b2_in = sem("s_b2_in")
        s_l1w_in = sem("s_l1w_in")
        s_vec_in = sem("s_vec_in")
        s_mask_in = sem("s_mask_in")
        s_ad_in = sem("s_ad_in")
        s_zf_out = sem("s_zf_out")
        s_pset = sem("s_pset")
        s_bset = sem("s_bset")
        s_zset = sem("s_zset")
        s_ctx_copied = sem("s_ctx_copied")
        s_var1 = sem("s_var1")
        s_rstd1 = sem("s_rstd1")
        s_nmr1 = sem("s_nmr1")
        s_xh = sem("s_xh")
        s_dft = sem("s_dft")
        s_dft_ev = sem("s_dft_ev")
        s_proj = sem("s_proj")
        s_q_ev = sem("s_q_ev")
        s_qk = sem("s_qk")
        s_corr = sem("s_corr")
        s_corr_ev = sem("s_corr_ev")
        s_maxed = sem("s_maxed")
        s_exped = sem("s_exped")
        s_chosen = sem("s_chosen")
        s_sT = sem("s_sT")
        s_sT_ev = sem("s_sT_ev")
        s_spec = sem("s_spec")
        s_sv = sem("s_sv")
        s_inv = sem("s_inv")
        s_agg = sem("s_agg")
        s_outp = sem("s_outp")
        s_x1 = sem("s_x1")
        s_var2 = sem("s_var2")
        s_rstd2_ok = sem("s_rstd2_ok")
        s_xh2 = sem("s_xh2")
        s_xh2_kept = sem("s_xh2_kept")
        s_xT2 = sem("s_xT2")
        s_xT2_ev = sem("s_xT2_ev")
        s_logit = sem("s_logit")
        s_logit_ev = sem("s_logit_ev")
        s_lg_exp = sem("s_lg_exp")
        s_onehot = sem("s_onehot")
        s_counted = sem("s_counted")
        s_slots = sem("s_slots")
        s_scat = sem("s_scat")
        s_ctx2 = sem("s_ctx2")
        s_ctxT = sem("s_ctxT")
        s_ctxT_ev = sem("s_ctxT_ev")
        s_kp = sem("s_kp")
        s_kp_ev = sem("s_kp_ev")
        s_vw = sem("s_vw")
        s_vw_ev = sem("s_vw_ev")
        s_cT = sem("s_cT")
        s_cT_ev = sem("s_cT_ev")
        s_aidx = sem("s_aidx")
        s_ag = sem("s_ag")
        s_abg = sem("s_abg")
        s_asum = sem("s_asum")
        s_aT = sem("s_aT")
        s_aT_ev = sem("s_aT_ev")
        s_wrep = sem("s_wrep")
        s_xr_in = sem("s_xr_in")
        s_xrT = sem("s_xrT")
        s_xrT_ev = sem("s_xrT_ev")
        s_w1c = sem("s_w1c")
        s_f1 = sem("s_f1")
        s_gelu = sem("s_gelu")
        s_f2 = sem("s_f2")
        s_y = sem("s_y")
        s_y_out = sem("s_y_out")
        s_x2 = sem("s_x2")
        s_var3 = sem("s_var3")
        s_nmr3 = sem("s_nmr3")
        s_x2b = sem("s_x2b")
        s_norm = sem("s_norm")
        s_rstd3_ok = sem("s_rstd3_ok")
        s_xh3 = sem("s_xh3")
        s_xT3 = sem("s_xT3")
        s_xT3_ev = sem("s_xT3_ev")
        s_qp = sem("s_qp")
        s_qp_ev = sem("s_qp_ev")
        s_scr = sem("s_scr")
        s_scr_max = sem("s_scr_max")
        s_p_ok = sem("s_p_ok")
        s_pT = sem("s_pT")
        s_pT_ev = sem("s_pT_ev")
        s_pv = sem("s_pv")
        s_o = sem("s_o")
        s_varo = sem("s_varo")
        s_rstdo_ok = sem("s_rstdo_ok")
        s_var4 = sem("s_var4")
        s_rstd4_ok = sem("s_rstd4_ok")
        s_xh4 = sem("s_xh4")
        s_xT4 = sem("s_xT4")
        s_xT4_ev = sem("s_xT4_ev")
        s_ad = sem("s_ad")
        s_fin = sem("s_fin")
        s_out_done = sem("s_out_done")
        g_in = [sem(f"s_gather{i}") for i in range(2)]

        def tiles(t, g):
            return t[:, bass.ds(PER * g, PER), :]

        def tokens_of(ap):
            return ap.rearrange("(t b) l d -> (b l) t d", b=2)

        block = es.enter_context(nc.Block())

        LAST = GROUPS - 1

        def sweep(eng, step, lag, last=GROUPS):
            for j in range(lag + 1):
                step(j, j)
            with eng.Fori(lag + 1, last) as j:
                step(j, lag + 1)
            for j in range(last, GROUPS + lag):
                step(j, j)

        def on(k, lag):
            return lag <= k <= LAST + lag

        @block.sync
        def _(sp):
            xv, cv = tokens_of(x), tokens_of(ctx)
            sp.dma_start(cst[:], consts).then_inc(s_c_in, 16)
            sp.dma_start(x_all[:, 0:4], xv[:, 0:4]).then_inc(s_x_in0, 16)
            sp.dma_start(ctx_all[:, 0:4], cv[:, 0:4]).then_inc(s_ctx_in0, 16)
            for w, dst in ((Wv0, wv0k0[:, 0:D]), (Wk0, wv0k0[:, D:2 * D]), (Wq0, wq0[:]), (Wo0, wo0[:])):
                sp.dma_start(dst, w).then_inc(s_w0_in, 16)
            sp.dma_start(x_all[:, 4:16], xv[:, 4:16]).then_inc(s_x_in1, 16)
            sp.dma_start(ctx_all[:, 4:16], cv[:, 4:16]).then_inc(s_ctx_in1, 16)
            sp.dma_start(wg_s[:], wg).then_inc(s_wg_in, 16)
            sp.dma_start(rows35[0:32, :], b1.rearrange("e (c h) -> (e c) h", c=HC)).then_inc(s_rows_in, 16)
            for i, b in enumerate((bq1, bk1, bv1)):
                sp.dma_start(rows35[32 + i:33 + i, :], b.unsqueeze(0)).then_inc(s_rows_in, 16)
            for w, dst in ((Wq1, wq1), (Wk1, wk1), (Wv1, wv1), (Wo1, wo1)):
                sp.dma_start(dst[:], w).then_inc(s_l1w_in, 16)
            sp.dma_start(w1_all[:], w1.rearrange("e d h -> d e h")).then_inc(s_w1_in, 16)
            sp.dma_start(w2_all[:], w2.rearrange("e (c h) d -> h e c d", c=HC)).then_inc(s_w2_in, 16)
            sp.dma_start(b2_b[:].rearrange("p e d -> p (e d)"),
                         b2.rearrange("e d -> (e d)").partition_broadcast(P)).then_inc(s_b2_in, 16)
            sp.wait_ge(s_scat, 16 * 2 * TILES)

            def load_rows(e, first=False):
                if not first:
                    sp.wait_ge(s_xrT, e)
                sp.dma_start(xr_g[:], xbuf[bass.ds(e * CAP, CAP), :].rearrange("(p c) d -> p c d", c=SC)
                             ).then_inc(s_xr_in, 16)

            def store_rows(e):
                sp.wait_ge(s_y, e + 1)
                sp.dma_start(ybuf[bass.ds(e * CAP, CAP), :].rearrange("(p c) d -> p c d", c=SC), y_g[:]
                             ).then_inc(s_y_out, 16)

            load_rows(0, first=True)
            load_rows(1)
            with sp.Fori(2, EXPERTS) as e:
                load_rows(e)
                store_rows(e - 2)
            store_rows(EXPERTS - 2)
            store_rows(EXPERTS - 1)
            ov = tokens_of(out)
            with sp.Fori(0, GROUPS) as g:
                sp.wait_ge(s_fin, g + 1)
                sp.dma_start(tiles(ov, g), fin_g[:]).then_inc(s_out_done, 16)
            sp.wait_ge(s_out_done, 16 * GROUPS)
            sp.wait_ge(s_zf_out, 64)

        @block.gpsimd
        def _(pool):
            pool.memset(bias3[:], 0.0).then_inc(s_pset, 1)
            pool.memset(b_sel[:], 0.0).then_inc(s_pset, 1)
            pool.memset(biasf[:], 0.0).then_inc(s_pset, 1)
            pool.memset(top[:], SENTINEL).then_inc(s_pset, 1)
            pool.memset(corr_g[:], SENTINEL).then_inc(s_pset, 1)
            pool.memset(ones16[:], 1.0).then_inc(s_pset, 1)
            pool.memset(zeros[:], 0.0).then_inc(s_zset, 1)
            pool.wait_ge(s_c_in, 16)

            def copy_ctx(j):
                if isinstance(j, int) and j in (0, 2):
                    pool.wait_ge(s_ctx_in0 if j == 0 else s_ctx_in1, 16)
                pool.tensor_copy(ctx_g[:], tiles(ctx_all, j)).then_inc(s_ctx_copied, 1)

            copy_ctx(0)
            for part in range(2):
                cols = slice(4 * part, 4 + 12 * part)
                pool.wait_ge(s_var1, part + 1)
                pool.tensor_tensor(rstd1[:, cols], ve1[:, cols], neghalf[:, cols], ALU.pow).then_inc(s_rstd1, 1)

            def step(j, k):
                if on(k, 4):
                    pool.wait_ge(s_xh2, j - 3)
                    pool.tensor_copy(tiles(xh2_all, j - 4), xh2_g[:]).then_inc(s_xh2_kept, 1)
                if k < LAST:
                    pool.wait_ge(s_dft, j + 1)
                    copy_ctx(j + 1)
                if on(k, 3):
                    pool.wait_ge(s_var2, j - 2)
                    pool.tensor_tensor(rstd2[:], ve2[:], neghalf[:, 0:PER], ALU.pow).then_inc(s_rstd2_ok, 1)

            sweep(pool, step, 4, LAST)

            pool.wait_ge(s_ad_in, 64)
            pool.wait_ge(s_aidx, 1)
            for i in range(PICKS):
                pool.indirect_dma_start(out=a_rows[:, i, :], out_offset=None, in_=WA.rearrange("a o d -> (a o) d"),
                                        in_offset=bass.IndirectOffsetOnAxis(ap=a_idx[:, i:i + 1], axis=0)
                                        ).then_inc(s_ag, 16)
            pool.indirect_dma_start(out=b_sel[0:PICKS, :], out_offset=None, in_=bA,
                                    in_offset=bass.IndirectOffsetOnAxis(ap=ids_c[:], axis=0)).then_inc(s_abg, 16)
            pool.wait_ge(s_slots, 1)
            pool.wait_ge(s_zf_out, 64)
            pool.wait_ge(s_xh2_kept, GROUPS)
            for k in range(2):
                for t in range(TILES):
                    pool.indirect_dma_start(out=xbuf, in_=xh2_all[:, t, :], in_offset=None,
                                            out_offset=bass.IndirectOffsetOnAxis(ap=to_slot[:, k, t:t + 1], axis=0),
                                            bounds_check=SLOTS - 1, oob_is_err=False).then_inc(s_scat, 16)

            pool.wait_ge(s_w1_in, 16)

            def first_layer(e, first=False):
                if not first:
                    pool.wait_ge(s_f1, HC * e)
                pool.tensor_copy(w1_g[:], w1_all[:, bass.ds(e, 1), :].rearrange("p a h -> p (a h)")
                                 ).then_inc(s_w1c, 1)

            first_layer(0, first=True)
            with pool.Fori(1, EXPERTS) as e:
                first_layer(e)

            pool.wait_ge(s_vec_in, 48)
            pool.wait_ge(s_y_out, 16 * EXPERTS)

            def gather(j, parity, tile):
                for k in range(2):
                    t = PER * j + tile
                    pool.indirect_dma_start(out=y_all[:, t, k, :], out_offset=None, in_=ybuf,
                                            in_offset=bass.IndirectOffsetOnAxis(
                                                ap=from_slot[:, k, t:t + 1], axis=0)
                                            ).then_inc(g_in[parity], 16)

            def step(j, k):
                if k < LAST:
                    if k > 0:
                        pool.wait_ge(s_x2, j)
                    for tile in range(PER):
                        gather(j + 1, (k + 1) % 2, tile)
                if k < GROUPS + 3:
                    pool.wait_ge(s_var3, j + 1)
                    if k > 0:
                        pool.wait_ge(s_norm, j)
                    pool.tensor_tensor(rstd3[:].rearrange("p n t -> p (n t)"), ve3[:], neghalf[:, 0:3 * PER], ALU.pow
                                       ).then_inc(s_rstd3_ok, 1)
                if on(k, 0):
                    pool.tensor_tensor(tiles(x_all, j), tiles(x1_all, j),
                                       beta0_b[:].unsqueeze(1).to_broadcast([P, PER, D]), ALU.add).then_inc(s_x2b, 1)

            for tile in range(PER):
                gather(0, 0, tile)
            for j in range(GROUPS + 3):
                step(j, j)

        @block.scalar
        def _(act):
            for i, b in enumerate((bv0, bk0, bq0, bo0)):
                if i == 0:
                    act.wait_ge(s_pset, 3)
                act.dma_start(biasf[0:65:32, i * D:(i + 1) * D], b.partition_broadcast(3)).then_inc(s_b0_in, 16)
            for v, dst in ((bo1, bo1_b), (g0, g0_b), (beta0, beta0_b)):
                act.dma_start(dst[:], v.partition_broadcast(P)).then_inc(s_vec_in, 16)
            act.dma_start(ids_b[:], ids.partition_broadcast(P)).then_inc(s_ad_in, 16)
            act.dma_start(w_b[:], weights.partition_broadcast(P)).then_inc(s_ad_in, 16)
            act.dma_start(ids_c[:], ids.unsqueeze(1)).then_inc(s_ad_in, 16)
            act.dma_start(w_c[:], weights.unsqueeze(1)).then_inc(s_ad_in, 16)
            for b in range(2):
                src = mask.rearrange("(t b) a l -> b (a t) l", b=2)[b]
                act.dma_start(mask_i[b * LEN:(b + 1) * LEN, :, :],
                              src.partition_broadcast(LEN)).then_inc(s_mask_in, 16)
            act.wait_ge(s_zset, 1)
            for i in range(4):
                act.dma_start(xbuf[i * 1024:(i + 1) * 1024, :].rearrange("(p r) d -> p (r d)", p=P), zeros[:]
                              ).then_inc(s_zf_out, 16)
            act.activation(warm[:], zeros[:, 0:1], ACT.Exp)
            act.wait_ge(s_pset, 6)

            def normalise(j):
                for t in range(PER):
                    last = act.activation(xh_g[:, t, :], x_all[:, bass.ds(PER * j + t, 1), :].rearrange("p a d -> p (a d)"),
                                          ACT.Identity, bias=nmr1[:, bass.ds(PER * j + t, 1)],
                                          scale=rstd1[:, bass.ds(PER * j + t, 1)])
                last.then_inc(s_xh, 1)

            act.wait_ge(s_nmr1, 1)
            normalise(0)

            def step(j, k):
                if on(k, 0):
                    act.wait_ge(s_dft, j + 1)
                    if k > 0:
                        act.wait_ge(s_proj, j)
                    act.activation(xf_g[:], bank[0][:, 0:GC].rearrange("p (t f) -> p t f", t=PER), ACT.Copy)
                    cf = bank[0][:, GC:2 * GC].rearrange("p (t f) -> p t f", t=PER)
                    act.activation(cf_g[:, :, 0:128], cf, ACT.Copy)
                    act.activation(cf_g[:, :, 128:192], cf[:, :, 0:64], ACT.Copy).then_inc(s_dft_ev, 1)
                if k < LAST:
                    if k == 1:
                        act.wait_ge(s_nmr1, 2)
                    normalise(j + 1)
                if on(k, 2):
                    act.wait_ge(s_sT, j - 1)
                    if k > 2:
                        act.wait_ge(s_spec, j - 2)
                    act.activation(sT_g[:], bank[4][:, 0:GC], ACT.Copy).then_inc(s_sT_ev, 1)
                if on(k, 4):
                    act.wait_ge(s_xT2, j - 3)
                    if k > 4:
                        act.wait_ge(s_logit, j - 4)
                    act.activation(xT2_g[:], bank[7][:, 0:GC], ACT.Copy).then_inc(s_xT2_ev, 1)
                if on(k, 1):
                    act.wait_ge(s_corr, j)
                    if k > 1:
                        act.wait_ge(s_chosen, j - 1)
                    act.activation(corr_g[:, :, 0:LEN], bank[3][:, 0:GC].rearrange("p (s l) -> p s l", s=NSEQ),
                                   ACT.Copy).then_inc(s_corr_ev, 1)
                    act.wait_ge(s_maxed, j)
                    act.activation(exp_g[:], diff_g[:], ACT.Exp).then_inc(s_exped, 1)
                if on(k, 0):
                    act.wait_ge(s_proj, j + 1)
                    if k > 0:
                        act.wait_ge(s_qk, j)
                    for t in range(PER):
                        act.activation(q_g[:, t, :], bank[1 + t][:, 3 * D:4 * D], ACT.Copy)
                        act.activation(v_all[:, bass.ds(PER * j + t, 1), :], bank[1 + t][:, 0:D], ACT.Copy
                                       ).then_inc(s_q_ev, 1)
                if on(k, 4):
                    act.wait_ge(s_logit, j - 3)
                    act.activation(tiles(lg_all, j - 4),
                                   bank[7][:, GC:GC + PER * EXPERTS].rearrange("p (t e) -> p t e", t=PER),
                                   ACT.Copy).then_inc(s_logit_ev, 1)

            sweep(act, step, 4, LAST)

            act.wait_ge(s_cT, 1)
            act.activation(cols35[:], bank[0][:, 0:35], ACT.Copy).then_inc(s_cT_ev, 1)
            act.wait_ge(s_lg_exp, 1)
            act.activation(sc_b[:], sc_a[:], ACT.Exp).then_inc(s_lg_exp, 1)
            act.wait_ge(s_cT_ev, 1)

            def keys_values(j):
                act.wait_ge(s_ctxT, j + 1)
                act.activation(ctxT_g[:], bank[1][:, 0:GC], ACT.Copy).then_inc(s_ctxT_ev, 1)
                act.wait_ge(s_kp, j + 1)
                act.activation(tiles(kT_all, j), bank[2][:, 0:GC].rearrange("p (t k) -> p t k", t=PER), ACT.Identity,
                               bias=cols35[:, 33:34])
                act.activation(vT_g[:], bank[2][:, GC:2 * GC], ACT.Identity,
                               bias=cols35[:, 34:35]).then_inc(s_kp_ev, 1)
                act.wait_ge(s_vw, j + 1)
                act.activation(tiles(vw_all, j), bank[3][:, 0:GC].rearrange("p (t d) -> p t d", t=PER), ACT.Copy
                               ).then_inc(s_vw_ev, 1)

            with act.Fori(0, GROUPS) as j:
                keys_values(j)

            act.wait_ge(s_aT, 1)
            act.activation(a_mat[:], bank[0][:, 128:256], ACT.Copy).then_inc(s_aT_ev, 1)

            def evict_rows(e, first=False):
                act.wait_ge(s_xrT, e + 1)
                if not first:
                    act.wait_ge(s_f1, HC * e)
                act.activation(xrT_g[:], bank[5][:, :], ACT.Copy).then_inc(s_xrT_ev, 1)

            def gelu(e, first=False):
                for c in range(HC):
                    act.wait_ge(s_f1, HC * e + c + 1)
                    if not first:
                        act.wait_ge(s_f2, e)
                    act.activation(h_g[:, c, :], bank[1 + c][:, :], ACT.Gelu,
                                   bias=cols35[:, bass.ds(HC * e + c, 1)]).then_inc(s_gelu, 1)

            evict_rows(0, first=True)
            gelu(0, first=True)
            evict_rows(1)
            with act.Fori(1, EXPERTS - 1) as e:
                gelu(e)
                evict_rows(e + 1)
            gelu(EXPERTS - 1)

            def normalise(dst, src, g, n):
                for t in range(PER):
                    last = act.activation(dst[:, t, :], src[:, bass.ds(PER * g + t, 1), :].rearrange("p a d -> p (a d)"),
                                          ACT.Identity, bias=nmr3[:, n, t:t + 1], scale=rstd3[:, n, t:t + 1])
                return last

            def step(j, k):
                if on(k, 2):
                    act.wait_ge(s_pT, j - 1)
                    if k > 2:
                        act.wait_ge(s_pv, j - 2)
                    act.activation(pT_g[:], bank[1][:, 0:GC], ACT.Copy).then_inc(s_pT_ev, 1)
                if on(k, 1):
                    act.wait_ge(s_xT3, j)
                    if k > 1:
                        act.wait_ge(s_qp, j - 1)
                    act.activation(xT3_g[:], bank[0][:, 0:GC], ACT.Copy).then_inc(s_xT3_ev, 1)
                if on(k, 4):
                    act.wait_ge(s_xT4, j - 3)
                    if k > 4:
                        act.wait_ge(s_ad, j - 4)
                    act.activation(xT4_g[:], bank[5][:, 0:GC], ACT.Copy).then_inc(s_xT4_ev, 1)
                if on(k, 1):
                    act.wait_ge(s_qp, j)
                    if k > 1:
                        act.wait_ge(s_scr, j - 1)
                    act.activation(qT_g[:], bank[2][:, 0:GC], ACT.Identity, bias=cols35[:, 32:33]
                                   ).then_inc(s_qp_ev, 1)
                if k < GROUPS + 3:
                    act.wait_ge(s_nmr3, j + 1)
                if on(k, 0):
                    if k > 0:
                        act.wait_ge(s_xT3, j)
                    last = normalise(xh3_g, x1_all, j, 0)
                if on(k, 3):
                    if k > 3:
                        act.wait_ge(s_xT4, j - 3)
                    last = normalise(xh4_g, x_all, j - 3, 2)
                if k < GROUPS + 3:
                    last.then_inc(s_norm, 1)
                if on(k, 1):
                    act.wait_ge(s_scr_max, j)
                    if k > 1:
                        act.wait_ge(s_o, j - 1)
                    for t in range(PER):
                        last = act.activation(p_g[:, t, :], sc_g[:, t, :], ACT.Exp, bias=nmax[:, t:t + 1],
                                              accum_out=psums[:, t:t + 1])
                    last.then_inc(s_p_ok, 1)

            act.activation(warm[:], zeros[:, 0:1], ACT.Exp)
            sweep(act, step, 4)

        @block.tensor
        def _(pe):
            pe.wait_ge(s_c_in, 16)
            pe.wait_ge(s_w0_in, 64)
            pe.wait_ge(s_bset, 1)
            pe.wait_ge(s_pset, 6)

            def step(j, k):
                if on(k, 0):
                    pe.wait_ge(s_xh, j + 1)
                    pe.wait_ge(s_ctx_copied, j + 1)
                    if k > 0:
                        pe.wait_ge(s_dft_ev, j)
                    for t in range(PER):
                        pe.matmul(bank[0][:, t * P:(t + 1) * P], xh_g[:, t, :], fwd, start=True, stop=True)
                        last = pe.matmul(bank[0][:, GC + t * P:GC + (t + 1) * P], ctx_g[:, t, :], fwd,
                                         start=True, stop=True)
                    last.then_inc(s_dft, 1)
                if on(k, 3):
                    pe.wait_ge(s_sv, j - 2)
                    if k > 3:
                        pe.wait_ge(s_x1, j - 3)
                    for t in range(PER):
                        pe.matmul(bank[6][:, t * P:(t + 1) * P], sv_g[:, t, 0, :], c1, start=True, stop=False)
                        last = pe.matmul(bank[6][:, t * P:(t + 1) * P], sv_g[:, t, 1, :], c2, start=False, stop=True)
                    last.then_inc(s_inv, 1)
                if on(k, 2):
                    pe.wait_ge(s_chosen, j - 1)
                    if k > 2:
                        pe.wait_ge(s_sT_ev, j - 2)
                    for t in range(PER):
                        last = pe.transpose(bank[4][:, t * P:(t + 1) * P],
                                            s_g[:, 2 * t:2 * t + 2, :].rearrange("p s l -> p (s l)"), ident)
                    last.then_inc(s_sT, 1)
                if on(k, 4):
                    pe.wait_ge(s_xh2, j - 3)
                    if k > 4:
                        pe.wait_ge(s_logit_ev, j - 4)
                    for t in range(PER):
                        last = pe.transpose(bank[7][:, t * P:(t + 1) * P], xh2_g[:, t, :], ident)
                    last.then_inc(s_xT2, 1)
                if on(k, 1):
                    pe.wait_ge(s_qk, j)
                    if k > 1:
                        pe.wait_ge(s_corr_ev, j - 1)
                    for t in range(PER):
                        pe.matmul(bank[3][:, t * P:(t + 1) * P], qk_g[:, t, 0, :], c1, start=True, stop=False)
                        last = pe.matmul(bank[3][:, t * P:(t + 1) * P], qk_g[:, t, 1, :], c2, start=False, stop=True)
                    last.then_inc(s_corr, 1)
                if on(k, 3):
                    pe.wait_ge(s_agg, j - 2)
                    for t in range(PER):
                        o = bank[6][:, GC + t * D:GC + (t + 1) * D]
                        pe.matmul(o, agg_g[:, 2 * t:2 * t + 2, :].rearrange("p s l -> p (s l)"), wo0[:],
                                  start=True, stop=False)
                        last = pe.matmul(o, at_all[:], bias3[:, 3 * D:4 * D], start=False, stop=True)
                    last.then_inc(s_outp, 1)
                if on(k, 0):
                    pe.wait_ge(s_dft_ev, j + 1)
                    if k > 0:
                        pe.wait_ge(s_qk, j)
                    if k > 0:
                        pe.wait_ge(s_q_ev, PER * j)
                    for t in range(PER):
                        b = bank[1 + t]
                        pe.matmul(b[:, 0:2 * D], cf_g[:, t, 0:128], wv0k0[:], start=True, stop=False)
                        pe.matmul(b[:, 0:2 * D], at_dc[:], bias3[:, 0:2 * D], start=False, stop=True)
                        pe.matmul(b[:, 2 * D:3 * D], cf_g[:, t, 64:192], wv0k0[:, D:2 * D], start=True, stop=True)
                        pe.matmul(b[:, 3 * D:4 * D], xf_g[:, t, :], wq0[:], start=True, stop=False)
                        last = pe.matmul(b[:, 3 * D:4 * D], at_dc[:], bias3[:, 2 * D:3 * D], start=False, stop=True)
                    last.then_inc(s_proj, 1)
                if on(k, 4):
                    pe.wait_ge(s_xT2_ev, j - 3)
                    if k == 4:
                        pe.wait_ge(s_wg_in, 16)
                    for t in range(PER):
                        last = pe.matmul(bank[7][:, GC + t * EXPERTS:GC + (t + 1) * EXPERTS],
                                         xT2_g[:, t * P:(t + 1) * P], wg_s[:], start=True, stop=True)
                    last.then_inc(s_logit, 1)
                if on(k, 2):
                    pe.wait_ge(s_sT_ev, j - 1)
                    if k > 2:
                        pe.wait_ge(s_sv, j - 2)
                    spec = bank[5][:, :].rearrange("p (t h d) -> p t h d", t=PER, h=2)
                    for h, basis in enumerate((fwd, turned)):
                        last = pe.matmul(spec[:, :, h, :], basis, sT_g[:].rearrange("p (t d) -> p t d", t=PER),
                                         start=True, stop=True)
                    last.then_inc(s_spec, 1)

            sweep(pe, step, 4)

            pe.wait_ge(s_rows_in, 64)
            pe.wait_ge(s_dft_ev, GROUPS)
            pe.transpose(bank[0][:, 0:35], rows35[:], ident[0:35, 0:35]).then_inc(s_cT, 1)
            pe.wait_ge(s_onehot, 1)
            pe.matmul(bank[7][:, 0:256], before16[:], hot16[:].rearrange("p e k t -> p (e k t)"), start=True, stop=True)
            pe.matmul(bank[7][:, 256:512], ones16[:], hot16[:].rearrange("p e k t -> p (e k t)"),
                      start=True, stop=True).then_inc(s_counted, 1)

            pe.wait_ge(s_l1w_in, 64)
            pe.wait_ge(s_q_ev, PER * GROUPS)
            pe.wait_ge(s_qk, GROUPS)
            pe.wait_ge(s_corr_ev, GROUPS)

            def keys_values(j, first=False):
                pe.wait_ge(s_ctx2, j + 1)
                if not first:
                    pe.wait_ge(s_ctxT_ev, j)
                for t in range(PER):
                    last = pe.transpose(bank[1][:, t * P:(t + 1) * P], ctx_g[:, t, :], ident)
                last.then_inc(s_ctxT, 1)
                pe.wait_ge(s_ctxT_ev, j + 1)
                if not first:
                    pe.wait_ge(s_kp_ev, j)
                pe.matmul(bank[2][:, 0:GC], wk1[:], ctxT_g[:], start=True, stop=True)
                pe.matmul(bank[2][:, GC:2 * GC], wv1[:], ctxT_g[:], start=True, stop=True).then_inc(s_kp, 1)
                pe.wait_ge(s_kp_ev, j + 1)
                if not first:
                    pe.wait_ge(s_vw_ev, j)
                for t in range(PER):
                    last = pe.matmul(bank[3][:, t * D:(t + 1) * D], vT_g[:, t * P:(t + 1) * P], wo1[:],
                                     start=True, stop=True)
                last.then_inc(s_vw, 1)

            keys_values(0, True)
            with pe.Fori(1, GROUPS) as j:
                keys_values(j)

            pe.wait_ge(s_asum, 1)
            pe.wait_ge(s_wrep, 1)
            pe.wait_ge(s_abg, 16)
            pe.transpose(bank[0][:, 128:256], a_sum[:], ident).then_inc(s_aT, 1)

            def turn_rows(e, first=False):
                pe.wait_ge(s_xr_in, 16 * (e + 1))
                if not first:
                    pe.wait_ge(s_xrT_ev, e)
                for c in range(SC):
                    last = pe.transpose(bank[5][:, c * P:(c + 1) * P], xr_g[:, c, :], ident)
                last.then_inc(s_xrT, 1)

            def expert(e, turn=True, first=False):
                pe.wait_ge(s_xrT_ev, e + 1)
                pe.wait_ge(s_w1c, e + 1)
                for c in range(HC):
                    if not first:
                        pe.wait_ge(s_gelu, HC * (e - 1) + c + 1)
                    pe.matmul(bank[1 + c][:, :], w1_g[:, c * P:(c + 1) * P], xrT_g[:], start=True, stop=True
                              ).then_inc(s_f1, 1)
                if turn:
                    turn_rows(e + 1)
                if not first:
                    pe.wait_ge(s_y, e)
                for c in range(HC):
                    pe.wait_ge(s_gelu, HC * e + c + 1)
                    for s in range(SC):
                        last = pe.matmul(bank[6][:, s * D:(s + 1) * D], h_g[:, c, s * P:(s + 1) * P],
                                         w2_all[:, bass.ds(e, 1), c, :].rearrange("p a d -> p (a d)"),
                                         start=(c == 0 and s == 0), stop=(c == HC - 1), skip_group_check=True)
                last.then_inc(s_f2, 1)

            pe.wait_ge(s_vw_ev, GROUPS)
            pe.wait_ge(s_w2_in, 16)
            turn_rows(0, first=True)
            expert(0, first=True)
            with pe.Fori(1, EXPERTS - 1) as e:
                expert(e)
            expert(EXPERTS - 1, turn=False)

            def step(j, k):
                if on(k, 2):
                    pe.wait_ge(s_p_ok, j - 1)
                    if k > 2:
                        pe.wait_ge(s_pT_ev, j - 2)
                    for t in range(PER):
                        last = pe.transpose(bank[1][:, t * P:(t + 1) * P], p_g[:, t, :], ident)
                    last.then_inc(s_pT, 1)
                if on(k, 1):
                    pe.wait_ge(s_norm, j)
                    if k > 1:
                        pe.wait_ge(s_xT3_ev, j - 1)
                    for t in range(PER):
                        last = pe.transpose(bank[0][:, t * P:(t + 1) * P], xh3_g[:, t, :], ident)
                    last.then_inc(s_xT3, 1)
                if on(k, 4):
                    pe.wait_ge(s_norm, j)
                    if k > 4:
                        pe.wait_ge(s_xT4_ev, j - 4)
                    for t in range(PER):
                        last = pe.transpose(bank[5][:, t * P:(t + 1) * P], xh4_g[:, t, :], ident)
                    last.then_inc(s_xT4, 1)
                if on(k, 2):
                    pe.wait_ge(s_pT_ev, j - 1)
                    if k > 2:
                        pe.wait_ge(s_o, j - 2)
                    for t in range(PER):
                        last = pe.matmul(bank[4][:, t * D:(t + 1) * D], pT_g[:, t * P:(t + 1) * P],
                                         vw_all[:, bass.ds(PER * (j - 2) + t, 1), :].rearrange("p a d -> p (a d)"),
                                         start=True, stop=True)
                    last.then_inc(s_pv, 1)
                if on(k, 1):
                    pe.wait_ge(s_xT3_ev, j)
                    if k > 1:
                        pe.wait_ge(s_qp_ev, j - 1)
                    pe.matmul(bank[2][:, 0:GC], wq1[:], xT3_g[:], start=True, stop=True).then_inc(s_qp, 1)
                if on(k, 4):
                    pe.wait_ge(s_xT4_ev, j - 3)
                    if k > 4:
                        pe.wait_ge(s_fin, j - 4)
                    for t in range(PER):
                        pe.matmul(bank[3][:, t * D:(t + 1) * D], xT4_g[:, t * P:(t + 1) * P], a_mat[:],
                                  start=True, stop=False)
                        last = pe.matmul(bank[3][:, t * D:(t + 1) * D], w_rep[:], b_sel[:], start=False, stop=True)
                    last.then_inc(s_ad, 1)
                if on(k, 1):
                    pe.wait_ge(s_qp_ev, j)
                    if k > 1:
                        pe.wait_ge(s_scr_max, j - 1)
                    for t in range(PER):
                        last = pe.matmul(bank[7][:, t * P:(t + 1) * P], qT_g[:, t * P:(t + 1) * P],
                                         kT_all[:, bass.ds(PER * (j - 1) + t, 1), :].rearrange("p a d -> p (a d)"),
                                         start=True, stop=True)
                    last.then_inc(s_scr, 1)

            pe.wait_ge(s_aT_ev, 1)
            sweep(pe, step, 4)

        @block.vector
        def _(v):
            v.memset(at_dc[:], 0.0)
            v.memset(at_all[:], 0.0)
            v.memset(w_rep[:], 0.0)
            v.memset(mv3[:], 0.0)
            v.memset(rstd3[:], 0.0)
            v.drain()
            for r in (0, 32, 64):
                v.memset(at_all[r:r + 1, :], 1.0)
                v.memset(at_dc[r:r + 1, 0:1], float(LEN))
                v.memset(at_dc[r:r + 1, 32:33], float(LEN))
            v.wait_ge(s_pset, 6)
            v.wait_ge(s_b0_in, 64)
            v.tensor_copy(bhi[:], biasf[:])
            v.drain()
            v.tensor_tensor(bres[:], biasf[:], bhi[:], ALU.subtract)
            v.drain()
            v.tensor_copy(bmid[:], bres[:])
            v.drain()
            v.tensor_tensor(bres[:], bres[:], bmid[:], ALU.subtract)
            v.tensor_copy(bias3[0:1, :], bhi[0:1, :])
            v.tensor_copy(bias3[32:33, :], bmid[32:33, :])
            v.drain()
            v.tensor_copy(bias3[64:65, :], bres[64:65, :]).then_inc(s_bset, 1)

            v.wait_ge(s_c_in, 16)
            v.wait_ge(s_ad_in, 64)
            v.tensor_scalar(a_idx[:], ids_b[:], float(D), lane, ALU.mult, ALU.add).then_inc(s_aidx, 1)
            v.tensor_scalar(w_rep[0:PICKS, :], ident[0:PICKS, :], 0.0, w_c[:], ALU.mult, ALU.add).then_inc(s_wrep, 1)

            v.wait_ge(s_x_in0, 16)
            for part in range(2):
                if part:
                    v.wait_ge(s_x_in1, 16)
                cols = slice(4 * part, 4 + 12 * part)
                for t in range(cols.start, cols.stop):
                    v.bn_stats(st1[:, t, :], x_all[:, t, :])
                v.drain()
                for t in range(cols.start, cols.stop):
                    v.bn_aggr(mv1[:, t, :], st1[:, t, :])
                v.drain()
                v.tensor_scalar(ve1[:, cols], mv1[:, cols, 1], EPS, None, ALU.add).then_inc(s_var1, 1)
                v.wait_ge(s_rstd1, part + 1)
                v.scalar_tensor_tensor(out=nmr1[:, cols], in0=mv1[:, cols, 0], scalar=-1.0, in1=rstd1[:, cols],
                                       op0=ALU.mult, op1=ALU.mult).then_inc(s_nmr1, 1)
            v.tensor_copy(before16[:], before)

            def step(j, k):
                if on(k, 4):
                    v.wait_ge(s_rstd2_ok, j - 3)
                    if k > 4:
                        v.wait_ge(s_xT2, j - 4)
                        v.wait_ge(s_xh2_kept, j - 4)
                    for t in range(PER):
                        last = v.tensor_scalar(xh2_g[:, t, :], x1_all[:, bass.ds(PER * (j - 4) + t, 1), :],
                                               mv2[:, t, 0:1], rstd2[:, t:t + 1], ALU.subtract, ALU.mult)
                    last.then_inc(s_xh2, 1)
                if on(k, 3):
                    v.wait_ge(s_inv, j - 2)
                    if k > 3:
                        v.wait_ge(s_outp, j - 3)
                    rs = rs_all[:, bass.ds(j - 3, 1), :].rearrange("p a s -> p (a s)").unsqueeze(2)
                    v.tensor_tensor(agg_g[:], bank[6][:, 0:GC].rearrange("p (s l) -> p s l", s=NSEQ),
                                    rs.to_broadcast([P, NSEQ, LEN]), ALU.mult).then_inc(s_agg, 1)
                if on(k, 1):
                    v.wait_ge(s_corr_ev, j)
                    v.nop(nofuse=True)
                    for q in range(NSEQ):
                        v.max(top[:, q, 0:8], corr_g[:, q, 0:LEN])
                    v.drain()
                    first = top[:, :, 0:1]
                    v.tensor_tensor(diff_g[:, :, 0:LEN], corr_g[:, :, 0:LEN], first.to_broadcast([P, NSEQ, LEN]),
                                    ALU.subtract)
                    v.tensor_tensor(diff_g[:, :, LEN:LEN + TOPK], top[:, :, 0:TOPK],
                                    first.to_broadcast([P, NSEQ, TOPK]), ALU.subtract).then_inc(s_maxed, 1)
                if on(k, 3):
                    v.wait_ge(s_outp, j - 2)
                    v.tensor_tensor(tiles(x1_all, j - 3), bank[6][:, GC:2 * GC].rearrange("p (t d) -> p t d", t=PER),
                                    tiles(x_all, j - 3), ALU.add).then_inc(s_x1, 1)
                    v.drain()
                    for t in range(PER):
                        v.bn_stats(st2[:, t, :], x1_all[:, bass.ds(PER * (j - 3) + t, 1), :])
                if on(k, 1):
                    for q in range(NSEQ):
                        v.match_replace(out=picked[:, q, :],
                                        in_to_replace=top[:, q, :].rearrange("p (a b) -> p a b", a=2)[:, :, 0:TOPK],
                                        in_values=corr_g[:, q, :], imm_value=CHOSEN)
                if 1 <= k <= LAST + 3:
                    v.drain()
                if on(k, 3):
                    for t in range(PER):
                        v.bn_aggr(mv2[:, t, :], st2[:, t, :])
                if on(k, 1):
                    v.wait_ge(s_exped, j)
                    v.tensor_reduce(ssum[:], exp_g[:, :, LEN:LEN + TOPK], AX, ALU.add)
                    if k > 1:
                        v.wait_ge(s_sT, j - 1)
                    v.scalar_tensor_tensor(out=s_g[:], in0=picked[:, :, 0:LEN], scalar=CHOSEN / 2,
                                           in1=exp_g[:, :, 0:LEN], op0=ALU.is_ge, op1=ALU.mult
                                           ).then_inc(s_chosen, 1)
                if 1 <= k <= LAST + 3:
                    v.drain()
                if on(k, 3):
                    v.tensor_scalar(ve2[:], mv2[:, :, 1], EPS, None, ALU.add).then_inc(s_var2, 1)
                if on(k, 1):
                    v.reciprocal(rs_all[:, bass.ds(j - 1, 1), :], ssum[:])
                if on(k, 0):
                    v.wait_ge(s_proj, j + 1)
                    v.wait_ge(s_q_ev, PER * (j + 1))
                    if k > 0:
                        v.wait_ge(s_corr, j)
                    for t in range(PER):
                        last = v.tensor_tensor(qk_g[:, t, :, :], q_g[:, t:t + 1, :].to_broadcast([P, 2, D]),
                                               bank[1 + t][:, D:3 * D].rearrange("p (h d) -> p h d", h=2), ALU.mult)
                    last.then_inc(s_qk, 1)
                if on(k, 2):
                    v.wait_ge(s_spec, j - 1)
                    if k > 2:
                        v.wait_ge(s_inv, j - 2)
                    v.tensor_tensor(sv_g[:], tiles(v_all, j - 2).unsqueeze(2).to_broadcast([P, PER, 2, D]),
                                    bank[5][:, :].rearrange("p (t h d) -> p t h d", t=PER, h=2), ALU.mult
                                    ).then_inc(s_sv, 1)

            sweep(v, step, 4)

            def whole(ap):
                return ap.unsqueeze(2).to_broadcast([P, TILES, EXPERTS])

            v.wait_ge(s_logit_ev, GROUPS)
            v.tensor_reduce(col[:, 0, :], lg_all[:], AX, ALU.max)
            v.drain()
            v.tensor_tensor(sc_a[:], lg_all[:], whole(col[:, 0, :]), ALU.subtract).then_inc(s_lg_exp, 1)
            v.wait_ge(s_lg_exp, 2)
            v.tensor_reduce(col[:, 1, :], sc_b[:], AX, ALU.add)
            v.drain()
            v.reciprocal(col[:, 2, :], col[:, 1, :])
            v.drain()
            v.tensor_tensor(sc_a[:], sc_b[:], whole(col[:, 2, :]), ALU.mult)
            v.drain()
            cur = sc_a
            for k in range(2):
                v.tensor_reduce(col[:, 3 + k, :], cur[:], AX, ALU.max)
                v.drain()
                v.tensor_tensor(sc_t[:], cur[:], whole(col[:, 3 + k, :]), ALU.is_equal)
                v.drain()
                v.tensor_tensor(sc_t[:], sc_t[:], prio.unsqueeze(1).to_broadcast([P, TILES, EXPERTS]), ALU.mult)
                v.drain()
                v.tensor_reduce(col[:, 5, :], sc_t[:], AX, ALU.max)
                v.drain()
                v.tensor_tensor(hot[:, :, k, :].rearrange("p e t -> p t e"), sc_t[:], whole(col[:, 5, :]),
                                ALU.is_equal)
                v.drain()
                if k == 0:
                    v.scalar_tensor_tensor(out=sc_b[:], in0=hot[:, :, 0, :].rearrange("p e t -> p t e"), scalar=-2.0,
                                           in1=sc_a[:], op0=ALU.mult, op1=ALU.add)
                    v.drain()
                    cur = sc_b
            v.tensor_copy(hot16[:], hot[:]).then_inc(s_onehot, 1)
            v.tensor_tensor(col[:, 6, :], col[:, 3, :], col[:, 4, :], ALU.add)
            v.drain()
            v.tensor_scalar(col[:, 6, :], col[:, 6, :], GATE_EPS, None, ALU.max)
            v.drain()
            v.reciprocal(col[:, 7, :], col[:, 6, :])
            v.drain()
            v.tensor_tensor(gate[:], col[:, 3:5, :], col[:, 7:8, :].to_broadcast([P, 2, TILES]), ALU.mult)
            v.wait_ge(s_counted, 1)
            flat = "p e k t -> p (e k t)"
            v.tensor_tensor_scan(run_s[:], segment, bank[7][:, 256:512], 0.0, ALU.mult, ALU.add)
            v.drain()
            v.tensor_tensor(run_s[:], run_s[:], bank[7][:, 256:512], ALU.subtract)
            v.drain()
            v.tensor_tensor(where[:].rearrange(flat), bank[7][:, 0:256], run_s[:], ALU.add)
            v.drain()
            for h, dst, add in ((0, pos, None), (1, base, slot0)):
                if h == 0:
                    v.tensor_tensor(prod[:], hot[:], where[:], ALU.mult)
                else:
                    v.tensor_tensor(prod[:].rearrange("p e k t -> p e (k t)"), hot[:].rearrange("p e k t -> p e (k t)"),
                                    slot0.unsqueeze(2).to_broadcast([P, EXPERTS, 2 * TILES]), ALU.mult)
                v.drain()
                v.tensor_reduce(dst[:], prod[:].rearrange("p e k t -> p k t e"), AX, ALU.add)
                v.drain()
            v.tensor_scalar(keep[:], pos[:], float(CAP), None, ALU.is_lt)
            v.drain()
            v.tensor_tensor(gate[:], gate[:], keep[:], ALU.mult)
            v.tensor_tensor(tmp2[:], pos[:], keep[:], ALU.mult)
            v.drain()
            v.tensor_tensor(from_slot[:], tmp2[:], base[:], ALU.add)
            v.drain()
            v.tensor_scalar(tmp2[:], keep[:], -float(SLOTS), float(SLOTS), ALU.mult, ALU.add)
            v.drain()
            v.tensor_tensor(tmp2[:], tmp2[:], base[:], ALU.add)
            v.drain()
            v.tensor_tensor(to_slot[:], tmp2[:], pos[:], ALU.add).then_inc(s_slots, 1)

            def copy_ctx(j, first=False):
                if not first:
                    v.wait_ge(s_ctxT, j)
                v.tensor_copy(ctx_g[:], tiles(ctx_all, j)).then_inc(s_ctx2, 1)

            copy_ctx(0, first=True)
            with v.Fori(1, GROUPS) as j:
                copy_ctx(j)

            v.wait_ge(s_ag, 16 * PICKS)
            v.tensor_scalar(a_sum[:], a_rows[:, 0, :], w_b[:, 0:1], None, ALU.mult)
            for i in range(1, PICKS):
                v.drain()
                last = v.scalar_tensor_tensor(out=a_sum[:], in0=a_rows[:, i, :], scalar=w_b[:, i:i + 1], in1=a_sum[:],
                                              op0=ALU.mult, op1=ALU.add)
            last.then_inc(s_asum, 1)

            v.wait_ge(s_mask_in, 32)
            for b in range(2):
                rows, mine, other = slice(b * LEN, (b + 1) * LEN), slice(b * LEN, (b + 1) * LEN),                     slice((1 - b) * LEN, (2 - b) * LEN)
                v.tensor_scalar(live[rows, :, mine], mask_i[rows], 0.0, None, ALU.not_equal)
                v.memset(live[rows, :, other], 0.0)
                v.memset(penalty[rows, :, other], FOREIGN)
            v.drain()
            for b in range(2):
                rows, mine = slice(b * LEN, (b + 1) * LEN), slice(b * LEN, (b + 1) * LEN)
                last = v.tensor_scalar(penalty[rows, :, mine], live[rows, :, mine], -MASKED, MASKED, ALU.mult, ALU.add)
            v.drain()

            v.wait_ge(s_b2_in, 16)

            def expert_out(e, first=False):
                v.wait_ge(s_f2, e + 1)
                if not first:
                    v.wait_ge(s_y_out, 16 * e)
                v.tensor_tensor(y_g[:], bank[6][:, :].rearrange("p (s d) -> p s d", s=SC),
                                b2_b[:, bass.ds(e, 1), :].to_broadcast([P, SC, D]), ALU.add).then_inc(s_y, 1)

            expert_out(0, first=True)
            with v.Fori(1, EXPERTS) as e:
                expert_out(e)

            v.wait_ge(s_vec_in, 48)

            def row(t3, t):
                return t3[:, bass.ds(t, 1), :].rearrange("p a d -> p (a d)")

            def step(j, k):
                if on(k, 3):
                    for t in range(PER):
                        v.scalar_tensor_tensor(out=t_g[:, t, :], in0=o_g[:, t, :], scalar=mv3[:, 1, t, 0:1],
                                               in1=g0_b[:], op0=ALU.subtract, op1=ALU.mult)
                if on(k, 0):
                    v.wait_ge(g_in[k % 2], 32 * (j - k % 2) + 64)
                    for t in range(PER):
                        v.scalar_tensor_tensor(out=row(x1_all, PER * j + t),
                                               in0=y_all[:, bass.ds(PER * j + t, 1), 0, :].rearrange("p a d -> p (a d)"),
                                               scalar=gate[:, 0, bass.ds(PER * j + t, 1)], in1=row(x1_all, PER * j + t),
                                               op0=ALU.mult, op1=ALU.add)
                if on(k, 2):
                    v.wait_ge(s_p_ok, j - 1)
                    v.reciprocal(prec[:], psums[:])
                v.drain()
                if on(k, 3):
                    v.wait_ge(s_x2b, j - 2)
                    for t in range(PER):
                        v.scalar_tensor_tensor(out=row(x_all, PER * (j - 3) + t), in0=t_g[:, t, :],
                                               scalar=rstd3[:, 1, t:t + 1], in1=row(x_all, PER * (j - 3) + t),
                                               op0=ALU.mult, op1=ALU.add)
                if on(k, 0):
                    for t in range(PER):
                        last = v.scalar_tensor_tensor(
                            out=row(x1_all, PER * j + t),
                            in0=y_all[:, bass.ds(PER * j + t, 1), 1, :].rearrange("p a d -> p (a d)"),
                            scalar=gate[:, 1, bass.ds(PER * j + t, 1)], in1=row(x1_all, PER * j + t),
                            op0=ALU.mult, op1=ALU.add)
                    last.then_inc(s_x2, 1)
                if on(k, 2):
                    v.wait_ge(s_pv, j - 1)
                    for t in range(PER):
                        last = v.scalar_tensor_tensor(out=o_g[:, t, :], in0=bank[4][:, t * D:(t + 1) * D],
                                                      scalar=prec[:, t:t + 1], in1=bo1_b[:], op0=ALU.mult, op1=ALU.add)
                    last.then_inc(s_o, 1)
                if k < GROUPS + 3:
                    v.drain()
                    for n, lag in ((0, 0), (1, 2), (2, 3)):
                        for t in range(PER):
                            if on(k, lag):
                                v.bn_stats(st3[:, n, t, :], o_g[:, t, :] if n == 1 else
                                           row(x_all if n else x1_all, PER * (j - lag) + t))
                    v.drain()
                    for n, lag in ((0, 0), (1, 2), (2, 3)):
                        for t in range(PER):
                            if on(k, lag):
                                v.bn_aggr(mv3[:, n, t, :], st3[:, n, t, :])
                    v.drain()
                    v.tensor_scalar(ve3[:], mv3[:, :, :, 1].rearrange("p n t -> p (n t)"), EPS, None, ALU.add
                                    ).then_inc(s_var3, 1)
                if on(k, 4):
                    v.wait_ge(s_ad, j - 3)
                    if k > 4:
                        v.wait_ge(s_out_done, 16 * (j - 4))
                    v.tensor_tensor(fin_g[:], bank[3][:, 0:GC].rearrange("p (t d) -> p t d", t=PER),
                                    tiles(x_all, j - 4), ALU.add).then_inc(s_fin, 1)
                if on(k, 1):
                    v.wait_ge(s_scr, j)
                    v.scalar_tensor_tensor(out=sc_g[:], in0=bank[7][:, 0:GC].rearrange("p (t k) -> p t k", t=PER),
                                           scalar=SCALE, in1=tiles(live, j - 1), op0=ALU.mult, op1=ALU.mult)
                    v.drain()
                    v.tensor_tensor(sc_g[:], sc_g[:], tiles(penalty, j - 1), ALU.add)
                if k < GROUPS + 3:
                    v.wait_ge(s_rstd3_ok, j + 1)
                    v.scalar_tensor_tensor(out=nmr3[:], in0=mv3[:, :, :, 0], scalar=-1.0, in1=rstd3[:],
                                           op0=ALU.mult, op1=ALU.mult).then_inc(s_nmr3, 1)
                if on(k, 1):
                    v.drain()
                    v.tensor_reduce(nmax[:], sc_g[:], AX, ALU.max)
                    v.drain()
                    v.tensor_scalar(nmax[:], nmax[:], -1.0, None, ALU.mult).then_inc(s_scr_max, 1)

            for j in range(GROUPS + 4):
                step(j, j)


_INS = ["x", "ctx_1024", "mask_Bx1xS2_ik1", "L0_xattn_Wq", "L0_xattn_bq", "L0_xattn_Wk", "L0_xattn_bk",
        "L0_xattn_Wv", "L0_xattn_bv", "L0_xattn_Wo", "L0_xattn_bo", "L0_ffn_wg", "L0_ffn_w1", "L0_ffn_b1",
        "L0_ffn_w2", "L0_ffn_b2", "L1_xattn_Wq", "L1_xattn_bq", "L1_xattn_Wk", "L1_xattn_bk", "L1_xattn_Wv",
        "L1_xattn_bv", "L1_xattn_Wo", "L1_xattn_bo", "L1_xattn_g0", "L1_xattn_beta0", "L1_ffn_W", "L1_ffn_b",
        "L1_ffn_ids", "L1_ffn_weights"]


def kernel(**inputs):
    import concourse.bacc as _bacc
    from concourse.bass_utils import run_bass_kernel_spmd as _run

    nc = _bacc.Bacc("TRN2", target_bir_lowering=False, num_devices=1)
    arrays, args = {}, []
    data = [(name, inputs[name]) for name in _INS] + [("constants", constants())]
    for name, a in data:
        a = np.ascontiguousarray(a)
        arrays[f"in_{name}"] = a
        args.append(nc.dram_tensor(f"in_{name}", a.shape, mybir.dt.from_np(a.dtype), kind="ExternalInput").ap())
    args.append(nc.dram_tensor("out_0", (SEQS, LEN, D), F32, kind="ExternalOutput").ap())
    build(nc, *args)
    r = _run(nc, [arrays], core_ids=[0])
    return r.results[0]["out_0"]
```

```python
from contextlib import ExitStack

import numpy as np
import concourse.bass as bass
from concourse import mybir

F32 = mybir.dt.float32
BF16 = mybir.dt.bfloat16
I32 = mybir.dt.int32
ALU = mybir.AluOpType
ACT = mybir.ActivationFunctionType
AX = mybir.AxisListType.X

P = 128
SEQS, LEN, D = 32, 64, 128
TOKENS = SEQS * LEN
TILES = TOKENS // P
PER = 2
GROUPS = TILES // PER
GC = PER * P
NSEQ = PER * P // LEN
TOPK = int(np.log(LEN))
PAD = 68
EXPERTS, HID = 8, 512
HC = HID // P
CAP = -(-2 * TOKENS // EXPERTS)
SLOTS = EXPERTS * CAP
SC = CAP // P
CHUNKS = EXPERTS * SC
MARKS = 7
POOL_FROM = 3 * MARKS
POOL_HALF = 28
WARM_UP = 13
AHEAD = 5
ADAPTERS, PICKS = 32, 8
EPS = 1e-5
GATE_EPS = 1e-9
SCALE = float(1.0 / np.sqrt(np.float32(D)))
SENTINEL = -3e38
CHOSEN = 3e38
MASKED = -1e9
FOREIGN = -1e30


def dft_constants():
    t = np.arange(LEN)
    fwd = np.zeros((P, 2, 2, 32))
    c1 = np.zeros((2, 2, 32, 2, LEN))
    c2 = np.zeros((2, 2, 32, 2, LEN))
    for b in range(2):
        rows = slice(b * LEN, (b + 1) * LEN)
        for k in range(32):
            cos, sin = np.cos(2 * np.pi * k * t / LEN), np.sin(2 * np.pi * k * t / LEN)
            last = np.cos(np.pi * t)
            fwd[rows, 0, b, k] = cos
            fwd[rows, 1, b, k] = sin if k else last
            w = (2.0 if k else 1.0) / LEN
            c1[0, b, k, b] = w * cos
            c1[1, b, k, b] = w * (cos if k else last)
            if k:
                c2[0, b, k, b] = w * sin
                c2[1, b, k, b] = -w * sin
    return fwd.reshape(P, P), c1.reshape(P, P), c2.reshape(P, P)


def constants():
    fwd, c1, c2 = dft_constants()
    before = np.triu(np.ones((P, P)), 1)
    count = np.broadcast_to(np.arange(P), (P, P))
    small = np.zeros((P, P))
    small[:, 8:16] = 8 - np.arange(8)[None, :]
    small[:, 16] = np.arange(P)
    small[:, 32:48] = -0.5
    small[:, 17] = 1 + np.arange(P)
    small[:, 48:64] = np.arange(TILES)[None, :]
    seg = np.ones((P, EXPERTS, 2 * TILES))
    seg[:, :, 0] = 0.0
    return np.concatenate([np.eye(P), fwd, c1, c2, before, count, small, seg.reshape(P, -1)],
                          axis=1).astype(np.float32)


def build(nc, x, ctx, mask, Wq0, bq0, Wk0, bk0, Wv0, bv0, Wo0, bo0, wg, w1, b1, w2, b2,
          Wq1, bq1, Wk1, bk1, Wv1, bv1, Wo1, bo1, g0, beta0, WA, bA, ids, weights, consts, out):
    es = ExitStack()
    with es:
        def sb(name, shape, dt=F32):
            return es.enter_context(nc.sbuf_tensor(name, shape, dt))

        def pb(name):
            return es.enter_context(nc.psum_tensor(name, [P, 512], F32))

        def sem(name):
            return es.enter_context(nc.semaphore(name))

        xbuf = nc.dram_tensor("expert_rows_in", [1 + TOKENS, D], F32, kind="Internal").ap()
        ybuf = nc.dram_tensor("expert_rows_out", [SLOTS, D], F32, kind="Internal").ap()

        cst = sb("cst", [P, 7 * P + EXPERTS * 2 * TILES])
        ident = cst[:, 0:128]
        fwd = cst[:, 128:256]
        c1 = cst[:, 256:384]
        c2 = cst[:, 384:512]
        before = cst[:, 512:640]
        count = cst[:, 640:768]
        small = cst[:, 768:896]
        prio = small[:, 8:16]
        lane = small[:, 16:17]
        neghalf = small[:, 32:48]
        lane1 = small[:, 17:18]
        tile_no = small[:, 48:64]
        segment = cst[:, 896:896 + 2 * TILES * EXPERTS]

        x_all = sb("x_all", [P, TILES, D])
        ctx_all = sb("ctx_all", [P, TILES, D])
        x1_all = sb("x1_all", [P, TILES, D])
        y_all = sb("y_all", [P, TILES, 2, D])
        v_all = y_all
        live = y_all[:, :, 0, :]
        wv0k0 = sb("wv0k0", [P, 2 * D])
        wq0 = sb("wq0", [P, D])
        wo0 = sb("wo0", [P, D])
        wg_s = sb("wg_s", [P, EXPERTS])
        biasf = sb("biasf", [P, 6 * D])
        bhi = sb("bhi", [P, 6 * D], BF16)
        bmid = sb("bmid", [P, 6 * D], BF16)
        bres = sb("bres", [P, 6 * D])
        bias3 = sb("bias3", [P, 6 * D], BF16)
        at_dc = sb("at_dc", [P, P], BF16)
        at_all = sb("at_all", [P, P], BF16)
        before16 = sb("before16", [P, P], BF16)
        ones16 = sb("ones16", [P, P], BF16)

        st1 = sb("st1", [P, TILES, 6])
        mv1 = sb("mv1", [P, TILES, 2])
        ve1 = sb("ve1", [P, TILES])
        rstd1 = sb("rstd1", [P, TILES])
        nmr1 = sb("nmr1", [P, TILES])
        st2 = sb("st2", [P, 2, 6])
        mv2 = sb("mv2", [P, PER, 2])
        ve2 = sb("ve2", [P, PER])
        rstd2 = sb("rstd2", [P, PER])
        xh_g = sb("xh_g", [P, PER, D])
        ctx_g = sb("ctx_g", [P, PER, D])
        xcf_g = sb("xcf_g", [P, 2, PER, P])
        q_g = sb("q_g", [P, PER, 2, D])
        qk_g = sb("qk_g", [P, PER, 2, D])
        corr_g = sb("corr_g", [P, NSEQ, PAD])
        top = sb("top", [P, NSEQ, 16])
        picked = sb("picked", [P, NSEQ, PAD])
        diff_g = sb("diff_g", [P, NSEQ, LEN + 4])
        exp_g = sb("exp_g", [P, NSEQ, LEN + 4])
        ssum = sb("ssum", [P, NSEQ])
        rs_all = sb("rs_all", [P, GROUPS, NSEQ])
        s_g = sb("s_g", [P, NSEQ, LEN])
        sT_g = sb("sT_g", [P, GC])
        sv_g = sb("sv_g", [P, PER, 2, D])
        agg_g = sb("agg_g", [P, NSEQ, LEN])
        xh2_g = sb("xh2_g", [P, PER, D])
        xT2_g = sb("xT2_g", [P, GC])
        lg_all = sb("lg_all", [P, TILES, EXPERTS])

        sc_a = sb("sc_a", [P, TILES, EXPERTS])
        sc_b = sb("sc_b", [P, TILES, EXPERTS])
        sc_t = sb("sc_t", [P, TILES, EXPERTS])
        hot = sb("hot", [P, EXPERTS, 2, TILES], BF16)
        col = sb("col", [P, 8, TILES])
        run_s = sb("run_s", [P, EXPERTS * 2 * TILES])
        where = sb("where", [P, EXPERTS, 2, TILES])
        prod = sb("prod", [P, EXPERTS, 2, TILES])
        first = sb("first", [P, 2, TILES])
        pos = sb("pos", [P, 2, TILES])
        base = sb("base", [P, 2, TILES])
        keep = sb("keep", [P, 2, TILES])
        tmp2 = sb("tmp2", [P, 2, TILES])
        from_slot = sb("from_slot", [P, 2, TILES], I32)
        gate = sb("gate", [P, 2, TILES])
        chunk = sb("chunk", [P, 2, TILES])
        chunk_of = sb("chunk_of", [P, 2, TILES])
        place = sb("place", [P, 2, TILES])
        count16 = sb("count16", [P, P], BF16)
        hot_chunk = sb("hot_chunk", [P, 2 * TILES, CHUNKS], BF16)
        hot_id = sb("hot_id", [P, 2 * TILES, 2, CHUNKS], BF16)
        ids_f = sb("ids_f", [P, CHUNKS])
        row_of = sb("row_of", [P, CHUNKS], I32)
        zeros = sb("zeros", [1, D])

        w1_all = sb("w1_all", [P, EXPERTS, HID])
        w2_all = sb("w2_all", [P, EXPERTS, HC, D])
        rows35 = sb("rows35", [35, P])
        cols35 = sb("cols35", [P, 35])
        b2_b = sb("b2_b", [P, EXPERTS, D])
        w1_g = sb("w1_g", [P, HID])
        xr_g = sb("xr_g", [P, 2, SC, D])
        xrT_g = sb("xrT_g", [P, CAP])
        h_g = sb("h_g", [P, HC, CAP])
        hot_place = h_g[:].rearrange("p c s -> p (c s)").bitcast(BF16).rearrange("p (i q) -> p i q", q=P)
        y_g = sb("y_g", [P, SC, D])

        wq1 = sb("wq1", [P, D])
        wk1 = sb("wk1", [P, D])
        wv1 = sb("wv1", [P, D])
        wo1 = sb("wo1", [P, D])
        vT_g = sb("vT_g", [P, 2, GC])
        kT_all = sb("kT_all", [P, TILES, P])
        vw_all = sb("vw_all", [P, TILES, D])
        g0_b = sb("g0_b", [P, D])
        mask_i = sb("mask_i", [P, TILES * 2 * LEN], I32)
        penalty = sb("penalty", [P, TILES, P])
        ids_b = sb("ids_b", [P, PICKS], I32)
        w_b = sb("w_b", [P, PICKS])
        ids_c = sb("ids_c", [PICKS, 1], I32)
        w_c = sb("w_c", [PICKS, 1])
        w_rep = sb("w_rep", [P, P])
        b_sel = sb("b_sel", [P, D])
        a_idx = sb("a_idx", [P, PICKS], I32)
        a_rows = sb("a_rows", [P, PICKS, D])
        a_sum = sb("a_sum", [P, D])
        a_mat = sb("a_mat", [P, D])
        xh3_g = sb("xh3_g", [P, PER, D])
        xT3_g = sb("xT3_g", [P, GC])
        qT_g = sb("qT_g", [P, GC])
        sc_g = sb("sc_g", [P, PER, P])
        nmax = sb("nmax", [P, PER])
        p_g = sb("p_g", [P, PER, P])
        psums = sb("psums", [P, PER])
        pT_g = sb("pT_g", [P, GC])
        t_g = sb("t_g", [P, PER, D])
        st3 = sb("st3", [P, 3, PER, 6])
        mv3 = sb("mv3", [P, 3, PER, 2])
        eps3 = sb("eps3", [P, 3, PER])
        ve3 = sb("ve3", [P, 3 * PER])
        rstd3 = sb("rstd3", [P, 3, PER])
        nmr3 = sb("nmr3", [P, 3, PER])
        xh4_g = sb("xh4_g", [P, PER, D])
        xT4_g = sb("xT4_g", [P, GC])
        fin_g = sb("fin_g", [P, PER, D])
        warm = sb("warm", [P, 2])

        bank = [pb(f"bank{i}") for i in range(8)]

        s_c_in = sem("s_c_in")
        s_x_in0 = sem("s_x_in0")
        s_x_in1 = sem("s_x_in1")
        s_x_in2 = sem("s_x_in2")
        s_ctx_in0 = sem("s_ctx_in0")
        s_ctx_in1 = sem("s_ctx_in1")
        s_w0_in = sem("s_w0_in")
        s_wg_in = sem("s_wg_in")
        s_b0_in = sem("s_b0_in")
        s_b1_in = sem("s_b1_in")
        s_w1_in = sem("s_w1_in")
        s_w2_in = sem("s_w2_in")
        s_rows_in = sem("s_rows_in")
        s_b2_in = sem("s_b2_in")
        s_l1w_in = sem("s_l1w_in")
        s_vec_in = sem("s_vec_in")
        s_mask_in = sem("s_mask_in")
        s_masked = sem("s_masked")
        s_ad_in = sem("s_ad_in")
        s_zf_out = sem("s_zf_out")
        s_warm = sem("s_warm")
        s_xh2_out = sem("s_xh2_out")
        s_marked = sem("s_marked")
        s_marked_pool = sem("s_marked_pool")
        s_place = sem("s_place")
        s_table = sem("s_table")
        s_row_of = sem("s_row_of")
        s_pset = sem("s_pset")
        s_bset = sem("s_bset")
        s_ctx_copied = sem("s_ctx_copied")
        s_var1 = sem("s_var1")
        s_rstd1 = sem("s_rstd1")
        s_nmr1 = sem("s_nmr1")
        s_xh = sem("s_xh")
        s_dft = sem("s_dft")
        s_dft_ev = sem("s_dft_ev")
        s_proj = sem("s_proj")
        s_qv = sem("s_qv")
        s_q_ev = sem("s_q_ev")
        s_v_ev = sem("s_v_ev")
        s_qk = sem("s_qk")
        s_corr = sem("s_corr")
        s_corr_ev = sem("s_corr_ev")
        s_maxed = sem("s_maxed")
        s_exped = sem("s_exped")
        s_chosen = sem("s_chosen")
        s_sT = sem("s_sT")
        s_sT_ev = sem("s_sT_ev")
        s_spec = sem("s_spec")
        s_sv = sem("s_sv")
        s_inv = sem("s_inv")
        s_agg = sem("s_agg")
        s_outp = sem("s_outp")
        s_x1 = sem("s_x1")
        s_var2 = sem("s_var2")
        s_rstd2_ok = sem("s_rstd2_ok")
        s_xh2 = sem("s_xh2")
        s_xT2 = sem("s_xT2")
        s_xT2_ev = sem("s_xT2_ev")
        s_logit = sem("s_logit")
        s_logit_ev = sem("s_logit_ev")
        s_lg_exp = sem("s_lg_exp")
        s_onehot = sem("s_onehot")
        s_counted = sem("s_counted")
        s_ctxT = sem("s_ctxT")
        s_ctxT_ev = sem("s_ctxT_ev")
        s_kp = sem("s_kp")
        s_kp_ev = sem("s_kp_ev")
        s_vw = sem("s_vw")
        s_vw_ev = sem("s_vw_ev")
        s_cT = sem("s_cT")
        s_cT_ev = sem("s_cT_ev")
        s_aidx = sem("s_aidx")
        s_ag = sem("s_ag")
        s_abg = sem("s_abg")
        s_asum = sem("s_asum")
        s_aT = sem("s_aT")
        s_aT_ev = sem("s_aT_ev")
        s_wrep = sem("s_wrep")
        s_xrT = sem("s_xrT")
        s_xrT_ev = sem("s_xrT_ev")
        s_w1c = sem("s_w1c")
        s_f1 = sem("s_f1")
        s_gelu = sem("s_gelu")
        s_f2 = sem("s_f2")
        s_y = sem("s_y")
        s_y_out = sem("s_y_out")
        s_var3 = sem("s_var3")
        s_nmr3 = sem("s_nmr3")
        s_rstd3_ok = sem("s_rstd3_ok")
        s_xh3 = sem("s_xh3")
        s_xT3 = sem("s_xT3")
        s_xT3_ev = sem("s_xT3_ev")
        s_qp = sem("s_qp")
        s_qp_ev = sem("s_qp_ev")
        s_scr = sem("s_scr")
        s_scr_read = sem("s_scr_read")
        s_scr_max = sem("s_scr_max")
        s_centred = sem("s_centred")
        s_offset = sem("s_offset")
        s_x3 = sem("s_x3")
        s_p_ok = sem("s_p_ok")
        s_pT = sem("s_pT")
        s_pT_ev = sem("s_pT_ev")
        s_pv = sem("s_pv")
        s_xh4 = sem("s_xh4")
        s_xT4 = sem("s_xT4")
        s_xT4_ev = sem("s_xT4_ev")
        s_ad = sem("s_ad")
        s_fin = sem("s_fin")
        s_out_done = sem("s_out_done")
        s_xr_in = [sem(f"s_xr_in{i}") for i in range(2)]
        g_in = [sem(f"s_gather{i}") for i in range(AHEAD + 1)]

        def tiles(t, g):
            return t[:, bass.ds(PER * g, PER), :]

        def tokens_of(ap):
            return ap.rearrange("(t b) l d -> (b l) t d", b=2)

        block = es.enter_context(nc.Block())

        LAST = GROUPS - 1
        PARTS = (slice(0, 4), slice(4, 8), slice(8, 16))

        def sweep(eng, step, lag, last=GROUPS):
            for j in range(lag + 1):
                step(j, j)
            with eng.Fori(lag + 1, last) as j:
                step(j, lag + 1)
            for j in range(last, GROUPS + lag):
                step(j, j)

        def on(k, lag):
            return lag <= k <= LAST + lag

        def last_steps(k):
            return k >= GROUPS

        @block.sync
        def _(sp):
            xv, cv = tokens_of(x), tokens_of(ctx)
            sp.dma_start(x_all[:, 0:4], xv[:, 0:4]).then_inc(s_x_in0, 16)
            sp.dma_start(cst[:], consts).then_inc(s_c_in, 16)
            sp.dma_start(ctx_all[:, 0:4], cv[:, 0:4]).then_inc(s_ctx_in0, 16)
            for w, dst in ((Wv0, wv0k0[:, 0:D]), (Wk0, wv0k0[:, D:2 * D]), (Wq0, wq0[:]), (Wo0, wo0[:])):
                sp.dma_start(dst, w).then_inc(s_w0_in, 16)
            sp.dma_start(x_all[:, 4:8], xv[:, 4:8]).then_inc(s_x_in1, 16)
            sp.dma_start(x_all[:, 8:16], xv[:, 8:16]).then_inc(s_x_in2, 16)
            sp.dma_start(ctx_all[:, 4:16], cv[:, 4:16]).then_inc(s_ctx_in1, 16)
            sp.dma_start(ids_b[:], ids.partition_broadcast(P)).then_inc(s_ad_in, 16)
            sp.dma_start(w_b[:], weights.partition_broadcast(P)).then_inc(s_ad_in, 16)
            sp.dma_start(ids_c[:], ids.unsqueeze(1)).then_inc(s_ad_in, 16)
            sp.dma_start(w_c[:], weights.unsqueeze(1)).then_inc(s_ad_in, 16)
            sp.dma_start(wg_s[:], wg).then_inc(s_wg_in, 16)
            sp.dma_start(rows35[0:32, :], b1.rearrange("e (c h) -> (e c) h", c=HC)).then_inc(s_rows_in, 16)
            for i, b in enumerate((bq1, bk1, bv1)):
                sp.dma_start(rows35[32 + i:33 + i, :], b.unsqueeze(0)).then_inc(s_rows_in, 16)
            for w, dst in ((Wq1, wq1), (Wk1, wk1), (Wv1, wv1), (Wo1, wo1)):
                sp.dma_start(dst[:], w).then_inc(s_l1w_in, 16)
            sp.dma_start(w1_all[:], w1.rearrange("e d h -> d e h")).then_inc(s_w1_in, 16)
            sp.wait_ge(s_pset, 7)
            sp.dma_start(xbuf[0:1, :], zeros[:]).then_inc(s_zf_out, 16)
            sp.dma_start(w2_all[:], w2.rearrange("e (c h) d -> h e c d", c=HC)).then_inc(s_w2_in, 16)
            sp.dma_start(b2_b[:].rearrange("p e d -> p (e d)"),
                         b2.rearrange("e d -> (e d)").partition_broadcast(P)).then_inc(s_b2_in, 16)
            sp.dma_start(g0_b[:], g0.partition_broadcast(P)).then_inc(s_vec_in, 16)
            sp.dma_start(mask_i[:], mask.rearrange("s a l -> (s a l)").partition_broadcast(P)).then_inc(s_mask_in, 16)

            rows = xbuf[1:1 + TOKENS, :].rearrange("(t p) d -> p t d", p=P)
            with sp.Fori(0, GROUPS) as j:
                sp.wait_ge(s_xh2, j + 1)
                sp.dma_start(tiles(rows, j), xh2_g[:]).then_inc(s_xh2_out, 16)

            with sp.Fori(0, EXPERTS) as e:
                sp.wait_ge(s_y, e + 1)
                sp.dma_start(ybuf[bass.ds(e * CAP, CAP), :].rearrange("(c p) d -> p c d", c=SC), y_g[:]
                             ).then_inc(s_y_out, 16)
            ov = tokens_of(out)
            with sp.Fori(0, GROUPS) as g:
                sp.wait_ge(s_fin, g + 1)
                sp.dma_start(tiles(ov, g), fin_g[:]).then_inc(s_out_done, 16)
            sp.wait_ge(s_out_done, 16 * GROUPS)
            sp.wait_ge(s_zf_out, 16)
            sp.wait_ge(s_xh2_out, 16 * GROUPS)
            sp.wait_ge(s_y_out, 16 * EXPERTS)

        @block.gpsimd
        def _(pool):
            pool.memset(biasf[:], 0.0).then_inc(s_pset, 1)
            pool.memset(ones16[:], 1.0).then_inc(s_pset, 1)
            pool.memset(bias3[:], 0.0).then_inc(s_pset, 1)
            pool.wait_ge(s_pset, 1)
            for i, b in ((3, bo0), (4, bo1), (5, beta0)):
                pool.dma_start(biasf[0:65:32, i * D:(i + 1) * D], b.partition_broadcast(3)).then_inc(s_b1_in, 16)
            pool.memset(b_sel[:], 0.0).then_inc(s_pset, 1)
            pool.memset(top[:], SENTINEL).then_inc(s_pset, 1)
            pool.memset(corr_g[:], SENTINEL).then_inc(s_pset, 1)
            pool.memset(zeros[:], 0.0).then_inc(s_pset, 1)
            pool.wait_ge(s_c_in, 16)

            def copy_ctx(j):
                if isinstance(j, int) and j in (0, 2):
                    pool.wait_ge(s_ctx_in0 if j == 0 else s_ctx_in1, 16)
                pool.tensor_copy(ctx_g[:], tiles(ctx_all, j)).then_inc(s_ctx_copied, 1)

            def deviation(part):
                cols = PARTS[part]
                pool.wait_ge(s_var1, part + 1)
                pool.tensor_tensor(rstd1[:, cols], ve1[:, cols], neghalf[:, cols], ALU.pow).then_inc(s_rstd1, 1)

            deviation(0)
            copy_ctx(0)
            deviation(1)

            def step(j, k):
                if k < LAST:
                    pool.wait_ge(s_dft, j + 1)
                    copy_ctx(j + 1)
                if k == 1:
                    deviation(2)
                if on(k, 3):
                    pool.wait_ge(s_var2, j - 2)
                    pool.tensor_tensor(rstd2[:], ve2[:], neghalf[:, 0:PER], ALU.pow).then_inc(s_rstd2_ok, 1)
                if isinstance(k, int) and k < 3:
                    if k == 0:
                        pool.wait_ge(s_ad_in, 64)
                        pool.wait_ge(s_aidx, 1)
                        pool.indirect_dma_start(out=b_sel[0:PICKS, :], out_offset=None, in_=bA,
                                                in_offset=bass.IndirectOffsetOnAxis(ap=ids_c[:], axis=0)
                                                ).then_inc(s_abg, 16)
                    for i in range(3 * k, min(3 * k + 3, PICKS)):
                        pool.indirect_dma_start(out=a_rows[:, i, :], out_offset=None,
                                                in_=WA.rearrange("a o d -> (a o) d"),
                                                in_offset=bass.IndirectOffsetOnAxis(ap=a_idx[:, i:i + 1], axis=0)
                                                ).then_inc(s_ag, 16)

            sweep(pool, step, 3, LAST)

            pool.wait_ge(s_place, 1)
            for i in range(POOL_FROM, 2 * TILES):
                last = pool.tensor_scalar(hot_place[:, i, :], count16[:], place[:, i // TILES, i % TILES:i % TILES + 1],
                                          None, ALU.is_equal)
                if i in (POOL_HALF - 1, 2 * TILES - 1):
                    last.then_inc(s_marked_pool, 1)
            pool.wait_ge(s_row_of, 1)
            pool.wait_ge(s_zf_out, 16)
            pool.wait_ge(s_xh2_out, 16 * GROUPS)
            for e in range(EXPERTS):
                if e > 1:
                    pool.wait_ge(s_xrT, e - 1)
                for c in range(SC):
                    pool.indirect_dma_start(out=xr_g[:, e % 2, c, :], out_offset=None, in_=xbuf,
                                            in_offset=bass.IndirectOffsetOnAxis(
                                                ap=row_of[:, e * SC + c:e * SC + c + 1], axis=0)
                                            ).then_inc(s_xr_in[e % 2], 16)

            pool.wait_ge(s_vec_in, 16)
            pool.wait_ge(s_y_out, 16 * EXPERTS)

            def gather(t):
                for k in range(2):
                    pool.indirect_dma_start(out=y_all[:, t, k, :], out_offset=None, in_=ybuf,
                                            in_offset=bass.IndirectOffsetOnAxis(
                                                ap=from_slot[:, k, t:t + 1], axis=0)
                                            ).then_inc(g_in[t % len(g_in)], 16)

            def step(j, k):
                if k < GROUPS + 4:
                    pool.wait_ge(s_var3, j + 1)
                    if k > 0:
                        pool.wait_ge(s_xh3, min(j, GROUPS))
                    if k > 4:
                        pool.wait_ge(s_xh4, j - 4)
                    cols = slice(0 if k < GROUPS else PER if k < GROUPS + 3 else 2 * PER,
                                 3 * PER if k > 3 else 2 * PER if k == 3 else PER)
                    pool.tensor_tensor(rstd3[:].rearrange("p n t -> p (n t)")[:, cols], ve3[:, cols],
                                       neghalf[:, cols], ALU.pow).then_inc(s_rstd3_ok, 1)
                for t in range(PER * k + AHEAD, min(PER * k + AHEAD + PER, TILES)):
                    gather(t)

            for t in range(AHEAD):
                gather(t)
            for j in range(GROUPS + 4):
                step(j, j)

        @block.scalar
        def _(act):
            act.wait_ge(s_warm, 1)
            act.activation(warm[:, 0:1], warm[:, 1:2], ACT.Exp)
            act.wait_ge(s_pset, 1)
            for i, b in ((0, bv0), (1, bk0), (2, bq0)):
                act.dma_start(biasf[0:65:32, i * D:(i + 1) * D], b.partition_broadcast(3)).then_inc(s_b0_in, 16)
            act.wait_ge(s_pset, 7)

            def normalise(j):
                for t in range(PER):
                    last = act.activation(xh_g[:, t, :], x_all[:, bass.ds(PER * j + t, 1), :].rearrange("p a d -> p (a d)"),
                                          ACT.Identity, bias=nmr1[:, bass.ds(PER * j + t, 1)],
                                          scale=rstd1[:, bass.ds(PER * j + t, 1)])
                last.then_inc(s_xh, 1)

            act.wait_ge(s_nmr1, 1)
            normalise(0)

            def step(j, k):
                if on(k, 2):
                    act.wait_ge(s_sT, j - 1)
                    if k > 2:
                        act.wait_ge(s_spec, j - 2)
                    act.activation(sT_g[:], bank[4][:, 0:GC], ACT.Copy).then_inc(s_sT_ev, 1)
                if on(k, 0):
                    act.wait_ge(s_dft, j + 1)
                    if k > 0:
                        act.wait_ge(s_proj, j)
                    act.activation(xcf_g[:].rearrange("p n t f -> p (n t f)"), bank[0][:, :], ACT.Copy
                                   ).then_inc(s_dft_ev, 1)
                if on(k, 1):
                    act.wait_ge(s_corr, j)
                    if k > 1:
                        act.wait_ge(s_chosen, j - 1)
                    act.activation(corr_g[:, :, 0:LEN], bank[3][:, 0:GC].rearrange("p (s l) -> p s l", s=NSEQ),
                                   ACT.Copy).then_inc(s_corr_ev, 1)
                if k < LAST:
                    if k in (1, 3):
                        act.wait_ge(s_nmr1, 2 if k == 1 else 3)
                    normalise(j + 1)
                if on(k, 1):
                    act.wait_ge(s_maxed, j)
                    act.activation(exp_g[:], diff_g[:], ACT.Exp).then_inc(s_exped, 1)
                if on(k, 0):
                    act.wait_ge(s_ctxT, j + 1)
                    act.activation(tiles(kT_all, j), bank[4][:, GC:2 * GC].rearrange("p (t k) -> p t k", t=PER),
                                   ACT.Copy).then_inc(s_ctxT_ev, 1)
                if on(k, 4):
                    act.wait_ge(s_xT2, j - 3)
                    if k > 4:
                        act.wait_ge(s_logit, j - 4)
                    act.activation(xT2_g[:], bank[7][:, 0:GC], ACT.Copy).then_inc(s_xT2_ev, 1)
                if on(k, 0):
                    act.wait_ge(s_qv, j + 1)
                    if k > 0:
                        act.wait_ge(s_qk, j)
                    lo, hi = slice(0, P // 2), slice(P // 2, P)
                    q, v = bank[2][:, 0:GC], bank[2][:, GC:2 * GC]
                    act.activation(q_g[:, :, 0, :], q.rearrange("p (t d) -> p t d", t=PER), ACT.Copy)
                    act.activation(q_g[lo, :, 1, :], q[hi].rearrange("p (t d) -> p t d", t=PER), ACT.Copy)
                    act.activation(q_g[hi, :, 1, :], q[lo].rearrange("p (t d) -> p t d", t=PER), ACT.Copy
                                   ).then_inc(s_q_ev, 1)
                    act.activation(v_all[:, bass.ds(PER * j, PER), 0, :], v.rearrange("p (t d) -> p t d", t=PER),
                                   ACT.Copy)
                    act.activation(v_all[lo, bass.ds(PER * j, PER), 1, :], v[hi].rearrange("p (t d) -> p t d", t=PER),
                                   ACT.Copy)
                    act.activation(v_all[hi, bass.ds(PER * j, PER), 1, :], v[lo].rearrange("p (t d) -> p t d", t=PER),
                                   ACT.Copy).then_inc(s_v_ev, 1)
                if on(k, 4):
                    act.wait_ge(s_logit, j - 3)
                    act.activation(tiles(lg_all, j - 4),
                                   bank[7][:, GC:GC + PER * EXPERTS].rearrange("p (t e) -> p t e", t=PER),
                                   ACT.Copy).then_inc(s_logit_ev, 1)

            sweep(act, step, 4, LAST)

            act.wait_ge(s_cT, 1)
            act.activation(cols35[:], bank[0][:, 0:35], ACT.Copy).then_inc(s_cT_ev, 1)
            act.wait_ge(s_lg_exp, 1)
            act.activation(sc_b[:], sc_a[:], ACT.Exp).then_inc(s_lg_exp, 1)
            act.wait_ge(s_cT_ev, 1)

            def keys_values(k):
                if k > 0:
                    j = k - 1
                    act.wait_ge(s_vw, j + 1)
                    act.activation(tiles(vw_all, j), bank[3 + j % 2][:, 0:GC].rearrange("p (t d) -> p t d", t=PER),
                                   ACT.Copy).then_inc(s_vw_ev, 1)
                if k < GROUPS:
                    act.wait_ge(s_kp, k + 1)
                    kv = bank[2 + 3 * (k % 2)]
                    act.activation(tiles(kT_all, k), kv[:, 0:GC].rearrange("p (t k) -> p t k", t=PER),
                                   ACT.Identity, bias=cols35[:, 33:34])
                    act.activation(vT_g[:, k % 2, :], kv[:, GC:2 * GC], ACT.Identity,
                                   bias=cols35[:, 34:35]).then_inc(s_kp_ev, 1)
                if k == GROUPS - 2:
                    act.activation(warm[:, 0:1], warm[:, 1:2], ACT.Gelu)

            for j in range(GROUPS + 1):
                keys_values(j)

            def evict_rows(e, first=False):
                act.wait_ge(s_xrT, e + 1)
                if not first:
                    act.wait_ge(s_f1, HC * e)
                act.activation(xrT_g[:], bank[5][:, :], ACT.Copy).then_inc(s_xrT_ev, 1)

            def gelu(e, first=False):
                for c in range(HC):
                    act.wait_ge(s_f1, HC * e + c + 1)
                    if not first:
                        act.wait_ge(s_f2, e)
                    act.activation(h_g[:, c, :], bank[1 + c][:, :], ACT.Gelu,
                                   bias=cols35[:, bass.ds(HC * e + c, 1)]).then_inc(s_gelu, 1)

            evict_rows(0, first=True)
            gelu(0, first=True)
            evict_rows(1)
            with act.Fori(1, EXPERTS - 1) as e:
                gelu(e)
                evict_rows(e + 1)
            gelu(EXPERTS - 1)

            act.wait_ge(s_aT, 1)
            act.activation(a_mat[:], bank[0][:, 128:256], ACT.Copy).then_inc(s_aT_ev, 1)

            def normalise(dst, src, g, n):
                for t in range(PER):
                    last = act.activation(dst[:, t, :], src[:, bass.ds(PER * g + t, 1), :].rearrange("p a d -> p (a d)"),
                                          ACT.Identity, bias=nmr3[:, n, t:t + 1], scale=rstd3[:, n, t:t + 1])
                return last

            def step(j, k):
                if on(k, 3):
                    act.wait_ge(s_pT, j - 2)
                    if k > 3:
                        act.wait_ge(s_pv, j - 3)
                    act.activation(pT_g[:], bank[1][:, 0:GC], ACT.Copy).then_inc(s_pT_ev, 1)
                if k > 0:
                    act.wait_ge(s_nmr3, j)
                if on(k, 1):
                    if k > 1:
                        act.wait_ge(s_xT3, j - 1)
                    normalise(xh3_g, x1_all, j - 1, 0).then_inc(s_xh3, 1)
                if on(k, 5):
                    if k > 5:
                        act.wait_ge(s_xT4, j - 5)
                    normalise(xh4_g, x_all, j - 5, 2).then_inc(s_xh4, 1)
                if on(k, 1):
                    act.wait_ge(s_xT3, j)
                    if k > 1:
                        act.wait_ge(s_qp, j - 1)
                    act.activation(xT3_g[:], bank[0][:, 0:GC], ACT.Copy).then_inc(s_xT3_ev, 1)
                if on(k, 5):
                    act.wait_ge(s_xT4, j - 4)
                    if k > 5:
                        act.wait_ge(s_ad, j - 5)
                    act.activation(xT4_g[:], bank[5][:, 0:GC], ACT.Copy).then_inc(s_xT4_ev, 1)
                if on(k, 2):
                    act.wait_ge(s_scr_max, j - 1)
                    for t in range(PER):
                        last = act.activation(p_g[:, t, :], sc_g[:, t, :], ACT.Exp, bias=nmax[:, t:t + 1],
                                              accum_out=psums[:, t:t + 1])
                    last.then_inc(s_p_ok, 1)
                if on(k, 1):
                    act.wait_ge(s_qp, j)
                    if k > 1:
                        act.wait_ge(s_scr, j - 1)
                    act.activation(qT_g[:], bank[2][:, 0:GC], ACT.Identity, bias=cols35[:, 32:33]
                                   ).then_inc(s_qp_ev, 1)
                if on(k, 5):
                    act.wait_ge(s_ad, j - 4)
                    if k > 5:
                        act.wait_ge(s_out_done, 16 * (j - 5))
                    act.activation(fin_g[:], bank[3][:, 0:GC].rearrange("p (t d) -> p t d", t=PER), ACT.Copy
                                   ).then_inc(s_fin, 1)

            act.activation(warm[:, 0:1], warm[:, 1:2], ACT.Exp)
            sweep(act, step, 5)

        @block.tensor
        def _(pe):
            pe.wait_ge(s_pset, 2)
            for i in range(WARM_UP):
                pe.matmul(bank[7][:, :].rearrange("p (a b) -> p a b", b=P), ones16[:],
                          ones16[:].unsqueeze(1).to_broadcast([P, 4, P]), start=True, stop=True)
            pe.wait_ge(s_c_in, 16)
            pe.wait_ge(s_w0_in, 64)
            pe.wait_ge(s_pset, 7)

            def step(j, k):
                def turn_xh2():
                    if on(k, 4):
                        pe.wait_ge(s_xh2, j - 3)
                        if k > 4:
                            pe.wait_ge(s_logit_ev, j - 4)
                        for t in range(PER):
                            last = pe.transpose(bank[7][:, t * P:(t + 1) * P], xh2_g[:, t, :], ident)
                        last.then_inc(s_xT2, 1)

                def project():
                    if on(k, 3):
                        pe.wait_ge(s_agg, j - 2)
                        if k == 3:
                            pe.wait_ge(s_bset, 2)
                        for t in range(PER):
                            o = bank[6][:, GC + t * D:GC + (t + 1) * D]
                            pe.matmul(o, agg_g[:, 2 * t:2 * t + 2, :].rearrange("p s l -> p (s l)"), wo0[:],
                                      start=True, stop=False)
                            last = pe.matmul(o, at_all[:], bias3[:, 3 * D:4 * D], start=False, stop=True)
                        last.then_inc(s_outp, 1)

                if on(k, 0):
                    pe.wait_ge(s_ctx_copied, j + 1)
                    if k > 0:
                        pe.wait_ge(s_ctxT_ev, j)
                    for t in range(PER):
                        last = pe.transpose(bank[4][:, GC + t * P:GC + (t + 1) * P], ctx_g[:, t, :], ident)
                    last.then_inc(s_ctxT, 1)
                if on(k, 2):
                    pe.wait_ge(s_chosen, j - 1)
                    if k == GROUPS:
                        pe.wait_ge(s_ctxT_ev, GROUPS)
                    if k > 2:
                        pe.wait_ge(s_sT_ev, j - 2)
                    for t in range(PER):
                        last = pe.transpose(bank[4][:, t * P:(t + 1) * P],
                                            s_g[:, 2 * t:2 * t + 2, :].rearrange("p s l -> p (s l)"), ident)
                    last.then_inc(s_sT, 1)
                if on(k, 0):
                    pe.wait_ge(s_xh, j + 1)
                    if k > 0:
                        pe.wait_ge(s_dft_ev, j)
                    for t in range(PER):
                        pe.matmul(bank[0][:, t * P:(t + 1) * P], xh_g[:, t, :], fwd, start=True, stop=True)
                        last = pe.matmul(bank[0][:, GC + t * P:GC + (t + 1) * P], ctx_g[:, t, :], fwd,
                                         start=True, stop=True)
                    last.then_inc(s_dft, 1)
                if on(k, 1):
                    pe.wait_ge(s_qk, j)
                    if k > 1:
                        pe.wait_ge(s_corr_ev, j - 1)
                    for t in range(PER):
                        pe.matmul(bank[3][:, t * P:(t + 1) * P], qk_g[:, t, 0, :], c1, start=True, stop=False)
                        last = pe.matmul(bank[3][:, t * P:(t + 1) * P], qk_g[:, t, 1, :], c2, start=False, stop=True)
                    last.then_inc(s_corr, 1)
                if on(k, 3):
                    pe.wait_ge(s_sv, j - 2)
                    if k > 3:
                        pe.wait_ge(s_x1, j - 3)
                    for t in range(PER):
                        pe.matmul(bank[6][:, t * P:(t + 1) * P], sv_g[:, t, 0, :], c1, start=True, stop=False)
                        last = pe.matmul(bank[6][:, t * P:(t + 1) * P], sv_g[:, t, 1, :], c2, start=False, stop=True)
                    last.then_inc(s_inv, 1)
                if on(k, 2):
                    pe.wait_ge(s_sT_ev, j - 1)
                    if k > 2:
                        pe.wait_ge(s_sv, j - 2)
                    pe.matmul(bank[5][:, 0:GC], fwd, sT_g[:], start=True, stop=True).then_inc(s_spec, 1)
                if not last_steps(k):
                    turn_xh2()
                if on(k, 0):
                    pe.wait_ge(s_dft_ev, j + 1)
                    if k == 0:
                        pe.wait_ge(s_bset, 1)
                    if k > 0:
                        pe.wait_ge(s_qk, j)
                        pe.wait_ge(s_v_ev, j)
                    for n, spec, w, part in ((0, 0, wq0[:], 2), (1, 1, wv0k0[:, 0:D], 0)):
                        for t in range(PER):
                            o = bank[2][:, (PER * n + t) * D:(PER * n + t + 1) * D]
                            pe.matmul(o, xcf_g[:, spec, t, :], w, start=True, stop=False)
                            last = pe.matmul(o, at_dc[:], bias3[:, part * D:(part + 1) * D], start=False, stop=True)
                    last.then_inc(s_qv, 1)
                    for t in range(PER):
                        o = bank[1][:, t * D:(t + 1) * D]
                        pe.matmul(o, xcf_g[:, 1, t, :], wv0k0[:, D:2 * D], start=True, stop=False)
                        last = pe.matmul(o, at_dc[:], bias3[:, D:2 * D], start=False, stop=True)
                    last.then_inc(s_proj, 1)
                project()
                if last_steps(k):
                    turn_xh2()
                if on(k, 4):
                    pe.wait_ge(s_xT2_ev, j - 3)
                    if k == 4:
                        pe.wait_ge(s_wg_in, 16)
                    for t in range(PER):
                        last = pe.matmul(bank[7][:, GC + t * EXPERTS:GC + (t + 1) * EXPERTS],
                                         xT2_g[:, t * P:(t + 1) * P], wg_s[:], start=True, stop=True)
                    last.then_inc(s_logit, 1)

            sweep(pe, step, 4)

            pe.wait_ge(s_rows_in, 64)
            pe.wait_ge(s_dft_ev, GROUPS)
            pe.transpose(bank[0][:, 0:35], rows35[:], ident[0:35, 0:35]).then_inc(s_cT, 1)

            pe.wait_ge(s_l1w_in, 64)
            pe.wait_ge(s_v_ev, GROUPS)
            pe.wait_ge(s_ctxT_ev, GROUPS)
            pe.wait_ge(s_sv, GROUPS)
            pe.wait_ge(s_corr_ev, GROUPS)

            def keys_values(k):
                if k < GROUPS:
                    kv = bank[2 + 3 * (k % 2)]
                    if k > 1:
                        pe.wait_ge(s_kp_ev, k - 1)
                    pe.matmul(kv[:, 0:GC], wk1[:], tiles(kT_all, k), start=True, stop=True)
                    pe.matmul(kv[:, GC:2 * GC], wv1[:], tiles(kT_all, k), start=True, stop=True).then_inc(s_kp, 1)
                if k > 0:
                    j = k - 1
                    pe.wait_ge(s_kp_ev, j + 1)
                    if j > 1:
                        pe.wait_ge(s_vw_ev, j - 1)
                    for t in range(PER):
                        o = bank[3 + j % 2][:, t * D:(t + 1) * D]
                        pe.matmul(o, vT_g[:, j % 2, t * P:(t + 1) * P], wo1[:], start=True, stop=False)
                        last = pe.matmul(o, at_all[:], bias3[:, 4 * D:5 * D], start=False, stop=True)
                    last.then_inc(s_vw, 1)

            for j in range(3):
                keys_values(j)
            pe.wait_ge(s_onehot, 1)
            pe.matmul(bank[7][:, 0:256], before16[:], hot[:].rearrange("p e k t -> p (e k t)"), start=True, stop=True)
            pe.matmul(bank[7][:, 256:512], ones16[:], hot[:].rearrange("p e k t -> p (e k t)"),
                      start=True, stop=True).then_inc(s_counted, 1)
            for j in range(3, 6):
                keys_values(j)
            order = [*range(POOL_FROM - MARKS), *range(POOL_FROM, POOL_HALF),
                     *range(POOL_FROM - MARKS, POOL_FROM), *range(POOL_HALF, 2 * TILES)]
            for n, i in enumerate(order):
                if i in (POOL_FROM, POOL_HALF):
                    pe.wait_ge(s_marked_pool, 1 if i == POOL_FROM else 2)
                elif i < POOL_FROM and i % MARKS == 0:
                    pe.wait_ge(s_marked, i // MARKS + 1)
                last = pe.matmul(bank[6][:, 0:2 * CHUNKS], hot_place[:, i, :],
                                 hot_id[:, i, :, :].rearrange("p h c -> p (h c)"),
                                 start=(n == 0), stop=(n == 2 * TILES - 1))
            last.then_inc(s_table, 1)
            for j in range(6, GROUPS + 1):
                keys_values(j)

            def turn_rows(e, half, nth, first=False):
                pe.wait_ge(s_xr_in[half], 16 * SC * nth)
                if not first:
                    pe.wait_ge(s_xrT_ev, e)
                for c in range(SC):
                    last = pe.transpose(bank[5][:, c * P:(c + 1) * P], xr_g[:, half, c, :], ident)
                last.then_inc(s_xrT, 1)

            def expert(e, next_half=None, nth=None, first=False):
                pe.wait_ge(s_xrT_ev, e + 1)
                pe.wait_ge(s_w1c, e + 1)
                for c in range(HC):
                    if not first:
                        pe.wait_ge(s_gelu, HC * (e - 1) + c + 1)
                    pe.matmul(bank[1 + c][:, :], w1_g[:, c * P:(c + 1) * P], xrT_g[:], start=True, stop=True
                              ).then_inc(s_f1, 1)
                if nth is not None:
                    turn_rows(e + 1, next_half, nth)
                if not first:
                    pe.wait_ge(s_y, e)
                for c in range(HC):
                    pe.wait_ge(s_gelu, HC * e + c + 1)
                    for s in range(SC):
                        last = pe.matmul(bank[6][:, s * D:(s + 1) * D], h_g[:, c, s * P:(s + 1) * P],
                                         w2_all[:, bass.ds(e, 1), c, :].rearrange("p a d -> p (a d)"),
                                         start=(c == 0 and s == 0), stop=(c == HC - 1), skip_group_check=True)
                last.then_inc(s_f2, 1)

            pe.wait_ge(s_kp_ev, GROUPS)
            turn_rows(0, 0, 1, first=True)
            pe.wait_ge(s_vw_ev, GROUPS)
            pe.wait_ge(s_w2_in, 16)
            expert(0, 1, 1, first=True)
            with pe.Fori(0, EXPERTS // 2 - 1) as i:
                expert(2 * i + 1, 0, i + 2)
                expert(2 * i + 2, 1, i + 2)
            expert(EXPERTS - 1)

            pe.wait_ge(s_asum, 1)
            pe.wait_ge(s_wrep, 1)
            pe.wait_ge(s_abg, 16)
            pe.transpose(bank[0][:, 128:256], a_sum[:], ident).then_inc(s_aT, 1)

            def step(j, k):
                if on(k, 2):
                    pe.wait_ge(s_qp_ev, j - 1)
                    if k > 2:
                        pe.wait_ge(s_scr_read, j - 2)
                    for t in range(PER):
                        last = pe.matmul(bank[7][:, t * P:(t + 1) * P], qT_g[:, t * P:(t + 1) * P],
                                         kT_all[:, bass.ds(PER * (j - 2) + t, 1), :].rearrange("p a d -> p (a d)"),
                                         start=True, stop=True)
                    last.then_inc(s_scr, 1)
                if on(k, 3):
                    pe.wait_ge(s_p_ok, j - 2)
                    if k > 3:
                        pe.wait_ge(s_pT_ev, j - 3)
                    for t in range(PER):
                        last = pe.transpose(bank[1][:, t * P:(t + 1) * P], p_g[:, t, :], ident)
                    last.then_inc(s_pT, 1)
                if on(k, 5):
                    pe.wait_ge(s_nmr3, j)
                    if k > 5:
                        pe.wait_ge(s_fin, j - 5)
                    both = bank[3][:, 0:GC].rearrange("p (t d) -> p t d", t=PER)
                    pe.matmul(both, ident, tiles(x_all, j - 5), start=True, stop=False, skip_group_check=True)
                    pe.matmul(both, w_rep[:], b_sel[:].unsqueeze(1).to_broadcast([P, PER, D]), start=False, stop=False,
                              skip_group_check=True)
                if on(k, 3):
                    pe.wait_ge(s_pT_ev, j - 2)
                    if k > 3:
                        pe.wait_ge(s_centred, j - 3)
                    for t in range(PER):
                        last = pe.matmul(bank[4][:, t * D:(t + 1) * D], pT_g[:, t * P:(t + 1) * P],
                                         vw_all[:, bass.ds(PER * (j - 3) + t, 1), :].rearrange("p a d -> p (a d)"),
                                         start=True, stop=True)
                    last.then_inc(s_pv, 1)
                if on(k, 1):
                    pe.wait_ge(s_xh3, j)
                    if k > 1:
                        pe.wait_ge(s_xT3_ev, j - 1)
                    for t in range(PER):
                        last = pe.transpose(bank[0][:, t * P:(t + 1) * P], xh3_g[:, t, :], ident)
                    last.then_inc(s_xT3, 1)
                if on(k, 5):
                    pe.wait_ge(s_xh4, j - 4)
                    if k > 5:
                        pe.wait_ge(s_xT4_ev, j - 5)
                    for t in range(PER):
                        last = pe.transpose(bank[5][:, t * P:(t + 1) * P], xh4_g[:, t, :], ident)
                    last.then_inc(s_xT4, 1)
                if on(k, 1):
                    pe.wait_ge(s_xT3_ev, j)
                    if k > 1:
                        pe.wait_ge(s_qp_ev, j - 1)
                    pe.matmul(bank[2][:, 0:GC], wq1[:], xT3_g[:], start=True, stop=True).then_inc(s_qp, 1)
                if on(k, 5):
                    pe.wait_ge(s_xT4_ev, j - 4)
                    for t in range(PER):
                        last = pe.matmul(bank[3][:, t * D:(t + 1) * D], xT4_g[:, t * P:(t + 1) * P], a_mat[:],
                                         start=False, stop=True, skip_group_check=True)
                    last.then_inc(s_ad, 1)
                if on(k, 3):
                    if k > 3:
                        pe.wait_ge(s_x3, j - 3)
                    both = bank[6][:, 0:GC].rearrange("p (t d) -> p t d", t=PER)
                    pe.matmul(both, ident, tiles(x1_all, j - 3), start=True, stop=False)
                    pe.matmul(both, at_all[:], bias3[:, 5 * D:6 * D].unsqueeze(1).to_broadcast([P, PER, D]),
                              start=False, stop=True).then_inc(s_offset, 1)

            pe.wait_ge(s_aT_ev, 1)
            pe.wait_ge(s_masked, 1)
            sweep(pe, step, 5)

        @block.vector
        def _(v):
            v.memset(warm[:], 0.0).then_inc(s_warm, 1)
            v.memset(at_dc[:], 0.0)
            v.memset(at_all[:], 0.0)
            v.memset(w_rep[:], 0.0)
            v.memset(mv3[:], 0.0)
            v.memset(rstd3[:], 0.0)
            v.memset(eps3[:], EPS)
            v.drain()
            for r in (0, 32, 64):
                v.memset(at_all[r:r + 1, :], 1.0)
                v.memset(at_dc[r:r + 1, 0:1], float(LEN))
                v.memset(at_dc[r:r + 1, 32:33], float(LEN))

            def statistics(part):
                v.wait_ge((s_x_in0, s_x_in1, s_x_in2)[part], 16)
                v.nop(nofuse=True)
                cols = PARTS[part]
                for t in range(cols.start, cols.stop):
                    v.bn_stats(st1[:, t, :], x_all[:, t, :])
                v.drain()
                for t in range(cols.start, cols.stop):
                    v.bn_aggr(mv1[:, t, :], st1[:, t, :])
                v.drain()
                v.tensor_scalar(ve1[:, cols], mv1[:, cols, 1], EPS, None, ALU.add).then_inc(s_var1, 1)

            def mean_over_deviation(part):
                cols = PARTS[part]
                v.wait_ge(s_rstd1, part + 1)
                v.scalar_tensor_tensor(out=nmr1[:, cols], in0=mv1[:, cols, 0], scalar=-1.0, in1=rstd1[:, cols],
                                       op0=ALU.mult, op1=ALU.mult).then_inc(s_nmr1, 1)

            statistics(0)
            mean_over_deviation(0)

            def split_biases(half):
                cols = slice(3 * D * half, 3 * D * (half + 1))
                v.tensor_copy(bhi[:, cols], biasf[:, cols])
                v.drain()
                v.tensor_tensor(bres[:, cols], biasf[:, cols], bhi[:, cols], ALU.subtract)
                v.tensor_copy(bias3[0:1, cols], bhi[0:1, cols])
                v.drain()
                v.tensor_copy(bmid[:, cols], bres[:, cols])
                v.drain()
                v.tensor_tensor(bres[:, cols], bres[:, cols], bmid[:, cols], ALU.subtract)
                v.tensor_copy(bias3[32:33, cols], bmid[32:33, cols])
                v.drain()
                v.tensor_copy(bias3[64:65, cols], bres[64:65, cols]).then_inc(s_bset, 1)

            v.wait_ge(s_pset, 7)
            v.wait_ge(s_b0_in, 48)
            split_biases(0)
            statistics(1)
            v.wait_ge(s_c_in, 16)
            v.wait_ge(s_ad_in, 64)
            v.tensor_scalar(a_idx[:], ids_b[:], float(D), lane, ALU.mult, ALU.add).then_inc(s_aidx, 1)
            v.tensor_scalar(w_rep[0:PICKS, :], ident[0:PICKS, :], 0.0, w_c[:], ALU.mult, ALU.add).then_inc(s_wrep, 1)
            v.tensor_copy(count16[:], count)
            v.tensor_scalar(before16[:], before, -1.0, None, ALU.add)

            def step(j, k):
                def normalise():
                    if on(k, 4):
                        v.wait_ge(s_rstd2_ok, j - 3)
                        if k > 4:
                            v.wait_ge(s_xT2, j - 4)
                            v.wait_ge(s_xh2_out, 16 * (j - 4))
                        for t in range(PER):
                            last = v.tensor_scalar(xh2_g[:, t, :], x1_all[:, bass.ds(PER * (j - 4) + t, 1), :],
                                                   mv2[:, t, 0:1], rstd2[:, t:t + 1], ALU.subtract, ALU.mult)
                        last.then_inc(s_xh2, 1)

                def aggregate():
                    if on(k, 3):
                        v.wait_ge(s_inv, j - 2)
                        if k > 3:
                            v.wait_ge(s_outp, j - 3)
                        rs = rs_all[:, bass.ds(j - 3, 1), :].rearrange("p a s -> p (a s)").unsqueeze(2)
                        v.tensor_tensor(agg_g[:], bank[6][:, 0:GC].rearrange("p (s l) -> p s l", s=NSEQ),
                                        rs.to_broadcast([P, NSEQ, LEN]), ALU.mult).then_inc(s_agg, 1)

                if not last_steps(k):
                    normalise()
                if on(k, 1):
                    v.wait_ge(s_corr_ev, j)
                    v.nop(nofuse=True)
                    for q in range(NSEQ):
                        v.max(top[:, q, 0:8], corr_g[:, q, 0:LEN])
                    v.drain()
                    first = top[:, :, 0:1]
                    v.tensor_tensor(diff_g[:, :, 0:LEN], corr_g[:, :, 0:LEN], first.to_broadcast([P, NSEQ, LEN]),
                                    ALU.subtract)
                    v.tensor_tensor(diff_g[:, :, LEN:LEN + TOPK], top[:, :, 0:TOPK],
                                    first.to_broadcast([P, NSEQ, TOPK]), ALU.subtract).then_inc(s_maxed, 1)
                aggregate()
                if last_steps(k):
                    normalise()
                if on(k, 1):
                    for q in range(NSEQ):
                        v.match_replace(out=picked[:, q, :],
                                        in_to_replace=top[:, q, :].rearrange("p (a b) -> p a b", a=2)[:, :, 0:TOPK],
                                        in_values=corr_g[:, q, :], imm_value=CHOSEN)
                if on(k, 2):
                    v.wait_ge(s_spec, j - 1)
                    if k > 2:
                        v.wait_ge(s_inv, j - 2)
                    v.tensor_tensor(sv_g[:], v_all[:, bass.ds(PER * (j - 2), PER), :, :],
                                    bank[5][:, 0:GC].rearrange("p (t d) -> p t d", t=PER).unsqueeze(2).to_broadcast(
                                        [P, PER, 2, D]), ALU.mult).then_inc(s_sv, 1)
                if 1 <= k <= LAST + 3:
                    v.drain()
                if on(k, 1):
                    v.wait_ge(s_exped, j)
                    v.tensor_reduce(ssum[:], exp_g[:, :, LEN:LEN + TOPK], AX, ALU.add)
                    if k > 1:
                        v.wait_ge(s_sT, j - 1)
                    v.scalar_tensor_tensor(out=s_g[:], in0=picked[:, :, 0:LEN], scalar=CHOSEN / 2,
                                           in1=exp_g[:, :, 0:LEN], op0=ALU.is_ge, op1=ALU.mult
                                           ).then_inc(s_chosen, 1)
                if on(k, 0):
                    v.wait_ge(s_proj, j + 1)
                    v.wait_ge(s_q_ev, j + 1)
                    if k > 0:
                        v.wait_ge(s_corr, j)
                    v.tensor_tensor(qk_g[:], q_g[:],
                                    bank[1][:, 0:GC].rearrange("p (t d) -> p t d", t=PER).unsqueeze(2).to_broadcast(
                                        [P, PER, 2, D]), ALU.mult).then_inc(s_qk, 1)
                if on(k, 3):
                    v.wait_ge(s_outp, j - 2)
                    v.tensor_tensor(tiles(x1_all, j - 3), bank[6][:, GC:2 * GC].rearrange("p (t d) -> p t d", t=PER),
                                    tiles(x_all, j - 3), ALU.add).then_inc(s_x1, 1)
                    v.drain()
                    for t in range(PER):
                        v.bn_stats(st2[:, t, :], x1_all[:, bass.ds(PER * (j - 3) + t, 1), :])
                    v.drain()
                    for t in range(PER):
                        v.bn_aggr(mv2[:, t, :], st2[:, t, :])
                if k == 0:
                    mean_over_deviation(1)
                    statistics(2)
                if k == 1:
                    mean_over_deviation(2)
                    v.wait_ge(s_b1_in, 48)
                    split_biases(1)
                if on(k, 1) or on(k, 3):
                    v.drain()
                if on(k, 3):
                    v.tensor_scalar(ve2[:], mv2[:, :, 1], EPS, None, ALU.add).then_inc(s_var2, 1)
                if on(k, 1):
                    v.reciprocal(rs_all[:, bass.ds(j - 1, 1), :], ssum[:])

            sweep(v, step, 4)

            def whole(ap):
                return ap.unsqueeze(2).to_broadcast([P, TILES, EXPERTS])

            v.wait_ge(s_logit_ev, GROUPS)
            v.tensor_reduce(col[:, 0, :], lg_all[:], AX, ALU.max)
            v.drain()
            v.tensor_tensor(sc_a[:], lg_all[:], whole(col[:, 0, :]), ALU.subtract).then_inc(s_lg_exp, 1)
            v.wait_ge(s_lg_exp, 2)
            v.tensor_reduce(col[:, 1, :], sc_b[:], AX, ALU.add)
            v.drain()
            v.reciprocal(col[:, 2, :], col[:, 1, :])
            v.drain()
            v.tensor_tensor(sc_a[:], sc_b[:], whole(col[:, 2, :]), ALU.mult)
            v.drain()
            cur = sc_a
            for k in range(2):
                v.tensor_reduce(col[:, 3 + k, :], cur[:], AX, ALU.max)
                v.drain()
                v.tensor_tensor(sc_t[:], cur[:], whole(col[:, 3 + k, :]), ALU.is_equal)
                v.drain()
                v.tensor_tensor(sc_t[:], sc_t[:], prio.unsqueeze(1).to_broadcast([P, TILES, EXPERTS]), ALU.mult)
                v.drain()
                v.tensor_reduce(first[:, k, :], sc_t[:], AX, ALU.max)
                v.drain()
                last = v.tensor_tensor(hot[:, :, k, :].rearrange("p e t -> p t e"), sc_t[:], whole(first[:, k, :]),
                                       ALU.is_equal)
                if k == 1:
                    last.then_inc(s_onehot, 1)
                v.drain()
                if k == 0:
                    v.scalar_tensor_tensor(out=sc_b[:], in0=hot[:, :, 0, :].rearrange("p e t -> p t e"), scalar=-2.0,
                                           in1=sc_a[:], op0=ALU.mult, op1=ALU.add)
                    v.drain()
                    cur = sc_b
            v.tensor_tensor(col[:, 6, :], col[:, 3, :], col[:, 4, :], ALU.add)
            v.tensor_scalar(base[:], first[:], -float(CAP), float(EXPERTS * CAP), ALU.mult, ALU.add)
            v.drain()
            v.tensor_scalar(col[:, 6, :], col[:, 6, :], GATE_EPS, None, ALU.max)
            v.drain()
            v.reciprocal(col[:, 7, :], col[:, 6, :])
            v.drain()
            v.tensor_tensor(gate[:], col[:, 3:5, :], col[:, 7:8, :].to_broadcast([P, 2, TILES]), ALU.mult)
            v.wait_ge(s_counted, 1)
            flat = "p e k t -> p (e k t)"
            v.tensor_tensor_scan(run_s[:], segment, bank[7][:, 256:512], 0.0, ALU.mult, ALU.add)
            v.drain()
            v.tensor_tensor(where[:].rearrange(flat), bank[7][:, 0:256], run_s[:], ALU.add)
            v.drain()
            v.tensor_tensor(prod[:], hot[:], where[:], ALU.mult)
            v.drain()
            v.tensor_reduce(pos[:], prod[:].rearrange("p e k t -> p k t e"), AX, ALU.add)
            v.drain()
            v.tensor_scalar(chunk[:], pos[:], float(P), None, ALU.is_ge)
            v.tensor_scalar(keep[:], pos[:], float(CAP), None, ALU.is_lt)
            for c in range(2, SC):
                v.drain()
                v.scalar_tensor_tensor(out=chunk[:], in0=pos[:], scalar=float(c * P), in1=chunk[:],
                                       op0=ALU.is_ge, op1=ALU.add)
            v.tensor_tensor(gate[:], gate[:], keep[:], ALU.mult)
            v.tensor_tensor(tmp2[:], pos[:], keep[:], ALU.mult)
            v.drain()
            v.tensor_tensor(from_slot[:], tmp2[:], base[:], ALU.add)
            v.scalar_tensor_tensor(out=place[:], in0=chunk[:], scalar=-float(P), in1=pos[:],
                                   op0=ALU.mult, op1=ALU.add).then_inc(s_place, 1)
            v.scalar_tensor_tensor(out=chunk_of[:], in0=base[:], scalar=1.0 / P, in1=chunk[:],
                                   op0=ALU.mult, op1=ALU.add)
            v.drain()
            v.tensor_tensor(hot_chunk[:], chunk_of[:].rearrange("p k t -> p (k t)").unsqueeze(2).to_broadcast(
                [P, 2 * TILES, CHUNKS]), count[:, 0:CHUNKS].unsqueeze(1).to_broadcast([P, 2 * TILES, CHUNKS]),
                ALU.is_equal)
            v.drain()
            for k in range(2):
                pairs = slice(k * TILES, (k + 1) * TILES)
                v.tensor_tensor(hot_id[:, pairs, 0, :], hot_chunk[:, pairs, :],
                                tile_no.unsqueeze(2).to_broadcast([P, TILES, CHUNKS]), ALU.mult)
            v.tensor_scalar(hot_id[:, :, 1, :], hot_chunk[:], lane1, None, ALU.mult)
            for i in range(POOL_FROM):
                last = v.tensor_scalar(hot_place[:, i, :], count16[:], place[:, i // TILES, i % TILES:i % TILES + 1],
                                       None, ALU.is_equal)
                if i % MARKS == MARKS - 1:
                    last.then_inc(s_marked, 1)
            v.wait_ge(s_table, 1)
            v.tensor_copy(ids_f[:], bank[6][:, 0:CHUNKS])
            v.drain()
            v.scalar_tensor_tensor(out=row_of[:], in0=ids_f[:], scalar=float(P),
                                   in1=bank[6][:, CHUNKS:2 * CHUNKS], op0=ALU.mult, op1=ALU.add).then_inc(s_row_of, 1)

            def first_layer(e, first=False):
                if not first:
                    v.wait_ge(s_f1, HC * e)
                v.tensor_copy(w1_g[:], w1_all[:, bass.ds(e, 1), :].rearrange("p a h -> p (a h)")).then_inc(s_w1c, 1)

            v.wait_ge(s_w1_in, 16)
            first_layer(0, first=True)

            v.wait_ge(s_ag, 16 * PICKS)
            v.tensor_scalar(a_sum[:], a_rows[:, 0, :], w_b[:, 0:1], None, ALU.mult)
            for i in range(1, PICKS):
                v.drain()
                last = v.scalar_tensor_tensor(out=a_sum[:], in0=a_rows[:, i, :], scalar=w_b[:, i:i + 1], in1=a_sum[:],
                                              op0=ALU.mult, op1=ALU.add)
            last.then_inc(s_asum, 1)

            v.wait_ge(s_mask_in, 16)
            v.tensor_scalar(live, mask_i[:].rearrange("p (t k) -> p t k", k=P), 0.0, None, ALU.not_equal)
            v.drain()
            v.tensor_scalar(penalty[:], live, -MASKED, MASKED, ALU.mult, ALU.add)
            v.drain()
            for b in range(2):
                v.memset(penalty[b * LEN:(b + 1) * LEN, :, (1 - b) * LEN:(2 - b) * LEN], FOREIGN)
            v.wait_ge(s_kp_ev, GROUPS)
            v.tensor_tensor(kT_all[:], kT_all[:], live, ALU.mult).then_inc(s_masked, 1)

            v.wait_ge(s_b2_in, 16)

            def expert_out(e, first=False):
                v.wait_ge(s_f2, e + 1)
                if not first:
                    v.wait_ge(s_y_out, 16 * e)
                v.tensor_tensor(y_g[:], bank[6][:, :].rearrange("p (s d) -> p s d", s=SC),
                                b2_b[:, bass.ds(e, 1), :].to_broadcast([P, SC, D]), ALU.add).then_inc(s_y, 1)

            first_layer(1)
            expert_out(0, first=True)
            with v.Fori(1, EXPERTS - 1) as e:
                first_layer(e + 1)
                expert_out(e)
            expert_out(EXPERTS - 1)

            v.wait_ge(s_vec_in, 16)

            def step(j, k):
                if on(k, 0):
                    for t in range(PER):
                        i = PER * j + t
                        v.wait_ge(g_in[i % len(g_in)], 32 * (i // len(g_in) + 1))
                        v.scalar_tensor_tensor(out=x1_all[:, PER * j + t, :], in0=y_all[:, PER * j + t, 0, :],
                                               scalar=gate[:, 0, PER * j + t:PER * j + t + 1],
                                               in1=x1_all[:, PER * j + t, :], op0=ALU.mult, op1=ALU.add)
                if on(k, 4):
                    for t in range(PER):
                        last = v.scalar_tensor_tensor(out=t_g[:, t, :], in0=bank[4][:, t * D:(t + 1) * D],
                                                      scalar=mv3[:, 1, t, 0:1], in1=g0_b[:],
                                                      op0=ALU.subtract, op1=ALU.mult)
                    last.then_inc(s_centred, 1)
                v.drain()
                if on(k, 0):
                    for t in range(PER):
                        last = v.scalar_tensor_tensor(out=x1_all[:, PER * j + t, :], in0=y_all[:, PER * j + t, 1, :],
                                                      scalar=gate[:, 1, PER * j + t:PER * j + t + 1],
                                                      in1=x1_all[:, PER * j + t, :], op0=ALU.mult, op1=ALU.add)
                if on(k, 3):
                    v.wait_ge(s_p_ok, j - 2)
                    v.scalar_tensor_tensor(out=eps3[:, 1, :], in0=psums[:], scalar=EPS, in1=psums[:],
                                           op0=ALU.mult, op1=ALU.mult)
                if k > 0:
                    v.wait_ge(s_rstd3_ok, j)
                    v.scalar_tensor_tensor(out=nmr3[:], in0=mv3[:, :, :, 0], scalar=-1.0, in1=rstd3[:],
                                           op0=ALU.mult, op1=ALU.mult).then_inc(s_nmr3, 1)
                if on(k, 4):
                    v.wait_ge(s_offset, j - 3)
                    for t in range(PER):
                        last = v.scalar_tensor_tensor(out=x_all[:, PER * (j - 4) + t, :], in0=t_g[:, t, :],
                                                      scalar=rstd3[:, 1, t:t + 1], in1=bank[6][:, t * D:(t + 1) * D],
                                                      op0=ALU.mult, op1=ALU.add)
                    last.then_inc(s_x3, 1)
                if on(k, 2):
                    v.wait_ge(s_scr, j - 1)
                    v.scalar_tensor_tensor(out=sc_g[:], in0=bank[7][:, 0:GC].rearrange("p (t k) -> p t k", t=PER),
                                           scalar=SCALE, in1=tiles(penalty, j - 2), op0=ALU.mult, op1=ALU.add
                                           ).then_inc(s_scr_read, 1)
                if k < GROUPS + 4:
                    v.drain()
                    if on(k, 0):
                        for t in range(PER):
                            v.bn_stats(st3[:, 0, t, :], x1_all[:, PER * j + t, :])
                    if on(k, 4):
                        for t in range(PER):
                            v.bn_stats(st3[:, 2, t, :], x_all[:, PER * (j - 4) + t, :])
                    if on(k, 2):
                        v.tensor_reduce(nmax[:], sc_g[:], AX, ALU.max)
                    if on(k, 3):
                        v.wait_ge(s_pv, j - 2)
                        for t in range(PER):
                            v.bn_stats(st3[:, 1, t, :], bank[4][:, t * D:(t + 1) * D])
                    v.drain()
                    if on(k, 2):
                        v.tensor_scalar(nmax[:], nmax[:], -1.0, None, ALU.mult).then_inc(s_scr_max, 1)
                    for n, lag in ((0, 0), (1, 3), (2, 4)):
                        for t in range(PER):
                            if on(k, lag):
                                v.bn_aggr(mv3[:, n, t, :], st3[:, n, t, :])
                    v.drain()
                    v.tensor_tensor(ve3[:].rearrange("p (n t) -> p n t", n=3), mv3[:, :, :, 1], eps3[:], ALU.add
                                    ).then_inc(s_var3, 1)

            for j in range(GROUPS + 5):
                step(j, j)


_INS = ["x", "ctx_1024", "mask_Bx1xS2_ik1", "L0_xattn_Wq", "L0_xattn_bq", "L0_xattn_Wk", "L0_xattn_bk",
        "L0_xattn_Wv", "L0_xattn_bv", "L0_xattn_Wo", "L0_xattn_bo", "L0_ffn_wg", "L0_ffn_w1", "L0_ffn_b1",
        "L0_ffn_w2", "L0_ffn_b2", "L1_xattn_Wq", "L1_xattn_bq", "L1_xattn_Wk", "L1_xattn_bk", "L1_xattn_Wv",
        "L1_xattn_bv", "L1_xattn_Wo", "L1_xattn_bo", "L1_xattn_g0", "L1_xattn_beta0", "L1_ffn_W", "L1_ffn_b",
        "L1_ffn_ids", "L1_ffn_weights"]


def kernel(**inputs):
    import concourse.bacc as _bacc
    from concourse.bass_utils import run_bass_kernel_spmd as _run

    nc = _bacc.Bacc("TRN2", target_bir_lowering=False, num_devices=1)
    arrays, args = {}, []
    data = [(name, inputs[name]) for name in _INS] + [("constants", constants())]
    for name, a in data:
        a = np.ascontiguousarray(a)
        arrays[f"in_{name}"] = a
        args.append(nc.dram_tensor(f"in_{name}", a.shape, mybir.dt.from_np(a.dtype), kind="ExternalInput").ap())
    args.append(nc.dram_tensor("out_0", (SEQS, LEN, D), F32, kind="ExternalOutput").ap())
    build(nc, *args)
    r = _run(nc, [arrays], core_ids=[0])
    return r.results[0]["out_0"]
```
